# Optimizing a Trainium2 kernel written in Bass

```python
import numpy as np
import jax
import jax.numpy as jnp

def _softmax(x, axis=-1):
    return jax.nn.softmax(x, axis=axis)

def _gelu(x):
    return jax.nn.gelu(x, approximate=True)

def _silu(x):
    return jax.nn.silu(x)

def _sigmoid(x):
    return jax.nn.sigmoid(x)

def _layernorm(x, axis=-1, eps=1e-05):
    m = jnp.mean(x, axis=axis, keepdims=True)
    v = jnp.var(x, axis=axis, keepdims=True)
    return (x - m) / jnp.sqrt(v + eps)

def _scatter_add(tgt, idx, src, axis=0):
    return tgt.at[idx].add(src)

def _segment_sum(src, seg, n):
    return jax.ops.segment_sum(src, seg, n)
kernel_name = 'mk_xattn_ffn_d2_seqx_r8_fd53e4'

def setup_inputs(seed: int=0):
    np.random.seed(seed)
    _w = jnp.asarray

    def _rec_inputs():
        import jax
        import jax.numpy as jnp
        _rk = jax.random.key(seed)
        x = 2.818e-05 + 1 * jax.random.normal(jax.random.fold_in(_rk, 1), (4, 256, 256), jnp.float32)
        _lenS = 256 - jax.random.randint(jax.random.fold_in(_rk, 7), (4,), 0, max(1, 256 // 4) + 1, jnp.int32)
        _lenS2 = 256 - jax.random.randint(jax.random.fold_in(_rk, 8), (4,), 0, max(1, 256 // 4) + 1, jnp.int32)
        _ctx_1024P = jax.random.normal(jax.random.fold_in(_rk, 11), (4, 16, 128), jnp.float32)
        _ctx_1024c = jax.random.dirichlet(jax.random.fold_in(_rk, 511), 0.3 * jnp.ones((16,), jnp.float32), (4, 256))
        _ctx_1024t = jnp.einsum('bsk,bkd->bsd', _ctx_1024c, _ctx_1024P)
        _ctx_1024t = _ctx_1024t * jax.lax.rsqrt(jnp.mean(jnp.square(_ctx_1024t)) + 1e-12) * 0.953939
        ctx_1024 = 7.22013e-05 + 1.00017 * (_ctx_1024t + 0.3 * jax.random.normal(jax.random.fold_in(_rk, 611), (4, 256, 128), jnp.float32))
        fside_BxSx2_0 = jax.random.uniform(jax.random.fold_in(_rk, 12), (4, 256, 2), jnp.float32, 0.0, 0.999707)
        return (x, ctx_1024, fside_BxSx2_0)
    x, ctx_1024, fside_BxSx2_0 = _rec_inputs()

    def _L0_xattn_setup():
        import jax, jax.numpy as jnp
        import numpy as np
        B_, L_, D_MODEL = (4, 256, 128)
        D_STATE, D_CONV, EXPAND = (16, 4, 2)
        D_INNER = EXPAND * D_MODEL
        DT_RANK = (D_MODEL + 15) // 16

        def silu(x):
            return x * jax.nn.sigmoid(x)
        key = jax.random.key(seed)
        ks = jax.random.split(key, 10)
        f32 = jnp.float32
        hidden_states = jax.random.normal(ks[0], (B_, L_, D_MODEL), dtype=f32)
        z = jax.random.normal(ks[1], (B_, D_INNER, L_), dtype=f32)
        in_proj_w = jax.random.normal(ks[2], (D_INNER, D_MODEL), dtype=f32) * 0.02
        conv_w = jax.random.normal(ks[3], (D_INNER, 1, D_CONV), dtype=f32) * 0.1
        conv_b = jax.random.normal(ks[4], (D_INNER,), dtype=f32) * 0.02
        x_proj_w = jax.random.normal(ks[5], (DT_RANK + 2 * D_STATE, D_INNER), dtype=f32) * 0.02
        dt_proj_w = jax.random.uniform(ks[6], (D_INNER, DT_RANK), dtype=f32, minval=-DT_RANK ** (-0.5), maxval=DT_RANK ** (-0.5))
        dt = jnp.exp(jax.random.uniform(ks[7], (D_INNER,), dtype=f32, minval=np.log(0.001), maxval=np.log(0.1)))
        dt_proj_b = jnp.log(jnp.expm1(dt))
        A_log = jnp.log(jnp.broadcast_to(jnp.arange(1, D_STATE + 1, dtype=f32), (D_INNER, D_STATE)))
        D = jnp.ones((D_INNER,), f32)
        return {'hidden_states': hidden_states, 'z': z, 'in_proj_w': in_proj_w, 'conv_w': conv_w, 'conv_b': conv_b, 'x_proj_w': x_proj_w, 'dt_proj_w': dt_proj_w, 'dt_proj_b': dt_proj_b, 'A_log': A_log, 'D': D}
    _L0_xattn_all = _L0_xattn_setup()
    _L0_xattn_in = {k: v for k, v in _L0_xattn_all.items() if k in ('in_proj_w', 'conv_w', 'conv_b', 'x_proj_w', 'dt_proj_w', 'dt_proj_b', 'A_log', 'D')}
    del _L0_xattn_all

    def _L0_ffn_setup():
        import jax, jax.numpy as jnp
        import numpy as np
        _Q_IN = 128
        _LUT_MIN = -128
        _Q_OUT = 1 << 16
        _TOP_K = 2
        _EXP_LUT = (jnp.exp(jnp.arange(_LUT_MIN, 1, dtype=jnp.float32) / _Q_IN) * _Q_OUT).astype(jnp.int32)

        def softmax_integer(logits):
            li = jnp.round(logits.astype(jnp.float32) * _Q_IN).astype(jnp.int32)
            shifted = jnp.clip(li - li.max(axis=-1, keepdims=True), _LUT_MIN, None)
            exp_vals = _EXP_LUT[shifted - _LUT_MIN]
            exp_sum = jnp.clip(exp_vals.sum(axis=-1, keepdims=True), 1, None)
            return exp_vals.astype(jnp.float32) / exp_sum.astype(jnp.float32)
        key = jax.random.key(seed)
        k0, k1, k2, k3, k4 = jax.random.split(key, 5)
        B, S, H, I, E = (4, 256, 256, 704, 8)
        x = jax.random.normal(k0, (B, S, H), dtype=jnp.float32)
        w_gate = jax.random.normal(k1, (E, H), dtype=jnp.float32) * 0.02
        w1 = jax.random.normal(k2, (E, I, H), dtype=jnp.float32) * 0.02
        w2 = jax.random.normal(k3, (E, H, I), dtype=jnp.float32) * 0.02
        w3 = jax.random.normal(k4, (E, I, H), dtype=jnp.float32) * 0.02
        return {'x': x, 'w_gate': w_gate, 'w1': w1, 'w2': w2, 'w3': w3}
    _L0_ffn_all = _L0_ffn_setup()
    _L0_ffn_in = {k: v for k, v in _L0_ffn_all.items() if k in ('w_gate', 'w1', 'w2', 'w3')}
    del _L0_ffn_all

    def _L1_xattn_setup():
        import jax, jax.numpy as jnp
        import numpy as np
        DIM = 256
        CTX_DIM = 128
        N_HEADS = 32
        HEAD_DIM = DIM // N_HEADS
        POS_DIM = 2
        B, N, CTXN = (2, 256, 256)
        ROPE_BASE = 10000.0

        def apply_axial_rope(x, pos):
            b, n, h, d = x.shape
            p = pos.shape[-1]
            dpa = d // p
            half = dpa // 2
            freqs = ROPE_BASE ** (-jnp.arange(half, dtype=x.dtype) / half)
            ang = pos[..., :, None] * freqs
            cos = jnp.cos(ang)[:, :, None, :, :]
            sin = jnp.sin(ang)[:, :, None, :, :]
            xr = x.reshape(b, n, h, p, half, 2)
            x1, x2 = (xr[..., 0], xr[..., 1])
            out = jnp.stack([x1 * cos - x2 * sin, x1 * sin + x2 * cos], axis=-1)
            return out.reshape(b, n, h, d)
        key = jax.random.key(seed)
        ks = jax.random.split(key, 8)
        x = jax.random.normal(ks[0], (B, N, DIM), jnp.float32)
        ctx = jax.random.normal(ks[1], (B, CTXN, CTX_DIM), jnp.float32)
        pos_map = jax.random.uniform(ks[2], (B, N, POS_DIM), jnp.float32)
        ctx_pos_map = jax.random.uniform(ks[3], (B, CTXN, POS_DIM), jnp.float32)
        Wq = jax.random.normal(ks[4], (DIM, DIM), jnp.float32) / np.sqrt(DIM)
        Wkv = jax.random.normal(ks[5], (CTX_DIM, 2 * DIM), jnp.float32) / np.sqrt(CTX_DIM)
        Wout = jax.random.normal(ks[6], (DIM, DIM), jnp.float32) / np.sqrt(DIM)
        bout = jnp.zeros((DIM,), jnp.float32)
        return {'x': x, 'ctx': ctx, 'pos_map': pos_map, 'ctx_pos_map': ctx_pos_map, 'Wq': Wq, 'Wkv': Wkv, 'Wout': Wout, 'bout': bout}
    _L1_xattn_all = _L1_xattn_setup()
    _L1_xattn_in = {k: v for k, v in _L1_xattn_all.items() if k in ('Wq', 'Wkv', 'Wout', 'bout')}
    del _L1_xattn_all

    def _L1_ffn_setup():
        import jax, jax.numpy as jnp
        import numpy as np
        BLOCK = 32
        BITS = 8

        def bf16_round(x):
            return x.astype(jnp.bfloat16).astype(jnp.float32)

        def mx_quant(x):
            s = x.shape
            xb = x.reshape(s[:-1] + (s[-1] // BLOCK, BLOCK))
            amax = jnp.max(jnp.abs(xb), axis=-1, keepdims=True)
            shared_exp = jnp.floor(jnp.log2(jnp.where(amax > 0, amax, 1.0)))
            scale = jnp.exp2(shared_exp - (BITS - 2))
            q = jnp.clip(jnp.round(xb / scale), -2.0 ** (BITS - 1), 2.0 ** (BITS - 1) - 1) * scale
            q = jnp.where(amax > 0, q, 0.0).reshape(s)
            return x + jax.lax.stop_gradient(q - x)

        def mx_linear(x, W, b):
            y = jnp.einsum('btk,ok->bto', mx_quant(x), mx_quant(W))
            return bf16_round(y + b)

        def mx_layernorm(x, w, b, eps=1e-05):
            mu = jnp.mean(x, axis=-1, keepdims=True)
            var = jnp.mean(jnp.square(x - mu), axis=-1, keepdims=True)
            return bf16_round((x - mu) * jax.lax.rsqrt(var + eps) * w + b)

        def mx_gelu(x):
            c = jnp.float32(0.7978845608028654)
            return bf16_round(0.5 * x * (1.0 + jnp.tanh(c * (x + 0.044715 * x * x * x))))
        key = jax.random.key(seed)
        ks = jax.random.split(key, 5)
        B, S, H = (2, 256, 256)
        inputs = jax.random.normal(ks[0], (B, S, H), dtype=jnp.float32)
        ln_w = jnp.ones((H,), dtype=jnp.float32)
        ln_b = jnp.zeros((H,), dtype=jnp.float32)
        W1 = jax.random.normal(ks[1], (4 * H, H), dtype=jnp.float32) * (1.0 / np.sqrt(H))
        b1 = jnp.zeros((4 * H,), dtype=jnp.float32)
        W2 = jax.random.normal(ks[2], (H, 4 * H), dtype=jnp.float32) * (1.0 / np.sqrt(4 * H))
        b2 = jnp.zeros((H,), dtype=jnp.float32)
        return {'inputs': inputs, 'ln_w': ln_w, 'ln_b': ln_b, 'W1': W1, 'b1': b1, 'W2': W2, 'b2': b2}
    _L1_ffn_all = _L1_ffn_setup()
    _L1_ffn_in = {k: v for k, v in _L1_ffn_all.items() if k in ('ln_w', 'ln_b', 'W1', 'b1', 'W2', 'b2')}
    del _L1_ffn_all
    return {'x': x, 'ctx_1024': ctx_1024, 'fside_BxSx2_0': fside_BxSx2_0, 'L0_xattn_in_proj_w': _L0_xattn_in['in_proj_w'], 'L0_xattn_conv_w': _L0_xattn_in['conv_w'], 'L0_xattn_conv_b': _L0_xattn_in['conv_b'], 'L0_xattn_x_proj_w': _L0_xattn_in['x_proj_w'], 'L0_xattn_dt_proj_w': _L0_xattn_in['dt_proj_w'], 'L0_xattn_dt_proj_b': _L0_xattn_in['dt_proj_b'], 'L0_xattn_A_log': _L0_xattn_in['A_log'], 'L0_xattn_D': _L0_xattn_in['D'], 'L0_ffn_w_gate': _L0_ffn_in['w_gate'], 'L0_ffn_w1': _L0_ffn_in['w1'], 'L0_ffn_w2': _L0_ffn_in['w2'], 'L0_ffn_w3': _L0_ffn_in['w3'], 'L1_xattn_Wq': _L1_xattn_in['Wq'], 'L1_xattn_Wkv': _L1_xattn_in['Wkv'], 'L1_xattn_Wout': _L1_xattn_in['Wout'], 'L1_xattn_bout': _L1_xattn_in['bout'], 'L1_ffn_ln_w': _L1_ffn_in['ln_w'], 'L1_ffn_ln_b': _L1_ffn_in['ln_b'], 'L1_ffn_W1': _L1_ffn_in['W1'], 'L1_ffn_b1': _L1_ffn_in['b1'], 'L1_ffn_W2': _L1_ffn_in['W2'], 'L1_ffn_b2': _L1_ffn_in['b2']}

def reference(x, ctx_1024, fside_BxSx2_0, L0_xattn_in_proj_w, L0_xattn_conv_w, L0_xattn_conv_b, L0_xattn_x_proj_w, L0_xattn_dt_proj_w, L0_xattn_dt_proj_b, L0_xattn_A_log, L0_xattn_D, L0_ffn_w_gate, L0_ffn_w1, L0_ffn_w2, L0_ffn_w3, L1_xattn_Wq, L1_xattn_Wkv, L1_xattn_Wout, L1_xattn_bout, L1_ffn_ln_w, L1_ffn_ln_b, L1_ffn_W1, L1_ffn_b1, L1_ffn_W2, L1_ffn_b2):
    import jax
    import jax.numpy as jnp

    def _L0_xattn_ref(hidden_states, z, in_proj_w, conv_w, conv_b, x_proj_w, dt_proj_w, dt_proj_b, A_log, D):
        import jax, jax.numpy as jnp
        import numpy as np
        B_, L_, D_MODEL = (4, 256, 128)
        D_STATE, D_CONV, EXPAND = (16, 4, 2)
        D_INNER = EXPAND * D_MODEL
        DT_RANK = (D_MODEL + 15) // 16

        def silu(x):
            return x * jax.nn.sigmoid(x)
        Bsz, L, _ = hidden_states.shape
        d_inner, _, d_conv = conv_w.shape
        dt_rank = dt_proj_w.shape[1]
        d_state = A_log.shape[1]
        x = jnp.einsum('bld,ed->bel', hidden_states, in_proj_w)
        xc = jax.lax.conv_general_dilated(x, conv_w, window_strides=(1,), padding=[(d_conv - 1, 0)], feature_group_count=d_inner, dimension_numbers=('NCH', 'OIH', 'NCH'))
        x = silu(xc + conv_b[None, :, None])
        x_dbl = jnp.einsum('bdl,ed->bel', x, x_proj_w)
        dt_low, Bm, Cm = jnp.split(x_dbl, [dt_rank, dt_rank + d_state], axis=1)
        dt = jnp.einsum('brl,dr->bdl', dt_low, dt_proj_w)
        dt = jax.nn.softplus(dt + dt_proj_b[None, :, None])
        A = -jnp.exp(A_log)
        dt_t = jnp.moveaxis(dt, -1, 0)
        B_t = jnp.moveaxis(Bm, -1, 0)
        C_t = jnp.moveaxis(Cm, -1, 0)
        u_t = jnp.moveaxis(x, -1, 0)

        def step(state, inp):
            d, b, c, u = inp
            dA = jnp.exp(d[..., None] * A)
            state = state * dA + (d * u)[..., None] * b[:, None, :]
            y = jnp.einsum('bdn,bn->bd', state, c)
            return (state, y)
        state0 = jnp.zeros((Bsz, d_inner, d_state), x.dtype)
        _, ys = jax.lax.scan(step, state0, (dt_t, B_t, C_t, u_t))
        y = jnp.moveaxis(ys, 0, 2)
        y = y + D[None, :, None] * x
        y = y * silu(z)
        return jnp.swapaxes(y, 1, 2)

    def _L0_ffn_ref(x, w_gate, w1, w2, w3):
        import jax, jax.numpy as jnp
        import numpy as np
        _Q_IN = 128
        _LUT_MIN = -128
        _Q_OUT = 1 << 16
        _TOP_K = 2
        _EXP_LUT = (jnp.exp(jnp.arange(_LUT_MIN, 1, dtype=jnp.float32) / _Q_IN) * _Q_OUT).astype(jnp.int32)

        def softmax_integer(logits):
            li = jnp.round(logits.astype(jnp.float32) * _Q_IN).astype(jnp.int32)
            shifted = jnp.clip(li - li.max(axis=-1, keepdims=True), _LUT_MIN, None)
            exp_vals = _EXP_LUT[shifted - _LUT_MIN]
            exp_sum = jnp.clip(exp_vals.sum(axis=-1, keepdims=True), 1, None)
            return exp_vals.astype(jnp.float32) / exp_sum.astype(jnp.float32)
        orig_shape = x.shape
        H = orig_shape[-1]
        xf = x.reshape(-1, H)
        T = xf.shape[0]
        E = w_gate.shape[0]
        router_logits = xf @ w_gate.T
        routing_weights = softmax_integer(router_logits)
        top_w, top_i = jax.lax.top_k(routing_weights, _TOP_K)
        top_w = top_w / top_w.sum(axis=-1, keepdims=True)
        combine = jnp.zeros((T, E), xf.dtype).at[jnp.arange(T)[:, None], top_i].add(top_w)
        out = jnp.zeros_like(xf)
        for e in range(E):
            h = jax.nn.silu(xf @ w1[e].T) * (xf @ w3[e].T)
            out = out + combine[:, e:e + 1] * (h @ w2[e].T)
        return out.reshape(orig_shape)

    def _L1_xattn_ref(x, ctx, pos_map, ctx_pos_map, Wq, Wkv, Wout, bout):
        import jax, jax.numpy as jnp
        import numpy as np
        DIM = 256
        CTX_DIM = 128
        N_HEADS = 32
        HEAD_DIM = DIM // N_HEADS
        POS_DIM = 2
        B, N, CTXN = (2, 256, 256)
        ROPE_BASE = 10000.0

        def apply_axial_rope(x, pos):
            b, n, h, d = x.shape
            p = pos.shape[-1]
            dpa = d // p
            half = dpa // 2
            freqs = ROPE_BASE ** (-jnp.arange(half, dtype=x.dtype) / half)
            ang = pos[..., :, None] * freqs
            cos = jnp.cos(ang)[:, :, None, :, :]
            sin = jnp.sin(ang)[:, :, None, :, :]
            xr = x.reshape(b, n, h, p, half, 2)
            x1, x2 = (xr[..., 0], xr[..., 1])
            out = jnp.stack([x1 * cos - x2 * sin, x1 * sin + x2 * cos], axis=-1)
            return out.reshape(b, n, h, d)
        b, n, _ = x.shape
        ctx_n = ctx.shape[1]
        q = (x @ Wq).reshape(b, n, N_HEADS, HEAD_DIM)
        k, v = jnp.split(ctx @ Wkv, 2, axis=-1)
        k = k.reshape(b, ctx_n, N_HEADS, HEAD_DIM)
        v = v.reshape(b, ctx_n, N_HEADS, HEAD_DIM)
        q = apply_axial_rope(q, pos_map)
        k = apply_axial_rope(k, ctx_pos_map)
        scale = 1.0 / np.sqrt(HEAD_DIM).astype(np.float32)
        logits = jnp.einsum('bqhd,bkhd->bhqk', q, k) * scale
        w = jax.nn.softmax(logits, axis=-1)
        attn = jnp.einsum('bhqk,bkhd->bqhd', w, v)
        attn = attn.reshape(b, n, N_HEADS * HEAD_DIM)
        return attn @ Wout + bout

    def _L1_ffn_ref(inputs, ln_w, ln_b, W1, b1, W2, b2):
        import jax, jax.numpy as jnp
        import numpy as np
        BLOCK = 32
        BITS = 8

        def bf16_round(x):
            return x.astype(jnp.bfloat16).astype(jnp.float32)

        def mx_quant(x):
            s = x.shape
            xb = x.reshape(s[:-1] + (s[-1] // BLOCK, BLOCK))
            amax = jnp.max(jnp.abs(xb), axis=-1, keepdims=True)
            shared_exp = jnp.floor(jnp.log2(jnp.where(amax > 0, amax, 1.0)))
            scale = jnp.exp2(shared_exp - (BITS - 2))
            q = jnp.clip(jnp.round(xb / scale), -2.0 ** (BITS - 1), 2.0 ** (BITS - 1) - 1) * scale
            q = jnp.where(amax > 0, q, 0.0).reshape(s)
            return x + jax.lax.stop_gradient(q - x)

        def mx_linear(x, W, b):
            y = jnp.einsum('btk,ok->bto', mx_quant(x), mx_quant(W))
            return bf16_round(y + b)

        def mx_layernorm(x, w, b, eps=1e-05):
            mu = jnp.mean(x, axis=-1, keepdims=True)
            var = jnp.mean(jnp.square(x - mu), axis=-1, keepdims=True)
            return bf16_round((x - mu) * jax.lax.rsqrt(var + eps) * w + b)

        def mx_gelu(x):
            c = jnp.float32(0.7978845608028654)
            return bf16_round(0.5 * x * (1.0 + jnp.tanh(c * (x + 0.044715 * x * x * x))))
        x = bf16_round(inputs)
        residual = bf16_round(inputs)
        h = mx_layernorm(x, ln_w, ln_b)
        h = mx_linear(h, W1, b1)
        h = mx_gelu(h)
        h = mx_linear(h, W2, b2)
        return bf16_round(residual + h)
    x = x + _L0_xattn_ref(ctx_1024, _layernorm(x, axis=-1), L0_xattn_in_proj_w, L0_xattn_conv_w, L0_xattn_conv_b, L0_xattn_x_proj_w, L0_xattn_dt_proj_w, L0_xattn_dt_proj_b, L0_xattn_A_log, L0_xattn_D)
    x = x + _L0_ffn_ref(_layernorm(x, axis=-1), L0_ffn_w_gate, L0_ffn_w1, L0_ffn_w2, L0_ffn_w3)
    x = x + _L1_xattn_ref(_layernorm(x, axis=-1), ctx_1024, fside_BxSx2_0, fside_BxSx2_0, L1_xattn_Wq, L1_xattn_Wkv, L1_xattn_Wout, L1_xattn_bout)
    x = x + _L1_ffn_ref(_layernorm(x, axis=-1), L1_ffn_ln_w, L1_ffn_ln_b, L1_ffn_W1, L1_ffn_b1, L1_ffn_W2, L1_ffn_b2)
    return x

_drawn_inputs = setup_inputs


def setup_inputs(seed=0):
    import zlib

    import numpy as np

    out = dict(_drawn_inputs(seed))
    spreads = {'L0_xattn_D': (1.0, 0.6),
     'L1_xattn_bout': (0.0, 0.1),
     'L1_ffn_ln_w': (1.0, 0.2),
     'L1_ffn_ln_b': (0.0, 0.294),
     'L1_ffn_b1': (0.0, 0.272),
     'L1_ffn_b2': (0.0, 0.1)}
    factors = {'L0_xattn_in_proj_w': 4.59,
     'L0_xattn_conv_w': 4.753,
     'L0_xattn_conv_b': 8.0,
     'L0_xattn_x_proj_w': 8.0,
     'L0_xattn_dt_proj_w': 8.0,
     'L0_xattn_dt_proj_b': 8.0,
     'L0_xattn_A_log': 8.0,
     'L0_ffn_w_gate': 3.558,
     'L0_ffn_w1': 3.154,
     'L0_ffn_w2': 3.123,
     'L0_ffn_w3': 3.126}
    for name, (base, spread) in spreads.items():
        noise = np.random.default_rng([zlib.crc32(name.encode()), seed]).standard_normal(out[name].shape)
        drawn = base * np.exp(spread * noise) if base else spread * noise
        out[name] = jnp.asarray(drawn.astype(out[name].dtype))
    for name, factor in factors.items():
        out[name] = (out[name] * factor).astype(out[name].dtype)
    return out
```

```python
from contextlib import ExitStack

import numpy as np

import concourse.bass as bass
from concourse import mybir

P = 128
B, L, H = 4, 256, 256
T = B * L
NT = T // P
CTX = 128
DI, NST, DTR, TAPS = 256, 16, 8, 4
ND = DI // P
PADL = L + TAPS - 1
E, I = 8, 704
IC = I // 2
KI = (I + P - 1) // P
SLOT_TILES = (2 * T + E * (P - 1)) // P
NHEAD, HD = 32, 8
HPU = 4
UNITS = B * NHEAD // HPU
HS = 32
F = 4 * H
BLK = 32
LUTN = 129
EPS = 1e-5
MAGIC = 12582912.0

F32, BF16, F16 = mybir.dt.float32, mybir.dt.bfloat16, mybir.dt.float16
I32, U32 = mybir.dt.int32, mybir.dt.uint32
ALU = mybir.AluOpType
ACT = mybir.ActivationFunctionType
AX = mybir.AxisListType

LOG1P = (2.00000002, 0.6666624, 0.40026449, 0.27953006, 0.28165458)

def _columns(*sizes):
    at, out = 0, {}
    for name, n in sizes:
        out[name] = (at, at + n)
        at += n
    return out, at


MIX, MIX_N = _columns(("in_proj", DI), ("x_proj_bc", ND * 96), ("x_proj_dt", ND * DTR), ("conv_w", ND * TAPS),
                      ("conv_b", ND), ("dt_b", ND), ("skip", ND), ("a_log", ND * NST))
CON, CON_N = _columns(("ident", P), ("lut", LUTN), ("lut_key", LUTN), ("expert_order", NT * E),
                      ("tile_index", SLOT_TILES + 1), ("ones", E), ("freq", NT * 8), ("rope_sign", NT * 8))
LATE, LATE_N = _columns(("wq", 2 * H), ("wkv", 2 * H), ("wout", 2 * H), ("bout", H), ("ln_w", H), ("ln_b", H),
                        ("b1", F), ("b2", H))
ROUTE, ROUTE_N = _columns(("w_gate", 2 * E), ("pos", NT * 8))


def need(eng, sem, value):
    if not isinstance(value, int) or value > 0:
        eng.wait_ge(sem, value)


def skewed(eng, count, stages):
    late = max(s for s, _ in stages)
    first = late + late % 2 + 2
    loops = (count - first) // 2

    def peeled(r):
        for s, stage in stages:
            if 0 <= r - s < count:
                stage(r - s, (r - s) % 2)

    for r in range(first):
        peeled(r)
    with eng.Fori(0, loops) as v:
        for j in range(2):
            for s, stage in stages:
                stage(v * 2 + (first + j - s), (j - s) % 2)
    for r in range(first + 2 * loops, count + late):
        peeled(r)


def build(nc, x, ctx_t, mix, dt_proj, route, w13, w2, late, ffn_w1, ffn_w2, con, con16, bc_select, ident_b, out,
          upto=4):
    routed = nc.dram_tensor("routed_rows", (SLOT_TILES * P, H), F32, kind="Internal").ap()
    expert_out = nc.dram_tensor("expert_rows", (SLOT_TILES * P, H), F32, kind="Internal").ap()

    with ExitStack() as ctx:
        def sb(name, shape, dt=F32):
            return ctx.enter_context(nc.sbuf_tensor(name, shape, dt))

        def sem(name):
            return ctx.enter_context(nc.semaphore(name))

        ps = ctx.enter_context(nc.psum_tensor("ps", [P, 8, 512], F32))

        xa = sb("resid", [P, NT, H])
        zrow = sb("zeros", [P, H])
        xn = sb("normed", [P, NT, H])
        ctxt = sb("ctx_t", [P, T])
        mixp = sb("mix_params", [P, MIX_N])
        dtp = sb("dt_proj", [P, DI])
        routep = sb("route_params", [P, ROUTE_N])
        cons = sb("constants", [P, CON_N])
        cons16 = sb("constants16", [P, 3 * P], F16)
        identb = sb("ident_b", [P, P], BF16)
        w1q = sb("w1_quant_t", [P, 2, F], BF16)
        w2q = sb("w2_quant_t", [P, F // P, H], BF16)
        stats = sb("stats", [P, NT, 6])
        mv = sb("mean_var", [P, NT, 2])
        sd = sb("deviation", [P, NT])
        rs = sb("inv_deviation", [P, NT])
        gate_w = sb("gate_weights", [P, 2, NT])
        slots_i = sb("slots", [P, 2, NT], I32)
        tile_expert = sb("tile_expert", [P, SLOT_TILES + 1], I32)
        W13E = 2 * 2 * I
        W2E = KI * H
        weights = sb("weights", [P, E * (W13E + W2E)])
        work = sb("work", [P, 8000])

        w13s = weights[:, 0:E * W13E].rearrange("p (e m k n) -> p e m k n", e=E, m=2, k=2)
        w2s = weights[:, E * W13E:].rearrange("p (e j n) -> p e j n", e=E, j=KI)

        class Carve:
            def __init__(self, base, at=0):
                self.base, self.at = base, at

            def __call__(self, n, dt=F32):
                words = n if dt in (F32, I32, U32) else (n + 1) // 2
                got = self.base[:, self.at:self.at + words]
                self.at += words
                assert self.at <= self.base.shape[1], (self.at, self.base.shape)
                return got if dt == F32 else got.bitcast(dt)

        def col(table, tensor, name, a=0, b=None):
            lo, hi = table[name]
            return tensor[:, lo + a:(hi if b is None else lo + b)]

        ident = col(CON, cons, "ident")
        ident16, before16, ones16 = (cons16[:, i * P:(i + 1) * P] for i in range(3))

        EARLY = 5
        c = Carve(weights, EARLY * W13E)
        sel = c(32 * P, BF16)
        bcst = c(T, BF16)
        u = c(ND * T).rearrange("p (d t) -> p d t", d=ND)
        dts = c(ND * T).rearrange("p (d t) -> p d t", d=ND)
        dtu = c(ND * T).rearrange("p (d t) -> p d t", d=ND)
        decay = [[c(T) for _ in range(ND)] for _ in range(2)]
        state = [[c(T) for _ in range(ND)] for _ in range(2)]
        drive = [c(T) for _ in range(ND)]
        acoef = c(ND * NST)
        c = Carve(work)
        crow = [c(T) for _ in range(2)]
        dtl = c(T)
        c2 = Carve(weights, EARLY * W13E + 16 * P)
        c2.at = EARLY * W13E + 16 * P + T // 2 + 3 * ND * T
        xpad = c2(ND * B * PADL).rearrange("p (d b l) -> p d b l", d=ND, b=B)
        conv = c2(ND * T).rearrange("p (d t) -> p d t", d=ND)
        c3 = Carve(weights, EARLY * W13E + 16 * P + T // 2 + 3 * ND * T)
        sp_abs, sp_exp, sp_rec = (c3(ND * T) for _ in range(3))
        sp_relu = c3(ND * T)
        c3b = Carve(work, 3 * T)
        rem = c3b(T)
        sp_s, sp_s2 = sp_rec, sp_abs

        in_x, in_mix, in_misc, in_con, in_late, in_ffnw, out_done, zeroed = map(
            sem, ("in_x", "in_mix", "in_misc", "in_con", "in_late", "in_ffnw", "out_done", "zeroed"))
        in_w = sem("in_w")
        ln_stats, ln_mv, ln_sd, ln_out, ln_chain = map(sem, ("ln_stats", "ln_mv", "ln_sd", "ln_out", "ln_chain"))
        dve_step, act_step = sem("dve_step"), sem("act_step")
        zero_pad, proj_mm, proj_copied, conv_done, u_done = map(
            sem, ("zero_pad", "proj_mm", "proj_copied", "conv_done", "u_done"))
        xproj_mm, bc_top, dtl_copied, dt_mm, sp_parts, sp_sq, bc_split, dt_ready, a_ready = map(
            sem, ("xproj_mm", "bc_top", "dtl_copied", "dt_mm", "sp_parts", "sp_sq", "bc_split", "dt_ready", "a_ready"))
        b_mm, c_mm, c_copied, decay_done, drive_done, scan_done, prod_done, y_mm = map(
            sem, ("b_mm", "c_mm", "c_copied", "decay_done", "drive_done", "scan_done", "prod_done", "y_mm"))
        gate_done, gated, yt_mm, mixed = map(sem, ("gate_done", "gated", "yt_mm", "mixed"))
        xnt_mm, xnt_copied, logit_mm, picked, rank_mm, slots_ready, scattered = map(
            sem, ("xnt_mm", "xnt_copied", "logit_mm", "picked", "rank_mm", "slots_ready", "scattered"))
        wt_mm, wt_copied, wquant = map(sem, ("wt_mm", "wt_copied", "wquant"))
        row_in = [sem(f"row_in{i}") for i in range(2)]
        row_out = [sem(f"row_out{i}") for i in range(2)]
        row_mm, rowt_copied, up_mm, silu_done, h_done, ht_mm, ht_copied, down_mm, down_copied = map(
            sem, ("row_mm", "rowt_copied", "up_mm", "silu_done", "h_done", "ht_mm", "ht_copied", "down_mm",
                  "down_copied"))
        gathered = [sem(f"gathered{i}") for i in range(4)]
        combined = sem("combined")
        stack_zero, kv_mm, v_copied, roped, cast_hi, stacked, q_mm, rope_tab, sin_done = map(
            sem, ("stack_zero", "kv_mm", "v_copied", "roped", "cast_hi", "stacked", "q_mm", "rope_tab", "sin_done"))
        t1_mm, t1_copied, mx_mm, mx_done, shift_done, t2_mm, t2_copied, s_mm, exp_done, v_unit = map(
            sem, ("t1_mm", "t1_copied", "mx_mm", "mx_done", "shift_done", "t2_mm", "t2_copied", "s_mm", "exp_done",
                  "v_unit"))
        pv_mm, o_copied, ot_mm, o_norm, at_mm, at_copied, wo_mm, attn_done = map(
            sem, ("pv_mm", "o_copied", "ot_mm", "o_norm", "at_mm", "at_copied", "wo_mm", "attn_done"))
        o_rec, shift_hi, fq_chain, f2_chain, hq_ready = map(
            sem, ("o_rec", "shift_hi", "fq_chain", "f2_chain", "hq_ready"))
        hq_mm, hq_copied, f1_mm, f1_done, gelu_done, fq_done, ft_mm, ft_copied, f2_mm, f2_done = map(
            sem, ("hq_mm", "hq_copied", "f1_mm", "f1_done", "gelu_done", "fq_done", "ft_mm", "ft_copied", "f2_mm",
                  "f2_done"))

        c = Carve(work)
        rt = [c(NT * E) for _ in range(12)]
        rt_lut = c(NT * LUTN)
        mask16 = c(NT * E, F16)
        small = [c(NT) for _ in range(6)]
        cum = c(4 * E)
        texp = c((SLOT_TILES + 1) * E)
        xnt_at = c.at
        xnt = c(2 * T).rearrange("p (k t) -> p k t", k=2)
        fwq = c(2 * T, BF16)
        fw_y = c(2 * T)
        fw_scr = [c(64) for _ in range(4)]
        c = Carve(work, xnt_at)
        xg = [c(H) for _ in range(2)]
        xgt = [c(2 * P) for _ in range(2)]
        silu_h = [c(I) for _ in range(2)]
        hbuf = [c(I) for _ in range(2)]
        c = Carve(work)
        ht = [c(KI * P).rearrange("p (j s) -> p j s", j=KI) for _ in range(2)]
        yrow = [c(H) for _ in range(2)]
        assert c.at <= xnt_at
        fw_raw = [weights[:, (EARLY + m) * W13E:(EARLY + m) * W13E + 2048] for m in range(2)]

        c = Carve(weights)
        gat = [[c(H) for _ in range(2)] for _ in range(4)]
        late_s = c(LATE_N)
        late_end = c.at
        qst = c(UNITS * 2 * P, F16).rearrange("p (u t r) -> p u t r", u=UNITS, t=2)
        kst = c(UNITS * 2 * P, F16).rearrange("p (u t r) -> p u t r", u=UNITS, t=2)
        vst = c(UNITS * 2 * P).rearrange("p (u t r) -> p u t r", u=UNITS, t=2)
        rope_a = c(NT * H)
        rope_b = c(NT * H)
        xnt3 = c(2 * T).rearrange("p (k t) -> p k t", k=2)
        cos8, sin8, ang = c(NT * 8), c(NT * 8), c(2 * NT * 8)
        ang2 = c(2 * NT * 8)
        qkt = [c(4 * P, F16) for _ in range(2)]
        q2t = [c(2 * P, F16) for _ in range(2)]
        pexp = [c(HPU * 2 * L) for _ in range(2)]
        vu = [c(2 * P).rearrange("p (t r) -> p t r", t=2) for _ in range(2)]
        ost = [c(L) for _ in range(2)]
        mx = [c(2 * HPU) for _ in range(2)]
        nml = c(2 * HPU)
        orec = c(2 * HPU)
        attn = rope_b.rearrange("p (t u r) -> p t u r", t=2, u=UNITS)
        attnt = xnt3
        c = Carve(weights, late_end)
        xb = c(NT * H, BF16).rearrange("p (t h) -> p t h", t=NT)
        hn = c(NT * H)
        hb = c(NT * H, BF16)
        hqb = c(NT * H, BF16)
        hqt = c(2 * T, BF16).rearrange("p (k t) -> p k t", k=2)
        qs = [c(NT * H // BLK) for _ in range(4)]
        f1 = [c(F, BF16) for _ in range(2)]
        g1 = [c(F, BF16) for _ in range(2)]
        gy = [c(F, BF16) for _ in range(2)]
        gq = [c(F, BF16) for _ in range(2)]
        gqt = [c(F, BF16).rearrange("p (k t) -> p k t", k=F // P) for _ in range(2)]
        fs = [[c(F // BLK) for _ in range(4)] for _ in range(2)]
        f2 = [c(H, BF16) for _ in range(2)]
        r4 = [c(H, BF16) for _ in range(2)]

        bank16 = [ps[:, b, :].bitcast(F16) for b in range(8)]
        bankb = [ps[:, b, :].bitcast(BF16) for b in range(8)]
        block = ctx.enter_context(nc.Block())
        QN = 2

        @block.sync
        def _(sp):
            sp.dma_start(ctxt[:], ctx_t).then_inc(in_mix, 16)
            sp.dma_start(mixp[:], mix).then_inc(in_mix, 16)
            sp.dma_start(dtp[0:DTR, :], dt_proj).then_inc(in_mix, 16)
            sp.dma_start(xa[:], x.rearrange("(t p) h -> p t h", p=P)).then_inc(in_x, 16)
            sp.dma_start(sel, bc_select).then_inc(in_misc, 16)
            sp.dma_start(cons[:], con).then_inc(in_con, 16)
            sp.dma_start(cons16[:], con16).then_inc(in_con, 16)
            sp.dma_start(identb[:], ident_b).then_inc(in_con, 16)
            sp.dma_start(routep[:], route).then_inc(in_con, 16)
            if upto >= 2:
                for e in range(EARLY):
                    sp.dma_start(w13s[:, e].rearrange("p m k n -> p (m k n)"), w13[e]).then_inc(in_w, 16)
                sp.wait_ge(zero_pad, 3)
                sp.dma_start(routed.rearrange("(i p) h -> p i h", p=P),
                             zrow[:].unsqueeze(1).broadcast_to([P, SLOT_TILES, H])).then_inc(zeroed, 16)
                sp.wait_ge(mixed, B)
                for m, src in enumerate((ffn_w1, ffn_w2)):
                    sp.dma_start(fw_raw[m], src).then_inc(in_ffnw, 16)
                for e in range(E):
                    sp.dma_start(w2s[:, e].rearrange("p j n -> p (j n)"), w2[e]).then_inc(in_w, 16)
                for e in range(EARLY + 2, E):
                    sp.dma_start(w13s[:, e].rearrange("p m k n -> p (m k n)"), w13[e]).then_inc(in_w, 16)
                sp.wait_ge(wquant, QN)
                for e in range(EARLY, EARLY + 2):
                    sp.dma_start(w13s[:, e].rearrange("p m k n -> p (m k n)"), w13[e]).then_inc(in_w, 16)

                sp.wait_ge(scattered, 32 * NT)

                def load_rows(i, b):
                    need(sp, row_mm, i - 1)
                    sp.dma_start(xg[b], routed[bass.ds(i * P, P), :]).then_inc(row_in[b], 16)

                def store_rows(i, b):
                    sp.wait_ge(down_copied, i + 1)
                    sp.dma_start(expert_out[bass.ds(i * P, P), :], yrow[b]).then_inc(row_out[b], 16)

                skewed(sp, SLOT_TILES, [(0, load_rows), (3, store_rows)])
            if upto >= 3:
                sp.wait_ge(down_mm, SLOT_TILES)
                sp.dma_start(late_s, late).then_inc(in_late, 16)
            if upto < 4:
                sp.wait_ge([None, mixed, combined, attn_done][upto], [None, B, NT, NT][upto])
                sp.dma_start(out.rearrange("(t p) h -> p t h", p=P), xa[:]).then_inc(out_done, 16)
                sp.wait_ge(out_done, 16)
            else:
                with sp.Fori(0, NT) as t:
                    sp.wait_ge(f2_done, t + 1)
                    sp.dma_start(out[bass.ds(t * P, P), :], xa[:, bass.ds(t, 1), :].rearrange("p a h -> p (a h)")) \
                      .then_inc(out_done, 16)
                sp.wait_ge(out_done, 16 * NT)

        @block.gpsimd
        def _(pool):
            nc.gpsimd.memset(xpad[:, :, :, 0:TAPS - 1], 0.0).then_inc(zero_pad, 1)
            nc.gpsimd.memset(bcst, 0.0).then_inc(zero_pad, 1)
            nc.gpsimd.memset(zrow[:], 0.0).then_inc(zero_pad, 1)

            def times_c(n, b):
                pool.wait_ge(c_copied, n + 1)
                for d in range(ND):
                    pool.wait_ge(scan_done, n * ND + (d + 1))
                    nc.gpsimd.tensor_tensor(state[b][d], state[b][d], crow[b], ALU.mult).then_inc(prod_done, 1)

            skewed(pool, NST, [(0, times_c)])
            if upto < 2:
                return
            pool.wait_ge(zeroed, 16)
            pool.wait_ge(slots_ready, 1)
            pool.wait_ge(ln_out, 2 * NT)
            for t in range(NT):
                for s in range(2):
                    pool.indirect_dma_start(
                        routed, bass.IndirectOffsetOnAxis(ap=slots_i[:, s, t:t + 1].bitcast(U32), axis=0),
                        xn[:, t, :], None).then_inc(scattered, 16)
            for b in range(2):
                pool.wait_ge(row_out[b], 16 * ((SLOT_TILES + 1 - b) // 2))
            pool.wait_ge(down_mm, SLOT_TILES)
            for t in range(NT):
                need(pool, combined, t - 3)
                for s in range(2):
                    pool.indirect_dma_start(
                        gat[t % 4][s], None, expert_out,
                        bass.IndirectOffsetOnAxis(ap=slots_i[:, s, t:t + 1].bitcast(U32), axis=0),
                        ).then_inc(gathered[t % 4], 16)
            if upto < 3:
                return
            nc.gpsimd.memset(kst.rearrange("p u t r -> p (u t r)").bitcast(U32), 0).then_inc(stack_zero, 1)
            nc.gpsimd.memset(vst.rearrange("p u t r -> p (u t r)").bitcast(U32), 0).then_inc(stack_zero, 1)
            nc.gpsimd.memset(qst.rearrange("p u t r -> p (u t r)").bitcast(U32), 0).then_inc(stack_zero, 1)
            pool.wait_ge(stack_zero, 3)
            nc.gpsimd.memset(kst.rearrange("p u t (j r) -> p (u t j) r", r=HS)[:, :, 24:26], 1.0) \
              .then_inc(stack_zero, 1)
            nc.gpsimd.memset(vst.rearrange("p u t (j r) -> p (u t j) r", r=HS)[:, :, 8:9], 1.0) \
              .then_inc(stack_zero, 1)
            pool.wait_ge(v_copied, NT)
            pool.wait_ge(stack_zero, 5)

            def copy_v(n, b):
                need(pool, pv_mm, n - 1)
                nc.gpsimd.tensor_copy(vu[b], vst[:, bass.ds(n, 1)].rearrange("p a t r -> p (a t) r")) \
                  .then_inc(v_unit, 1)

            skewed(pool, UNITS, [(0, copy_v)])

        @block.tensor
        def _(pe):
            mm = nc.tensor.matmul
            pe.wait_ge(in_mix, 48)
            for d in range(ND):
                for h in range(2):
                    last = mm(ps[:, 2 * d + h, :], col(MIX, mixp, "in_proj", d * P, (d + 1) * P),
                              ctxt[:, h * 512:(h + 1) * 512], start=True, stop=True)
                last.then_inc(proj_mm, 1)
            for d in range(ND):
                pe.wait_ge(u_done, d + 1)
                for h in range(2):
                    uh = u[:, d, h * 512:(h + 1) * 512]
                    mm(ps[0:96, 4 + h, :], col(MIX, mixp, "x_proj_bc", d * 96, (d + 1) * 96), uh,
                       start=(d == 0), stop=(d == ND - 1))
                    last = mm(ps[0:DTR, 6 + h, :], col(MIX, mixp, "x_proj_dt", d * DTR, (d + 1) * DTR), uh,
                              start=(d == 0), stop=(d == ND - 1))
            last.then_inc(xproj_mm, 1)
            pe.wait_ge(dtl_copied, 1)
            for d in range(ND):
                for h in range(2):
                    last = mm(ps[:, 2 * d + h, :], dtp[0:DTR, d * P:(d + 1) * P], dtl[0:DTR, h * 512:(h + 1) * 512],
                              start=True, stop=True)
                last.then_inc(dt_mm, 1)
            pe.wait_ge(sp_parts, 2 * ND)
            pe.wait_ge(bc_split, 1)
            pe.wait_ge(in_misc, 16)
            pe.wait_ge(in_con, 64)

            def spread(n, b):
                need(pe, drive_done, 2 * n)
                lhs = sel[:, bass.ds(n * P, P)]
                for h in range(2):
                    last = mm(ps[:, h, :], lhs, bcst[:, h * 512:(h + 1) * 512], start=True, stop=True)
                last.then_inc(b_mm, 1)
                need(pe, c_copied, n)
                lhs = sel[:, bass.ds(n * P + NST * P, P)]
                for h in range(2):
                    last = mm(ps[:, 2 + h, :], lhs, bcst[:, h * 512:(h + 1) * 512], start=True, stop=True)
                last.then_inc(c_mm, 1)

            def add_y(n, b):
                for d in range(ND):
                    pe.wait_ge(prod_done, n * ND + (d + 1))
                    for h in range(2):
                        last = mm(ps[:, 4 + 2 * d + h, :], ident, state[b][d][:, h * 512:(h + 1) * 512],
                                  start=isinstance(n, int) and n == 0, stop=isinstance(n, int) and n == NST - 1)
                    last.then_inc(y_mm, 1)

            skewed(pe, NST, [(0, spread), (2, add_y)])
            pe.wait_ge(gated, ND)
            for b in range(B):
                for h in range(2):
                    for d in range(ND):
                        last = nc.tensor.transpose(ps[:, b, h * H + d * P:h * H + (d + 1) * P],
                                                   drive[d][:, b * L + h * P:b * L + (h + 1) * P], ident)
                last.then_inc(yt_mm, 1)
            if upto < 2:
                return

            def transpose_normed(dst_banks, seen):
                pe.wait_ge(ln_out, seen)
                for k in range(2):
                    for half in range(2):
                        for t in range(4):
                            last = nc.tensor.transpose(ps[:, dst_banks + 2 * k + half, t * P:(t + 1) * P],
                                                       xn[:, half * 4 + t, k * P:(k + 1) * P], ident)
                    last.then_inc(xnt_mm, 1)

            pe.wait_ge(mixed, B)
            transpose_normed(4, 2 * NT)
            pe.wait_ge(xnt_copied, 2)
            for t in range(NT):
                for k in range(2):
                    last = mm(ps[:, 0, t * E:(t + 1) * E], xnt[:, k, t * P:(t + 1) * P],
                              col(ROUTE, routep, "w_gate", k * E, (k + 1) * E),
                              start=(t == 0 and k == 0), stop=(t == NT - 1 and k == 1), skip_group_check=True)
            last.then_inc(logit_mm, 1)
            pe.wait_ge(picked, 1)
            mm(ps[:, 1, 0:NT * E], before16, mask16, start=True, stop=False, skip_group_check=True)
            for t in range(NT - 1):
                after = NT - 1 - t
                mm(ps[:, 1, (t + 1) * E:NT * E], ones16,
                   mask16[:, t * E:(t + 1) * E].unsqueeze(1).broadcast_to([P, after, E]),
                   start=False, stop=(t == NT - 2), skip_group_check=True)
            for t in range(NT):
                last = mm(ps[:, 2, 0:E], ones16, mask16[:, t * E:(t + 1) * E], start=(t == 0), stop=(t == NT - 1))
            last.then_inc(rank_mm, 1)
            for m in range(QN):
                pe.wait_ge(wquant, m + 1)
                need(pe, wt_copied, 2 * m)
                for q in range(2):
                    for t in range(8):
                        src = fwq[:, t * H + q * P:t * H + (q + 1) * P] if m == 0 else \
                            fwq[:, q * F + t * P:q * F + (t + 1) * P]
                        last = nc.tensor.transpose(bankb[4 + q][:, t * P:(t + 1) * P], src, identb[:])
                    last.then_inc(wt_mm, 1)
            pe.wait_ge(wt_copied, 2 * QN)
            pe.wait_ge(slots_ready, 1)
            pe.wait_ge(in_w, 16 * 2 * E)

            def expert_of(i):
                return pe.value_load(tile_expert[0:1, bass.ds(i, 1)], min_val=0, max_val=E - 1)

            def turn_rows(i, b):
                pe.wait_ge(row_in[b], (i // 2) * 16 + 16 if isinstance(i, int) else (i - b) * 8 + 16)
                need(pe, rowt_copied, i)
                for k in range(2):
                    last = nc.tensor.transpose(ps[:, 6, k * P:(k + 1) * P], xg[b][:, k * P:(k + 1) * P], ident)
                last.then_inc(row_mm, 1)

            def up(i, b):
                e = expert_of(i)
                pe.wait_ge(rowt_copied, i + 1)
                need(pe, h_done, i)
                for m in range(2):
                    for h in range(2):
                        for k in range(2):
                            last = mm(ps[:, 2 * m + h, 0:IC], xgt[b][:, k * P:(k + 1) * P],
                                      w13s[:, bass.ds(e, 1), m, k, h * IC:(h + 1) * IC]
                                      .rearrange("p a n -> p (a n)"), start=(k == 0), stop=(k == 1))
                    last.then_inc(up_mm, 1)

            def turn_h(i, b):
                pe.wait_ge(h_done, i + 1)
                need(pe, ht_copied, 2 * i)
                for j in range(KI):
                    w = min(P, I - j * P)
                    last = nc.tensor.transpose(ps[0:w, 4 + j // 3, (j % 3) * P:(j % 3 + 1) * P],
                                               hbuf[b][:, j * P:j * P + w], ident)
                    if j % 3 == 2:
                        last.then_inc(ht_mm, 1)

            def down(i, b):
                e = expert_of(i)
                pe.wait_ge(ht_copied, 2 * i + 2)
                need(pe, down_copied, i)
                for j in range(KI):
                    w = min(P, I - j * P)
                    last = mm(ps[:, 7, 0:H], ht[b][0:w, j, :],
                              w2s[0:w, bass.ds(e, 1), j, :].rearrange("p a n -> p (a n)"),
                              start=(j == 0), stop=(j == KI - 1))
                last.then_inc(down_mm, 1)

            skewed(pe, SLOT_TILES, [(2, turn_h), (0, turn_rows), (1, up), (2, down)])
            if upto < 3:
                return

            pe.wait_ge(in_late, 16)
            pe.wait_ge(down_copied, SLOT_TILES)
            for t in range(NT):
                last = mm(ps[:, t, :], ctxt[:, t * P:(t + 1) * P], col(LATE, late_s, "wkv"), start=True, stop=True)
                last.then_inc(kv_mm, 1)
            pe.wait_ge(roped, 1)
            transpose_normed(0, 3 * NT)
            pe.wait_ge(xnt_copied, 4)
            for t in range(NT):
                for k in range(2):
                    last = mm(ps[:, 4 + t // 2, (t % 2) * H:(t % 2 + 1) * H], xnt3[:, k, t * P:(t + 1) * P],
                              col(LATE, late_s, "wq", k * H, (k + 1) * H), start=(k == 0), stop=(k == 1))
            last.then_inc(q_mm, 1)
            pe.wait_ge(stacked, 2)
            pe.wait_ge(roped, 2)

            def turn_qk(n, b):
                need(pe, t2_copied, n - 1)
                need(pe, t1_copied, n)
                for a, st in enumerate((qst, kst)):
                    for t in range(2):
                        last = mm(ps[:, 6, (2 * a + t) * P:(2 * a + t + 1) * P],
                                  st[:, bass.ds(n, 1), t, :].rearrange("p a r -> p (a r)"), ident16,
                                  start=(a + t == 0), stop=(a + t == 3), skip_group_check=True)
                last.then_inc(t1_mm, 1)

            def row_scores(n, b):
                pe.wait_ge(t1_copied, n + 1)
                for half in range(2):
                    need(pe, mx_done, 2 * n + half - 1)
                    for j in range(2 * half, 2 * half + 2):
                        r = slice(j * HS, (j + 1) * HS)
                        for t in range(2):
                            last = mm(ps[:, j, t * L:(t + 1) * L], qkt[b][r, t * P:(t + 1) * P],
                                      qkt[b][r, 2 * P:4 * P], start=(t == 0), stop=(t == 1), skip_group_check=True)
                    last.then_inc(mx_mm, 1)

            def turn_q(n, b):
                pe.wait_ge(shift_done, n + 1)
                pe.wait_ge(t1_copied, n + 2 if not isinstance(n, int) else min(n + 2, UNITS))
                need(pe, t2_copied, n)
                for t in range(2):
                    last = mm(ps[:, 6, t * P:(t + 1) * P], qst[:, bass.ds(n, 1), t, :].rearrange("p a r -> p (a r)"),
                              ident16, start=(t == 0), stop=(t == 1), skip_group_check=True)
                last.then_inc(t2_mm, 1)

            def key_scores(n, b):
                pe.wait_ge(t2_copied, n + 1)
                for j in range(HPU):
                    need(pe, exp_done, HPU * n + (j - 1))
                    r = slice(j * HS, (j + 1) * HS)
                    for t in range(2):
                        last = mm(ps[:, 4 + j % 2, t * L:(t + 1) * L], qkt[b][r, (2 + t) * P:(3 + t) * P],
                                  q2t[b][r, :], start=(t == 0), stop=(t == 1), skip_group_check=True)
                    last.then_inc(s_mm, 1)

            def weigh_v(n, b):
                pe.wait_ge(exp_done, HPU * n + HPU)
                pe.wait_ge(v_unit, n + 1)
                need(pe, o_norm, n)
                for t in range(2):
                    for j in range(HPU):
                        last = mm(ps[j * HS:(j + 1) * HS, 7, 0:L], vu[b][:, t, j * HS:(j + 1) * HS],
                                  pexp[b][:, (j * 2 + t) * L:(j * 2 + t + 1) * L], start=(t == 0), stop=(t == 1),
                                  skip_group_check=True)
                last.then_inc(pv_mm, 1)

            def turn_o(n, b):
                pe.wait_ge(o_copied, n + 1)
                for t in range(2):
                    last = nc.tensor.transpose(ps[:, 7, L + t * P:L + (t + 1) * P], ost[b][:, t * P:(t + 1) * P],
                                               ident)
                last.then_inc(ot_mm, 1)

            skewed(pe, UNITS, [(4, turn_o), (1, row_scores), (2, turn_q), (2, key_scores), (0, turn_qk),
                               (3, weigh_v)])
            pe.wait_ge(o_norm, UNITS)
            pe.wait_ge(mx_done, 2 * UNITS)
            for k in range(2):
                for t in range(NT):
                    last = nc.tensor.transpose(
                        ps[:, 2 * k + t // 4, (t % 4) * P:(t % 4 + 1) * P],
                        attn[:, t % 2, (t // 2) * 8 + 4 * k:(t // 2) * 8 + 4 * k + 4, :]
                        .rearrange("p u r -> p (u r)"), ident)
                last.then_inc(at_mm, 1)
            pe.wait_ge(at_copied, 2)
            for t in range(NT):
                for k in range(2):
                    last = mm(ps[:, 4 + t // 2, (t % 2) * H:(t % 2 + 1) * H], attnt[:, k, t * P:(t + 1) * P],
                              col(LATE, late_s, "wout", k * H, (k + 1) * H), start=(k == 0), stop=(k == 1))
            last.then_inc(wo_mm, 1)
            if upto < 4:
                return

            pe.wait_ge(hq_ready, 1)
            for k in range(2):
                for t in range(NT):
                    last = nc.tensor.transpose(bankb[k][:, t * P:(t + 1) * P],
                                               hqb[:, t * H + k * P:t * H + (k + 1) * P], identb[:])
                last.then_inc(hq_mm, 1)
            pe.wait_ge(hq_copied, 2)

            def widen(t, b):
                need(pe, f1_done, t - 1)
                for h in range(2):
                    for k in range(2):
                        last = mm(ps[:, 2 * b + h, :], hqt[:, k, bass.ds(t * P, P)], w1q[:, k, h * 512:(h + 1) * 512],
                                  start=(k == 0), stop=(k == 1))
                last.then_inc(f1_mm, 1)

            def turn_f(t, b):
                pe.wait_ge(fq_done, t + 1)
                need(pe, ft_copied, t - 1)
                for j in range(F // P):
                    last = nc.tensor.transpose(bankb[4 + b][:, j * P:(j + 1) * P], gq[b][:, j * P:(j + 1) * P],
                                               identb[:])
                last.then_inc(ft_mm, 1)

            def narrow(t, b):
                pe.wait_ge(ft_copied, t + 1)
                need(pe, f2_done, t - 1)
                for j in range(F // P):
                    last = mm(ps[:, 6 + b, 0:H], gqt[b][:, j, :], w2q[:, j, :], start=(j == 0),
                              stop=(j == F // P - 1))
                last.then_inc(f2_mm, 1)

            skewed(pe, NT, [(0, widen), (1, turn_f), (2, narrow)])

        @block.scalar
        def _(act):
            A = nc.scalar.activation
            ln_round = [0]

            def deviation():
                ln_round[0] += 1
                act.wait_ge(ln_mv, NT * ln_round[0])
                A(sd[:], mv[:, :, 1], ACT.Sqrt, bias=eps_t).then_inc(ln_sd, 1)

            eps_t = EPS
            deviation()
            for d in range(ND):
                act.wait_ge(proj_mm, d + 1)
                for h in range(2):
                    A(xpad[:, d, 2 * h:2 * h + 2, TAPS - 1:], ps[:, 2 * d + h, :].rearrange("p (b l) -> p b l", b=2),
                      ACT.Copy).then_inc(proj_copied, 1)
            for d in range(ND):
                act.wait_ge(conv_done, d + 1)
                A(u[:, d, :], conv[:, d, :], ACT.Silu, bias=col(MIX, mixp, "conv_b", d, d + 1)).then_inc(u_done, 1)
            act.wait_ge(ln_out, NT)
            A(xn[:], xn[:], ACT.Silu).then_inc(gate_done, 1)
            act.wait_ge(xproj_mm, 1)
            A(dtl[0:DTR, :], ps[0:DTR, 6:8, :], ACT.Copy).then_inc(dtl_copied, 1)
            act.wait_ge(zero_pad, 2)
            A(bcst[0:96, :], ps[0:96, 4:6, :], ACT.Copy).then_inc(bc_top, 1)
            A(acoef, col(MIX, mixp, "a_log"), ACT.Exp).then_inc(act_step, 1)
            act.wait_ge(act_step, 1)
            A(acoef, acoef, ACT.Copy, scale=-1.0).then_inc(a_ready, 1)
            for d in range(ND):
                act.wait_ge(dt_mm, d + 1)
                v = ps[:, 2 * d:2 * d + 2, :]
                bias = col(MIX, mixp, "dt_b", d, d + 1)
                A(sp_abs[:, d * T:(d + 1) * T], v, ACT.Abs, bias=bias).then_inc(sp_parts, 1)
                A(sp_relu[:, d * T:(d + 1) * T], v, ACT.Relu, bias=bias).then_inc(sp_parts, 1)
            act.wait_ge(sp_parts, 2 * ND)
            A(sp_exp, sp_abs, ACT.Exp, scale=-1.0).then_inc(sp_sq, 1)
            act.wait_ge(dve_step, 1)
            A(sp_s2, sp_s, ACT.Square).then_inc(sp_sq, 1)
            act.wait_ge(a_ready, 1)
            act.wait_ge(dt_ready, 1)

            def decays(n, b):
                for d in range(ND):
                    need(act, scan_done, ND * (n - 2) + (d + 1) if not isinstance(n, int) or n >= 2 else 0)
                    A(decay[b][d], dts[:, d, :], ACT.Exp, scale=acoef[:, bass.ds(n + d * NST, 1)]) \
                        .then_inc(decay_done, 1)

            def copy_c(n, b):
                act.wait_ge(c_mm, n + 1)
                need(act, prod_done, ND * (n - 1))
                A(crow[b], ps[:, 2:4, :], ACT.Copy).then_inc(c_copied, 1)

            skewed(act, NST, [(0, decays), (0, copy_c)])
            if upto < 2:
                return

            def copy_normed(dst, bank, seen):
                for k in range(2):
                    act.wait_ge(xnt_mm, seen + k + 1)
                    A(dst[:, k, :], ps[:, bank + 2 * k:bank + 2 * k + 2, :], ACT.Copy).then_inc(xnt_copied, 1)

            deviation()
            copy_normed(xnt, 4, 0)
            for m, dst in enumerate((w1q, w2q)):
                for q in range(2):
                    act.wait_ge(wt_mm, 2 * m + q + 1)
                    if m == 0:
                        A(w1q[:, q, :], bankb[4 + q], ACT.Copy).then_inc(wt_copied, 1)
                    else:
                        A(w2q[:, :, q * P:(q + 1) * P], bankb[4 + q].rearrange("p (t r) -> p t r", r=P),
                          ACT.Copy).then_inc(wt_copied, 1)

            act.wait_ge(slots_ready, 1)
            act.wait_ge(logit_mm, 1)

            def copy_rows(i, b):
                act.wait_ge(row_mm, i + 1)
                need(act, up_mm, 2 * i - 2)
                A(xgt[b], ps[:, 6, 0:2 * P], ACT.Copy).then_inc(rowt_copied, 1)

            def silus(i, b):
                act.wait_ge(up_mm, 2 * i + 1)
                need(act, h_done, i - 1)
                A(silu_h[b].rearrange("p (h n) -> p h n", h=2), ps[:, 0:2, 0:IC], ACT.Silu).then_inc(silu_done, 1)

            def copy_ht(i, b):
                act.wait_ge(ht_mm, 2 * i + 1)
                need(act, down_mm, i - 1)
                A(ht[b][:, 0:3, :], ps[:, 4, 0:3 * P], ACT.Copy).then_inc(ht_copied, 1)
                act.wait_ge(ht_mm, 2 * i + 2)
                A(ht[b][:, 3:5, :], ps[:, 5, 0:2 * P], ACT.Copy)
                A(ht[b][0:I - 5 * P, 5, :], ps[0:I - 5 * P, 5, 2 * P:3 * P], ACT.Copy).then_inc(ht_copied, 1)

            skewed(act, SLOT_TILES, [(2, copy_ht), (0, copy_rows), (1, silus)])
            if upto < 3:
                return

            act.wait_ge(stack_zero, 5)
            for t in range(NT):
                act.wait_ge(kv_mm, t + 1)
                A(vst.rearrange("p (b g) t (j r) -> p b g t j r", b=B, r=HS)[:, t // 2, :, t % 2, :, 0:HD],
                  ps[:, t, H:2 * H].rearrange("p (g j r) -> p g j r", g=8, r=HD), ACT.Copy).then_inc(v_copied, 1)
            act.wait_ge(rope_tab, 1)
            A(ang, ang2, ACT.Sin).then_inc(sin_done, 1)

            def cast_stack(st, k):
                act.wait_ge(roped, k + 1)
                for t in range(NT):
                    dst = st.rearrange("p (b g) t (j r) -> p b g t j r", b=B, r=HS)[:, t // 2, :, t % 2]
                    src = rope_a[:, t * H:(t + 1) * H].rearrange("p (g j r) -> p g j r", g=8, r=HD)
                    second = 8 if k == 0 else 16
                    A(dst[:, :, :, 0:8], src, ACT.Copy).then_inc(cast_hi, 1)
                    A(dst[:, :, :, second:second + 8], src, ACT.Copy).then_inc(cast_hi, 1)

            cast_stack(kst, 0)
            deviation()
            copy_normed(xnt3, 0, 2)
            cast_stack(qst, 1)

            def copy_q2(n, b):
                act.wait_ge(t2_mm, n + 1)
                need(act, s_mm, HPU * (n - 1))
                A(q2t[b], ps[:, 6, 0:2 * P], ACT.Copy).then_inc(t2_copied, 1)

            def exps(n, b):
                need(act, pv_mm, n - 1)
                for j in range(HPU):
                    act.wait_ge(s_mm, HPU * n + (j + 1))
                    A(pexp[b][:, 2 * j * L:2 * (j + 1) * L], ps[:, 4 + j % 2, :], ACT.Exp,
                      scale=float(1.0 / np.sqrt(HD))).then_inc(exp_done, 1)

            def copy_qk(n, b):
                act.wait_ge(t1_mm, n + 1)
                need(act, s_mm, HPU * (n - 1))
                A(qkt[b], ps[:, 6, :], ACT.Copy).then_inc(t1_copied, 1)

            def copy_o(n, b):
                act.wait_ge(pv_mm, n + 1)
                need(act, ot_mm, n - 1)
                A(ost[b], ps[:, 7, 0:L], ACT.Copy).then_inc(o_copied, 1)

            skewed(act, UNITS, [(2, copy_q2), (2, exps), (0, copy_qk), (3, copy_o)])
            for k in range(2):
                act.wait_ge(at_mm, k + 1)
                A(attnt[:, k, :], ps[:, 2 * k:2 * k + 2, :], ACT.Copy).then_inc(at_copied, 1)
            if upto < 4:
                return

            deviation()
            deviation()
            for k in range(2):
                act.wait_ge(hq_mm, k + 1)
                A(hqt[:, k, :], bankb[k], ACT.Copy).then_inc(hq_copied, 1)

            def gelus(t, b):
                act.wait_ge(f1_done, t + 1)
                need(act, fq_done, t - 1)
                A(g1[b], f1[b], ACT.Gelu_apprx_tanh).then_inc(gelu_done, 1)

            def copy_f(t, b):
                act.wait_ge(ft_mm, t + 1)
                need(act, f2_mm, t - 1)
                A(gqt[b].rearrange("p k t -> p (k t)"), bankb[4 + b], ACT.Copy).then_inc(ft_copied, 1)

            skewed(act, NT, [(0, gelus), (1, copy_f)])

        @block.vector
        def _(dve):
            v = nc.vector
            chain = [0]

            def link(ins):
                chain[0] += 1
                ins.then_inc(ln_chain, 1)
                dve.wait_ge(ln_chain, chain[0])

            ln_round = [0]

            def layer_norm(src, dst, before_apply=None):
                ln_round[0] += 1
                k = ln_round[0]
                with dve.Fori(0, NT) as t:
                    v.bn_stats(stats[:, bass.ds(t, 1), :].rearrange("p a s -> p (a s)"),
                               src[:, bass.ds(t, 1), :].rearrange("p a h -> p (a h)")).then_inc(ln_stats, 1)
                dve.wait_ge(ln_stats, NT * k)
                for t in range(NT):
                    v.bn_aggr(mv[:, t, :], stats[:, t, :]).then_inc(ln_mv, 1)
                dve.wait_ge(ln_sd, k)
                link(v.reciprocal(rs[:], sd[:]))
                with dve.Fori(0, NT) as t:
                    v.tensor_scalar(dst[:, bass.ds(t, 1), :].rearrange("p a h -> p (a h)"),
                                    src[:, bass.ds(t, 1), :].rearrange("p a h -> p (a h)"),
                                    mv[:, bass.ds(t, 1), 0:1].rearrange("p a s -> p (a s)"), rs[:, bass.ds(t, 1)],
                                    ALU.subtract, ALU.mult).then_inc(ln_out, 1)

            dve.wait_ge(in_x, 16)
            layer_norm(xa, xn)
            dve.wait_ge(zero_pad, 1)
            for d in range(ND):
                dve.wait_ge(proj_copied, 2 * d + 2)
                acc = conv[:, d, :].rearrange("p (b l) -> p b l", b=B)
                w = [col(MIX, mixp, "conv_w", d * TAPS + k, d * TAPS + k + 1) for k in range(TAPS)]
                link(v.tensor_scalar(acc, xpad[:, d, :, 0:L], w[0], None, ALU.mult))
                for k in range(1, TAPS - 1):
                    link(v.scalar_tensor_tensor(out=acc, in0=xpad[:, d, :, k:k + L], scalar=w[k], in1=acc,
                                                op0=ALU.mult, op1=ALU.add))
                v.scalar_tensor_tensor(out=acc, in0=xpad[:, d, :, TAPS - 1:], scalar=w[TAPS - 1], in1=acc,
                                       op0=ALU.mult, op1=ALU.add).then_inc(conv_done, 1)
            dve.wait_ge(bc_top, 1)
            dve.wait_ge(zero_pad, 2)
            bc = ps[0:64, 4:6, :].rearrange("p a n -> p (a n)")
            link(v.tensor_tensor(rem[0:64, :], bc, bcst[0:64, :], ALU.subtract))
            link(v.tensor_copy(bcst[0:64, :], rem[0:64, :]))
            v.tensor_tensor(bcst[0:32, :], rem[0:32, :], bcst[0:32, :], ALU.subtract).then_inc(bc_split, 1)
            dve.wait_ge(sp_sq, 1)
            link(v.tensor_scalar(sp_rec, sp_exp, 2.0, None, ALU.add))
            link(v.reciprocal(sp_rec, sp_rec))
            v.tensor_tensor(sp_s, sp_exp, sp_rec, ALU.mult).then_inc(dve_step, 1)
            dve.wait_ge(sp_sq, 2)
            dflat = dts.rearrange("p d t -> p (d t)")
            link(v.tensor_scalar(dflat, sp_s2, LOG1P[4], None, ALU.mult))
            for cf in LOG1P[3:0:-1]:
                link(v.scalar_tensor_tensor(out=dflat, in0=dflat, scalar=cf, in1=sp_s2, op0=ALU.add, op1=ALU.mult))
            link(v.scalar_tensor_tensor(out=dflat, in0=dflat, scalar=LOG1P[0], in1=sp_s, op0=ALU.add, op1=ALU.mult))
            link(v.tensor_tensor(dflat, dflat, sp_relu, ALU.add))
            link(v.tensor_tensor(dtu.rearrange("p d t -> p (d t)"), dflat, u.rearrange("p d t -> p (d t)"), ALU.mult))
            v.memset(dts.rearrange("p d (b l) -> p (d b) l", b=B)[:, :, 0:1], 1e25).then_inc(dt_ready, 1)

            def drives(n, b):
                dve.wait_ge(b_mm, n + 1)
                for d in range(ND):
                    if not isinstance(n, int) or n:
                        dve.wait_ge(scan_done, ND * (n - 1) + (d + 1))
                    v.tensor_tensor(drive[d], dtu[:, d, :], ps[:, 0:2, :].rearrange("p a n -> p (a n)"), ALU.mult) \
                        .then_inc(drive_done, 1)

            def scans(n, b):
                for d in range(ND):
                    need(dve, y_mm, ND * (n - 2) + (d + 1) if not isinstance(n, int) or n >= 2 else 0)
                    dve.wait_ge(drive_done, ND * n + (d + 1))
                    dve.wait_ge(decay_done, ND * n + (d + 1))
                    v.tensor_tensor_scan(state[b][d], decay[b][d], drive[d], 0.0, ALU.mult, ALU.add) \
                        .then_inc(scan_done, 1)

            skewed(dve, NST, [(0, drives), (0, scans)])
            dve.wait_ge(y_mm, ND * NST)
            dve.wait_ge(gate_done, 1)
            for d in range(ND):
                y = ps[:, 4 + 2 * d:6 + 2 * d, :].rearrange("p a n -> p (a n)")
                link(v.scalar_tensor_tensor(out=drive[d], in0=u[:, d, :], scalar=col(MIX, mixp, "skip", d, d + 1),
                                            in1=y, op0=ALU.mult, op1=ALU.add))
                yb = drive[d].rearrange("p (b l) -> p b l", b=B)
                v.tensor_tensor(yb, yb, xn[:].rearrange("p (b e) l -> p b e l", e=ND)[:, :, d, :], ALU.mult) \
                    .then_inc(gated, 1)
            for b in range(B):
                dve.wait_ge(yt_mm, b + 1)
                v.tensor_tensor(xa[:, 2 * b:2 * b + 2, :].rearrange("p a h -> p (a h)"),
                                xa[:, 2 * b:2 * b + 2, :].rearrange("p a h -> p (a h)"), ps[:, b, :], ALU.add) \
                    .then_inc(mixed, 1)
            if upto < 2:
                return

            dve.wait_ge(mixed, B)
            layer_norm(xa, xn)
            dve.wait_ge(logit_mm, 1)
            li, sh, key, key2, oh1, oh2, pe_, tmp = rt[:8]

            def v3(a):
                return a.rearrange("p (t e) -> p t e", t=NT)

            def over(a):
                return a.unsqueeze(2).broadcast_to([P, NT, E])

            m_, k2_, ev, den, rec_, _ = small
            link(v.tensor_scalar(li, ps[:, 0, 0:NT * E], 128.0, MAGIC, ALU.mult, ALU.add))
            link(v.tensor_scalar(li, li, -MAGIC, None, ALU.add))
            link(v.tensor_reduce(m_, v3(li), AX.X, ALU.max))
            link(v.tensor_tensor(v3(sh), v3(li), over(m_), ALU.subtract))
            link(v.tensor_scalar(sh, sh, -128.0, None, ALU.max))
            link(v.scalar_tensor_tensor(out=key, in0=sh, scalar=float(E), in1=col(CON, cons, "expert_order"),
                                        op0=ALU.mult, op1=ALU.add))
            link(v.tensor_reduce(m_, v3(key), AX.X, ALU.max))
            link(v.tensor_tensor(v3(oh1), v3(key), over(m_), ALU.is_equal))
            link(v.scalar_tensor_tensor(out=key2, in0=oh1, scalar=-4096.0, in1=key, op0=ALU.mult, op1=ALU.add))
            link(v.tensor_reduce(m_, v3(key2), AX.X, ALU.max))
            link(v.tensor_tensor(v3(oh2), v3(key2), over(m_), ALU.is_equal))
            v.tensor_tensor(mask16, oh1, oh2, ALU.add).then_inc(picked, 1)
            link(v.tensor_tensor(tmp, oh2, sh, ALU.mult))
            link(v.tensor_reduce(k2_, v3(tmp), AX.X, ALU.add))
            lt = rt_lut.rearrange("p (t n) -> p t n", t=NT)
            link(v.tensor_tensor(lt, col(CON, cons, "lut_key").unsqueeze(1).broadcast_to([P, NT, LUTN]),
                                 k2_.unsqueeze(2).broadcast_to([P, NT, LUTN]), ALU.is_equal))
            link(v.tensor_tensor(lt, lt, col(CON, cons, "lut").unsqueeze(1).broadcast_to([P, NT, LUTN]), ALU.mult))
            link(v.tensor_reduce(ev, lt, AX.X, ALU.add))
            link(v.tensor_scalar(den, ev, 65536.0, None, ALU.add))
            link(v.reciprocal(rec_, den))
            link(v.tensor_scalar(gate_w[:, 0, :], rec_, 65536.0, None, ALU.mult))
            link(v.tensor_tensor(gate_w[:, 1, :], rec_, ev, ALU.mult))
            dve.wait_ge(rank_mm, 1)
            tiles, upto_, before = cum[:, 0:E], cum[:, E:2 * E], cum[:, 2 * E:3 * E]
            link(v.tensor_scalar(tiles, ps[:, 2, 0:E], 1.0 / P, (P - 1.0) / P - 0.5 + 0.5 / P, ALU.mult, ALU.add))
            link(v.tensor_scalar(tiles, tiles, MAGIC, -MAGIC, ALU.add, ALU.add))
            link(v.tensor_tensor_scan(upto_, col(CON, cons, "ones"), tiles, 0.0, ALU.mult, ALU.add))
            link(v.tensor_tensor(before, upto_, tiles, ALU.subtract))
            link(v.scalar_tensor_tensor(out=v3(pe_), in0=before.unsqueeze(1).broadcast_to([P, NT, E]),
                                        scalar=float(P), in1=v3(ps[:, 1, 0:NT * E]), op0=ALU.mult, op1=ALU.add))
            for s, oh in enumerate((oh1, oh2)):
                link(v.tensor_tensor(tmp, oh, pe_, ALU.mult))
                link(v.tensor_reduce(m_, v3(tmp), AX.X, ALU.add))
                link(v.tensor_copy(slots_i[:, s, :], m_))
            tx = texp.rearrange("p (i e) -> p i e", e=E)
            link(v.tensor_tensor(tx, col(CON, cons, "tile_index").unsqueeze(2).broadcast_to([P, SLOT_TILES + 1, E]),
                                 upto_.unsqueeze(1).broadcast_to([P, SLOT_TILES + 1, E]), ALU.is_ge))
            te = rt_lut[:, 0:SLOT_TILES + 1]
            link(v.tensor_reduce(te, tx, AX.X, ALU.add))
            v.tensor_scalar(tile_expert[:], te, float(E - 1), None, ALU.min).then_inc(slots_ready, 1)

            def mx_scales(scr, amax_in):
                am, e2, inv, sc = scr
                link(v.tensor_reduce(am, amax_in, AX.X, ALU.max, apply_absolute_value=True))
                link(v.tensor_scalar(am, am, 2.0 ** -100, None, ALU.max))
                link(v.tensor_scalar(e2.bitcast(I32), am.bitcast(I32), 0x7F800000, None, ALU.bitwise_and))
                link(v.tensor_scalar(inv.bitcast(I32), e2.bitcast(I32), -1.0, float(0x7F000000 + (6 << 23)),
                                     ALU.mult, ALU.add))
                link(v.tensor_scalar(sc, e2, 1.0 / 64, None, ALU.mult))

            def mx_quant(dst, src, y, scr, nb):
                def blocks(a):
                    return a.rearrange("p (n k) -> p n k", k=BLK)

                mx_scales(scr, blocks(src))
                _, _, inv, sc = scr
                link(v.tensor_tensor(blocks(y), blocks(src), inv.unsqueeze(2).broadcast_to([P, nb, BLK]), ALU.mult))
                link(v.tensor_scalar(y, y, MAGIC, -MAGIC, ALU.add, ALU.add))
                return v.scalar_tensor_tensor(out=blocks(dst), in0=blocks(y), scalar=127.0,
                                              in1=sc.unsqueeze(2).broadcast_to([P, nb, BLK]), op0=ALU.min,
                                              op1=ALU.mult)

            for m in range(QN):
                dve.wait_ge(in_ffnw, 16 * (m + 1) if m else 32)
                if m:
                    dve.wait_ge(wt_mm, 2 * m)
                mx_quant(fwq, fw_raw[m], fw_y, fw_scr, 64).then_inc(wquant, 1)

            dve.wait_ge(logit_mm, 1)

            def gate_h(i, b):
                dve.wait_ge(up_mm, 2 * i + 2)
                dve.wait_ge(silu_done, i + 1)
                need(dve, ht_mm, 2 * i - 2)
                v.tensor_tensor(hbuf[b].rearrange("p (h n) -> p h n", h=2),
                                silu_h[b].rearrange("p (h n) -> p h n", h=2), ps[:, 2:4, 0:IC], ALU.mult) \
                    .then_inc(h_done, 1)

            def copy_down(i, b):
                dve.wait_ge(down_mm, i + 1)
                need(dve, row_out[b], (i // 2) * 16 if isinstance(i, int) else (i - b) * 8)
                v.tensor_copy(yrow[b], ps[:, 7, 0:H]).then_inc(down_copied, 1)

            skewed(dve, SLOT_TILES, [(1, gate_h), (2, copy_down)])
            for t in range(NT):
                dve.wait_ge(gathered[t % 4], 32 * (t // 4 + 1))
                link(v.scalar_tensor_tensor(out=xa[:, t, :], in0=gat[t % 4][0], scalar=gate_w[:, 0, t:t + 1],
                                            in1=xa[:, t, :], op0=ALU.mult, op1=ALU.add))
                v.scalar_tensor_tensor(out=xa[:, t, :], in0=gat[t % 4][1], scalar=gate_w[:, 1, t:t + 1],
                                       in1=xa[:, t, :], op0=ALU.mult, op1=ALU.add).then_inc(combined, 1)
            if upto < 3:
                return
            dve.wait_ge(combined, NT)

            dve.wait_ge(in_late, 16)
            link(v.tensor_tensor(ang[:, 0:64], col(ROUTE, routep, "pos"), col(CON, cons, "freq"), ALU.mult))
            link(v.tensor_scalar(ang[:, 64:128], ang[:, 0:64], float(np.pi / 2), None, ALU.add))
            link(v.tensor_scalar(ang2, ang, float(1 / (2 * np.pi)), MAGIC, ALU.mult, ALU.add))
            link(v.tensor_scalar(ang2, ang2, -MAGIC, None, ALU.add))
            link(v.scalar_tensor_tensor(out=ang2, in0=ang2, scalar=float(-2 * np.pi), in1=ang, op0=ALU.mult,
                                        op1=ALU.add))
            v.tensor_scalar(ang2, ang2, 3.1415925, -3.1415925, ALU.min, ALU.max).then_inc(rope_tab, 1)
            dve.wait_ge(sin_done, 1)
            link(v.tensor_tensor(sin8, ang[:, 0:64], col(CON, cons, "rope_sign"), ALU.mult))

            def rope(banks_of, k):
                for t in range(NT):
                    src = banks_of(t).rearrange("p (h r) -> p h r", r=HD)
                    a = rope_a[:, t * H:(t + 1) * H].rearrange("p (h r) -> p h r", r=HD)
                    b = rope_b[:, t * H:(t + 1) * H].rearrange("p (h r) -> p h r", r=HD)
                    cs = ang[:, 64 + t * 8:72 + t * 8].unsqueeze(1).broadcast_to([P, NHEAD, HD])
                    sn = sin8[:, t * 8:t * 8 + 8].unsqueeze(1).broadcast_to([P, NHEAD, HD])
                    v.tensor_tensor(a, src, cs, ALU.mult)
                    v.tensor_tensor(b[:, :, 0::2], src[:, :, 1::2], sn[:, :, 0::2], ALU.mult)
                    link(v.tensor_tensor(b[:, :, 1::2], src[:, :, 0::2], sn[:, :, 1::2], ALU.mult))
                    last = v.tensor_tensor(a, a, b, ALU.add)
                last.then_inc(roped, 1)

            def low_halves(st, k):
                for t in range(NT):
                    dst = st.rearrange("p (b g) t (j r) -> p b g t j r", b=B, r=HS)[:, t // 2, :, t % 2]
                    src = rope_a[:, t * H:(t + 1) * H].rearrange("p (g j r) -> p g j r", g=8, r=HD)
                    dve.wait_ge(cast_hi, 2 * NT * k + 2 * t + 2)
                    low = 16 if k == 0 else 8
                    last = v.tensor_tensor(dst[:, :, :, low:low + 8], src, dst[:, :, :, 0:8], ALU.subtract)
                last.then_inc(stacked, 1)

            dve.wait_ge(kv_mm, NT)
            dve.wait_ge(v_copied, NT)
            rope(lambda t: ps[:, t, 0:H], 0)
            dve.wait_ge(roped, 1)
            low_halves(kst, 0)
            layer_norm(xa, xn)
            dve.wait_ge(q_mm, 1)
            dve.wait_ge(stacked, 1)
            rope(lambda t: ps[:, 4 + t // 2, (t % 2) * H:(t % 2 + 1) * H], 1)
            dve.wait_ge(roped, 2)
            low_halves(qst, 1)

            def norm_o(n, b):
                dve.wait_ge(ot_mm, n + 1)
                need(dve, o_norm, n)
                o = ps[:, 7, L:2 * L].rearrange("p (t j r) -> p t j r", t=2, r=HS)
                r = orec.rearrange("p (t j) -> p t j", t=2)
                v.reciprocal(r, o[:, :, :, HD]).then_inc(o_rec, 1)
                dve.wait_ge(o_rec, n + 1)
                v.tensor_tensor(attn[:, :, bass.ds(n, 1), :].rearrange("p t a (j r) -> p (t a) j r", r=HD), o[:, :, :, 0:HD],
                                r.unsqueeze(3).broadcast_to([P, 2, HPU, HD]), ALU.mult).then_inc(o_norm, 1)

            def maxima(n, b):
                for half in range(2):
                    dve.wait_ge(mx_mm, 2 * n + (half + 1))
                    v.tensor_reduce(mx[b][:, half * 4:half * 4 + 4],
                                    ps[:, 2 * half:2 * half + 2, :].rearrange("p j (t k) -> p (j t) k", t=2),
                                    AX.X, ALU.max).then_inc(mx_done, 1)

            def shift(n, b):
                dve.wait_ge(mx_done, 2 * n + 2)
                m3 = mx[b].rearrange("p (j t) -> p t j", t=2)
                dst = qst[:, bass.ds(n, 1)].rearrange("p a t (j r) -> p (a t) j r", r=HS)
                v.tensor_scalar(dst[:, :, :, 24], m3, -1.0, None, ALU.mult).then_inc(shift_hi, 1)
                dve.wait_ge(shift_hi, n + 1)
                v.scalar_tensor_tensor(out=dst[:, :, :, 25], in0=m3, scalar=-1.0, in1=dst[:, :, :, 24],
                                       op0=ALU.mult, op1=ALU.subtract).then_inc(shift_done, 1)

            skewed(dve, UNITS, [(4, norm_o), (1, maxima), (1, shift)])
            dve.wait_ge(wo_mm, 1)
            for t in range(NT):
                link(v.tensor_tensor(xa[:, t, :], xa[:, t, :], ps[:, 4 + t // 2, (t % 2) * H:(t % 2 + 1) * H],
                                     ALU.add))
                v.tensor_tensor(xa[:, t, :], xa[:, t, :], col(LATE, late_s, "bout"), ALU.add).then_inc(attn_done, 1)
            if upto < 4:
                return

            dve.wait_ge(attn_done, NT)
            layer_norm(xa, xb)
            dve.wait_ge(ln_out, 4 * NT)
            hn3 = hn.rearrange("p (t h) -> p t h", t=NT)
            layer_norm(xb, hn3)
            dve.wait_ge(ln_out, 5 * NT)
            link(v.tensor_tensor(hn3, hn3, col(LATE, late_s, "ln_w").unsqueeze(1).broadcast_to([P, NT, H]), ALU.mult))
            link(v.tensor_tensor(hb.rearrange("p (t h) -> p t h", t=NT), hn3,
                                 col(LATE, late_s, "ln_b").unsqueeze(1).broadcast_to([P, NT, H]), ALU.add))
            mx_quant(hqb, hb, hn, qs, NT * H // BLK).then_inc(hq_ready, 1)

            def add_b1(t, b):
                dve.wait_ge(f1_mm, t + 1)
                need(dve, gelu_done, t - 1)
                v.tensor_tensor(f1[b], ps[:, 2 * b:2 * b + 2, :].rearrange("p a n -> p (a n)"),
                                col(LATE, late_s, "b1"), ALU.add).then_inc(f1_done, 1)

            def quant_f(t, b):
                am, e2, inv, sc = fs[b]
                base = t * 7

                def linked(ins, k):
                    ins.then_inc(fq_chain, 1)
                    dve.wait_ge(fq_chain, base + k)

                def blocks(a):
                    return a.rearrange("p (n k) -> p n k", k=BLK)

                def wide(a):
                    return a.unsqueeze(2).broadcast_to([P, F // BLK, BLK])

                dve.wait_ge(gelu_done, t + 1)
                need(dve, ft_mm, t - 1)
                linked(v.tensor_reduce(am, blocks(g1[b]), AX.X, ALU.max, apply_absolute_value=True), 1)
                linked(v.tensor_scalar(am, am, 2.0 ** -100, None, ALU.max), 2)
                linked(v.tensor_scalar(e2.bitcast(I32), am.bitcast(I32), 0x7F800000, None, ALU.bitwise_and), 3)
                linked(v.tensor_scalar(inv.bitcast(I32), e2.bitcast(I32), -1.0, float(0x7F000000 + (6 << 23)),
                                       ALU.mult, ALU.add), 4)
                linked(v.tensor_scalar(sc, e2, 1.0 / 64, None, ALU.mult), 5)
                linked(v.tensor_tensor(blocks(gy[b]), blocks(g1[b]), wide(inv), ALU.mult), 6)
                linked(v.tensor_scalar(gy[b], gy[b], MAGIC, -MAGIC, ALU.add, ALU.add), 7)
                v.scalar_tensor_tensor(out=blocks(gq[b]), in0=blocks(gy[b]), scalar=127.0, in1=wide(sc),
                                       op0=ALU.min, op1=ALU.mult).then_inc(fq_done, 1)

            def finish(t, b):
                dve.wait_ge(f2_mm, t + 1)

                def linked(ins, k):
                    ins.then_inc(f2_chain, 1)
                    dve.wait_ge(f2_chain, t * 2 + k)

                def tile(a):
                    return a[:, bass.ds(t, 1), :].rearrange("p a h -> p (a h)")

                linked(v.tensor_tensor(f2[b], ps[:, 6 + b, 0:H], col(LATE, late_s, "b2"), ALU.add), 1)
                linked(v.tensor_tensor(r4[b], f2[b], tile(xb), ALU.add), 2)
                v.tensor_tensor(tile(xa), tile(xa), r4[b], ALU.add).then_inc(f2_done, 1)

            skewed(dve, NT, [(0, add_b1), (1, quant_f), (2, finish)])




def kernel(x, ctx_1024, fside_BxSx2_0, L0_xattn_in_proj_w, L0_xattn_conv_w, L0_xattn_conv_b, L0_xattn_x_proj_w,
           L0_xattn_dt_proj_w, L0_xattn_dt_proj_b, L0_xattn_A_log, L0_xattn_D, L0_ffn_w_gate, L0_ffn_w1, L0_ffn_w2,
           L0_ffn_w3, L1_xattn_Wq, L1_xattn_Wkv, L1_xattn_Wout, L1_xattn_bout, L1_ffn_ln_w, L1_ffn_ln_b, L1_ffn_W1,
           L1_ffn_b1, L1_ffn_W2, L1_ffn_b2):
    import ml_dtypes
    import concourse.bacc as bacc
    from concourse.bass_utils import run_bass_kernel_spmd

    def rows(a, n):
        a = np.asarray(a)
        return a.reshape(n, P, -1).transpose(1, 0, 2).reshape(P, -1)

    def every(a):
        return np.broadcast_to(np.asarray(a).reshape(1, -1), (P, np.asarray(a).size))

    xp = np.asarray(L0_xattn_x_proj_w)
    bc = np.concatenate([xp[DTR:]] * 3, axis=0).T
    w13 = np.stack([np.asarray(L0_ffn_w1), np.asarray(L0_ffn_w3)], 1)
    w13 = w13.transpose(0, 1, 3, 2).reshape(E, 2, 2, P, I).transpose(0, 3, 1, 2, 4).reshape(E, P, 4 * I)
    w2 = np.asarray(L0_ffn_w2).transpose(0, 2, 1)
    w2 = np.concatenate([w2, np.zeros((E, KI * P - I, H), w2.dtype)], 1)
    w2 = w2.reshape(E, KI, P, H).transpose(0, 2, 1, 3).reshape(E, P, KI * H)
    pos = np.repeat(np.asarray(fside_BxSx2_0).reshape(T, 2), 4, axis=1)

    eye = np.eye(P, dtype=np.float32)
    key = np.arange(-128, 1)
    lut = np.floor(np.exp(key / 128.0) * 65536)
    freq = np.array([1.0, 1.0, 0.01, 0.01] * 2, np.float32)
    before = np.triu(np.ones((P, P)), 1)
    con = np.concatenate([eye, every(lut), every(key), every(np.tile(np.arange(E)[::-1], NT)),
                          every(np.arange(SLOT_TILES + 1)), np.ones((P, E)), every(np.tile(freq, NT)),
                          every(np.tile([-1.0, 1.0], NT * 4))], axis=1).astype(np.float32)
    con16 = np.concatenate([eye, before, np.ones((P, P))], axis=1).astype(np.float16)
    k = np.arange(P)[:, None, None]
    j = np.arange(32)[None, :, None]
    select = np.broadcast_to((k % 32 == j) & (k < 96), (P, 32, P)).reshape(P, 32 * P)

    given = {
        "x": np.asarray(x).reshape(T, H),
        "ctx_t": np.asarray(ctx_1024).reshape(T, CTX).T,
        "mix": np.concatenate([np.asarray(L0_xattn_in_proj_w).T, rows(bc, ND), rows(xp[:DTR].T, ND),
                               rows(np.asarray(L0_xattn_conv_w).reshape(DI, TAPS), ND), rows(L0_xattn_conv_b, ND),
                               rows(L0_xattn_dt_proj_b, ND), rows(L0_xattn_D, ND), rows(L0_xattn_A_log, ND)], 1),
        "dt_proj": np.asarray(L0_xattn_dt_proj_w).T,
        "route": np.concatenate([rows(np.asarray(L0_ffn_w_gate).T, 2), rows(pos, NT)], 1),
        "w13": w13,
        "w2": w2,
        "late": np.concatenate([rows(L1_xattn_Wq, 2), np.asarray(L1_xattn_Wkv), rows(L1_xattn_Wout, 2),
                                every(L1_xattn_bout), every(L1_ffn_ln_w), every(L1_ffn_ln_b), every(L1_ffn_b1),
                                every(L1_ffn_b2)], 1),
        "ffn_w1": rows(L1_ffn_W1, F // P),
        "ffn_w2": rows(L1_ffn_W2, H // P),
        "con": con,
        "con16": con16,
        "bc_select": select.astype(ml_dtypes.bfloat16),
        "ident_b": eye.astype(ml_dtypes.bfloat16),
    }
    nc = bacc.Bacc("TRN2", target_bir_lowering=False, num_devices=1)
    arrays, aps = {}, {}
    for name, a in given.items():
        arrays[f"in_{name}"] = np.ascontiguousarray(a)
        aps[name] = nc.dram_tensor(f"in_{name}", a.shape, mybir.dt.from_np(a.dtype), kind="ExternalInput").ap()
    aps["out"] = nc.dram_tensor("out_x", (T, H), F32, kind="ExternalOutput").ap()
    build(nc, **aps)
    r = run_bass_kernel_spmd(nc, [arrays], core_ids=[0])
    return r.results[0]["out_x"].reshape(B, L, H)
```

```python
from contextlib import ExitStack
from functools import partial

import numpy as np

import concourse.bass as bass
from concourse import mybir

P = 128
B, L, H = 4, 256, 256
T = B * L
NT = T // P
CTX = 128
DI, NST, DTR, TAPS = 256, 16, 8, 4
ND = DI // P
PADL = L + TAPS - 1
E, I = 8, 704
IC = I // 2
KI = (I + P - 1) // P
SLOT_TILES = (2 * T + E * (P - 1)) // P
NHEAD, HD = 32, 8
HPU = 4
UNITS = B * NHEAD // HPU
HS = 32
F = 4 * H
BLK = 32
LUTN = 129
EPS = 1e-5
MAGIC = 12582912.0

F32, BF16, F16 = mybir.dt.float32, mybir.dt.bfloat16, mybir.dt.float16
I32, U32 = mybir.dt.int32, mybir.dt.uint32
ALU = mybir.AluOpType
ACT = mybir.ActivationFunctionType
AX = mybir.AxisListType

LOG1P = (2.00000002, 0.6666624, 0.40026449, 0.27953006, 0.28165458)

def _columns(*sizes):
    at, out = 0, {}
    for name, n in sizes:
        out[name] = (at, at + n)
        at += n
    return out, at


MIX, MIX_N = _columns(("in_proj", DI), ("x_proj_bc", ND * 96), ("x_proj_dt", ND * DTR), ("conv_w", ND * TAPS),
                      ("conv_b", ND), ("dt_b", ND), ("skip", ND), ("a_log", ND * NST))
CON, CON_N = _columns(("ident", P), ("lut", LUTN), ("lut_key", LUTN), ("expert_order", NT * E),
                      ("tile_index", SLOT_TILES + 1), ("ones", E), ("freq", NT * 8), ("rope_sign", NT * 8))
LATE, LATE_N = _columns(("wq", 2 * H), ("wout", 2 * H), ("bout", H), ("ln_w", H), ("ln_b", H),
                        ("b1", F), ("b2", H))
ROUTE, ROUTE_N = _columns(("w_gate", 2 * E), ("pos", NT * 8), ("wkv", 2 * H))


def need(eng, sem, value):
    if not isinstance(value, int) or value > 0:
        eng.wait_ge(sem, value)


def skewed(eng, count, stages, turn=2):
    late = max(s for s, _ in stages)
    first = late + late % 2 + turn
    loops = (count - first) // turn

    def peeled(r):
        for s, stage in stages:
            if 0 <= r - s < count:
                stage(r - s, (r - s) % turn)

    for r in range(first):
        peeled(r)
    with eng.Fori(0, loops) as v:
        for j in range(turn):
            for s, stage in stages:
                stage(v * turn + (first + j - s), (first + j - s) % turn)
    for r in range(first + turn * loops, count + late):
        peeled(r)


def build(nc, x, ctx_t, mix, dt_proj, route, w13, w2, late, ffn_w1, ffn_w2, con, con16, bc_select, ident_b, out,
          upto=4):
    routed = nc.dram_tensor("routed_rows", (SLOT_TILES * P, H), F32, kind="Internal").ap()
    expert_out = nc.dram_tensor("expert_rows", (SLOT_TILES * P, H), F32, kind="Internal").ap()

    with ExitStack() as ctx:
        def sb(name, shape, dt=F32):
            return ctx.enter_context(nc.sbuf_tensor(name, shape, dt))

        def sem(name):
            return ctx.enter_context(nc.semaphore(name))

        ps = ctx.enter_context(nc.psum_tensor("ps", [P, 8, 512], F32))

        xa = sb("resid", [P, NT, H])
        zrow = sb("zeros", [P, H])
        xn = sb("normed", [P, NT, H])
        ctxt = sb("ctx_t", [P, T])
        mixp = sb("mix_params", [P, MIX_N])
        dtp = sb("dt_proj", [P, DI])
        routep = sb("route_params", [P, ROUTE_N])
        cons = sb("constants", [P, CON_N])
        cons16 = sb("constants16", [P, 3 * P], F16)
        identb = sb("ident_b", [P, P], BF16)
        w1q = sb("w1_quant_t", [P, 2, F], BF16)
        w2q = sb("w2_quant_t", [P, F // P, H], BF16)
        stats = sb("stats", [P, NT, 6])
        mv = sb("mean_var", [P, NT, 2])
        sd = sb("deviation", [P, NT])
        rs = sb("inv_deviation", [P, NT])
        gate_w = sb("gate_weights", [P, 2, NT])
        slots_i = sb("slots", [P, 2, NT], I32)
        tile_expert = sb("tile_expert", [P, SLOT_TILES + 1], I32)
        ang = sb("angles", [P, 2 * NT * 8])
        ang2 = sb("angles_reduced", [P, 2 * NT * 8])
        sin8 = sb("signed_sin", [P, NT * 8])
        rope_s = sb("rope_scratch", [P, H])
        W13E = 2 * 2 * I
        W2E = KI * H
        weights = sb("weights", [P, E * (W13E + W2E)])
        work = sb("work", [P, 8000])

        w13s = weights[:, 0:E * W13E].rearrange("p (e m k n) -> p e m k n", e=E, m=2, k=2)
        w2s = weights[:, E * W13E:].rearrange("p (e j n) -> p e j n", e=E, j=KI)

        class Carve:
            def __init__(self, base, at=0):
                self.base, self.at = base, at

            def __call__(self, n, dt=F32):
                words = n if dt in (F32, I32, U32) else (n + 1) // 2
                got = self.base[:, self.at:self.at + words]
                self.at += words
                assert self.at <= self.base.shape[1], (self.at, self.base.shape)
                return got if dt == F32 else got.bitcast(dt)

        def col(table, tensor, name, a=0, b=None):
            lo, hi = table[name]
            return tensor[:, lo + a:(hi if b is None else lo + b)]

        ident = col(CON, cons, "ident")
        ident16, before16, ones16 = (cons16[:, i * P:(i + 1) * P] for i in range(3))

        EARLY = 5
        c = Carve(weights, EARLY * W13E)
        sel = c(32 * P, BF16)
        bcst = c(T, BF16)
        u = c(ND * T).rearrange("p (d t) -> p d t", d=ND)
        dts = c(ND * T).rearrange("p (d t) -> p d t", d=ND)
        dtu = c(ND * T).rearrange("p (d t) -> p d t", d=ND)
        decay = [[c(T) for _ in range(ND)] for _ in range(2)]
        state = [[c(T) for _ in range(ND)] for _ in range(2)]
        drive = [c(T) for _ in range(ND)]
        acoef = c(ND * NST)
        c = Carve(work)
        crow = [c(T) for _ in range(2)]
        dtl = c(T)
        c2 = Carve(weights, EARLY * W13E + 16 * P)
        c2.at = EARLY * W13E + 16 * P + T // 2 + 3 * ND * T
        xpad = c2(ND * B * PADL).rearrange("p (d b l) -> p d b l", d=ND, b=B)
        conv = c2(ND * T).rearrange("p (d t) -> p d t", d=ND)
        c3 = Carve(weights, EARLY * W13E + 16 * P + T // 2 + 3 * ND * T)
        sp_abs, sp_exp, sp_rec = (c3(ND * T) for _ in range(3))
        sp_relu = c3(ND * T)
        c3b = Carve(work, 3 * T)
        rem = c3b(T)
        sp_s, sp_s2 = sp_rec, sp_abs

        in_x, in_mix, in_misc, in_con, in_late, in_ffnw, out_done, zeroed = map(
            sem, ("in_x", "in_mix", "in_misc", "in_con", "in_late", "in_ffnw", "out_done", "zeroed"))
        in_w = sem("in_w")
        ln_stats, ln_mv, ln_sd, ln_out, ln_chain = map(sem, ("ln_stats", "ln_mv", "ln_sd", "ln_out", "ln_chain"))
        dve_step, act_step = sem("dve_step"), sem("act_step")
        zero_pad, proj_mm, proj_copied, conv_done, u_done = map(
            sem, ("zero_pad", "proj_mm", "proj_copied", "conv_done", "u_done"))
        xproj_mm, bc_top, dtl_copied, dt_mm, sp_parts, sp_sq, bc_split, dt_ready, a_ready = map(
            sem, ("xproj_mm", "bc_top", "dtl_copied", "dt_mm", "sp_parts", "sp_sq", "bc_split", "dt_ready", "a_ready"))
        b_mm, c_mm, c_copied, decay_done, drive_done, scan_done, prod_done, y_mm = map(
            sem, ("b_mm", "c_mm", "c_copied", "decay_done", "drive_done", "scan_done", "prod_done", "y_mm"))
        gate_done, gated, yt_mm, mixed = map(sem, ("gate_done", "gated", "yt_mm", "mixed"))
        xnt_mm, xnt_copied, logit_mm, picked, rank_mm, slots_ready, scattered = map(
            sem, ("xnt_mm", "xnt_copied", "logit_mm", "picked", "rank_mm", "slots_ready", "scattered"))
        wt_mm, wt_copied, wquant = map(sem, ("wt_mm", "wt_copied", "wquant"))
        row_in = [sem(f"row_in{i}") for i in range(2)]
        row_out = [sem(f"row_out{i}") for i in range(2)]
        row_mm, rowt_copied, up_mm, silu_done, h_done, ht_mm, ht_copied, down_mm, down_copied = map(
            sem, ("row_mm", "rowt_copied", "up_mm", "silu_done", "h_done", "ht_mm", "ht_copied", "down_mm",
                  "down_copied"))
        gathered = [sem(f"gathered{i}") for i in range(4)]
        combined = sem("combined")
        stack_zero, kv_mm, v_copied, roped, cast_hi, stacked, q_mm, rope_tab, sin_done = map(
            sem, ("stack_zero", "kv_mm", "v_copied", "roped", "cast_hi", "stacked", "q_mm", "rope_tab", "sin_done"))
        k_mm, v_mm, k_saved, v_saved, k_roped, rope_step, sin_signed, stack_ones = map(
            sem, ("k_mm", "v_mm", "k_saved", "v_saved", "k_roped", "rope_step", "sin_signed", "stack_ones"))
        masked = sem("masked")
        t1_mm, t1_copied, mx_mm, mx_done, shift_done, t2_mm, t2_copied, s_mm, exp_done, v_unit = map(
            sem, ("t1_mm", "t1_copied", "mx_mm", "mx_done", "shift_done", "t2_mm", "t2_copied", "s_mm", "exp_done",
                  "v_unit"))
        pv_mm, o_copied, ot_mm, o_norm, at_mm, at_copied, wo_mm, attn_done = map(
            sem, ("pv_mm", "o_copied", "ot_mm", "o_norm", "at_mm", "at_copied", "wo_mm", "attn_done"))
        o_rec, shift_hi, fq_chain, f2_chain, hq_ready = map(
            sem, ("o_rec", "shift_hi", "fq_chain", "f2_chain", "hq_ready"))
        hq_mm, hq_copied, f1_mm, f1_done, gelu_done, fq_done, ft_mm, ft_copied, f2_mm, f2_done = map(
            sem, ("hq_mm", "hq_copied", "f1_mm", "f1_done", "gelu_done", "fq_done", "ft_mm", "ft_copied", "f2_mm",
                  "f2_done"))

        c = Carve(work)
        rt = [c(NT * E) for _ in range(12)]
        rt_lut = c(NT * LUTN)
        mask16 = c(NT * E, F16)
        small = [c(NT) for _ in range(6)]
        cum = c(4 * E)
        texp = c((SLOT_TILES + 1) * E)
        xnt_at = c.at
        xnt = c(2 * T).rearrange("p (k t) -> p k t", k=2)
        fwq = c(2 * T, BF16)
        fw_y = c(2 * T)
        fw_scr = [c(64) for _ in range(4)]
        c = Carve(work, xnt_at)
        xg = [c(H) for _ in range(2)]
        xgt = [c(2 * P) for _ in range(2)]
        silu_h = [c(I) for _ in range(2)]
        hbuf = [c(I) for _ in range(2)]
        vraw = c(NT * H).rearrange("p (t h) -> p t h", t=NT)
        c = Carve(work)
        ht = [c(KI * P).rearrange("p (j s) -> p j s", j=KI) for _ in range(2)]
        yrow = [c(H) for _ in range(2)]
        assert c.at <= xnt_at
        fw_raw = [weights[:, (EARLY + m) * W13E:(EARLY + m) * W13E + 2048] for m in range(2)]

        c = Carve(weights)
        gat = [[c(H) for _ in range(2)] for _ in range(4)]
        late_s = c(LATE_N)
        late_end = c.at
        qst = c(UNITS * 2 * P, F16).rearrange("p (u t r) -> p u t r", u=UNITS, t=2)
        kst = c(UNITS * 2 * P, F16).rearrange("p (u t r) -> p u t r", u=UNITS, t=2)
        vst = c(UNITS * 2 * P).rearrange("p (u t r) -> p u t r", u=UNITS, t=2)
        rope_b = c(NT * H)
        orec = [c(UNITS // B * 2 * HPU) for _ in range(2)]
        rope_at = c.at
        rope_a = c(NT * H)
        xnt3 = c(2 * T).rearrange("p (k t) -> p k t", k=2)
        c = Carve(weights, rope_at)
        ost = c(UNITS * L).rearrange("p (u q) -> p u q", u=UNITS)
        c = Carve(work)
        qkt = [c(4 * P, F16) for _ in range(4)]
        q2t = [c(2 * P, F16) for _ in range(2)]
        kmask = [c(HPU * L, F16).rearrange("p (j k) -> p j k", j=HPU) for _ in range(4)]
        pexp = [c(HPU * 2 * L) for _ in range(2)]
        vu = [c(2 * P).rearrange("p (t r) -> p t r", t=2) for _ in range(2)]
        mx = [c(2 * HPU) for _ in range(2)]
        attn = rope_b.rearrange("p (t u r) -> p t u r", t=2, u=UNITS)
        attnt = xnt3
        c = Carve(weights, late_end)
        xb = c(NT * H, BF16).rearrange("p (t h) -> p t h", t=NT)
        hn = c(NT * H)
        hb = c(NT * H, BF16)
        hqb = c(NT * H, BF16)
        hqt = c(2 * T, BF16).rearrange("p (k t) -> p k t", k=2)
        qs = [c(NT * H // BLK) for _ in range(4)]
        f1 = [c(F, BF16) for _ in range(2)]
        g1 = [c(F, BF16) for _ in range(2)]
        gy = [c(F, BF16) for _ in range(2)]
        gq = [c(F, BF16) for _ in range(2)]
        gqt = [c(F, BF16).rearrange("p (k t) -> p k t", k=F // P) for _ in range(2)]
        fs = [[c(F // BLK) for _ in range(4)] for _ in range(2)]
        f2 = [c(H, BF16) for _ in range(2)]
        r4 = [c(H, BF16) for _ in range(2)]

        bank16 = [ps[:, b, :].bitcast(F16) for b in range(8)]
        bankb = [ps[:, b, :].bitcast(BF16) for b in range(8)]
        block = ctx.enter_context(nc.Block())
        QN = 2

        @block.sync
        def _(sp):
            sp.dma_start(ctxt[:], ctx_t).then_inc(in_mix, 16)
            sp.dma_start(mixp[:], mix).then_inc(in_mix, 16)
            sp.dma_start(dtp[0:DTR, :], dt_proj).then_inc(in_mix, 16)
            sp.dma_start(xa[:], x.rearrange("(t p) h -> p t h", p=P)).then_inc(in_x, 16)
            sp.dma_start(sel, bc_select).then_inc(in_misc, 16)
            sp.dma_start(cons[:], con).then_inc(in_con, 16)
            sp.dma_start(cons16[:], con16).then_inc(in_con, 16)
            sp.dma_start(identb[:], ident_b).then_inc(in_con, 16)
            sp.dma_start(routep[:], route).then_inc(in_con, 16)
            if upto >= 2:
                for e in range(EARLY):
                    sp.dma_start(w13s[:, e].rearrange("p m k n -> p (m k n)"), w13[e]).then_inc(in_w, 16)
                sp.wait_ge(zero_pad, 3)
                sp.dma_start(routed.rearrange("(i p) h -> p i h", p=P),
                             zrow[:].unsqueeze(1).broadcast_to([P, SLOT_TILES, H])).then_inc(zeroed, 16)
                sp.wait_ge(mixed, B)
                for m, src in enumerate((ffn_w1, ffn_w2)):
                    sp.dma_start(fw_raw[m], src).then_inc(in_ffnw, 16)
                for e in range(E):
                    sp.dma_start(w2s[:, e].rearrange("p j n -> p (j n)"), w2[e]).then_inc(in_w, 16)
                for e in range(EARLY + 2, E):
                    sp.dma_start(w13s[:, e].rearrange("p m k n -> p (m k n)"), w13[e]).then_inc(in_w, 16)
                sp.wait_ge(wquant, QN)
                for e in range(EARLY, EARLY + 2):
                    sp.dma_start(w13s[:, e].rearrange("p m k n -> p (m k n)"), w13[e]).then_inc(in_w, 16)

                sp.wait_ge(scattered, 32 * NT)

                def load_rows(i, b):
                    need(sp, row_mm, i - 1)
                    sp.dma_start(xg[b], routed[bass.ds(i * P, P), :]).then_inc(row_in[b], 16)

                def store_rows(i, b):
                    sp.wait_ge(down_copied, i + 1)
                    sp.dma_start(expert_out[bass.ds(i * P, P), :], yrow[b]).then_inc(row_out[b], 16)

                skewed(sp, SLOT_TILES, [(0, load_rows), (3, store_rows)])
            if upto >= 3:
                sp.wait_ge(down_mm, SLOT_TILES)
                sp.dma_start(late_s, late).then_inc(in_late, 16)
            if upto < 4:
                sp.wait_ge([None, mixed, combined, attn_done][upto], [None, B, NT, NT][upto])
                sp.dma_start(out.rearrange("(t p) h -> p t h", p=P), xa[:]).then_inc(out_done, 16)
                sp.wait_ge(out_done, 16)
            else:
                with sp.Fori(0, NT) as t:
                    sp.wait_ge(f2_done, t + 1)
                    sp.dma_start(out[bass.ds(t * P, P), :], xa[:, bass.ds(t, 1), :].rearrange("p a h -> p (a h)")) \
                      .then_inc(out_done, 16)
                sp.wait_ge(out_done, 16 * NT)

        @block.gpsimd
        def _(pool):
            nc.gpsimd.memset(xpad[:, :, :, 0:TAPS - 1], 0.0).then_inc(zero_pad, 1)
            nc.gpsimd.memset(bcst, 0.0).then_inc(zero_pad, 1)
            nc.gpsimd.memset(zrow[:], 0.0).then_inc(zero_pad, 1)

            def times_c(n, b):
                pool.wait_ge(c_copied, n + 1)
                for d in range(ND):
                    pool.wait_ge(scan_done, n * ND + (d + 1))
                    nc.gpsimd.tensor_tensor(state[b][d], state[b][d], crow[b], ALU.mult).then_inc(prod_done, 1)

            skewed(pool, NST, [(0, times_c)])
            if upto < 2:
                return
            pool.wait_ge(zeroed, 16)
            pool.wait_ge(slots_ready, 1)
            pool.wait_ge(ln_out, 2 * NT)
            for t in range(NT):
                for s in range(2):
                    pool.indirect_dma_start(
                        routed, bass.IndirectOffsetOnAxis(ap=slots_i[:, s, t:t + 1].bitcast(U32), axis=0),
                        xn[:, t, :], None).then_inc(scattered, 16)
            steps = [0]

            def rope_link(ins):
                steps[0] += 1
                ins.then_inc(rope_step, 1)
                pool.wait_ge(rope_step, steps[0])

            pool.wait_ge(k_saved, 2)
            pool.wait_ge(sin_signed, 1)
            for t in range(NT):
                k = xn[:, t, :].rearrange("p (h r) -> p h r", r=HD)
                a = rope_s[:].rearrange("p (h r) -> p h r", r=HD)
                b = zrow[:].rearrange("p (h r) -> p h r", r=HD)
                cs = ang[:, 64 + t * 8:72 + t * 8].unsqueeze(1).broadcast_to([P, NHEAD, HD])
                sn = sin8[:, t * 8:t * 8 + 8].unsqueeze(1).broadcast_to([P, NHEAD, HD])
                rope_link(nc.gpsimd.tensor_tensor(a, k, cs, ALU.mult))
                rope_link(nc.gpsimd.tensor_tensor(b[:, :, 0::2], k[:, :, 1::2], sn[:, :, 0::2], ALU.mult))
                rope_link(nc.gpsimd.tensor_tensor(b[:, :, 1::2], k[:, :, 0::2], sn[:, :, 1::2], ALU.mult))
                ins = nc.gpsimd.tensor_tensor(k, a, b, ALU.add)
                ins.then_inc(k_roped, 1)
                pool.wait_ge(k_roped, t + 1)
            for b in range(2):
                pool.wait_ge(row_out[b], 16 * ((SLOT_TILES + 1 - b) // 2))
            pool.wait_ge(down_mm, SLOT_TILES)
            for t in range(NT):
                need(pool, combined, t - 3)
                for s in range(2):
                    pool.indirect_dma_start(
                        gat[t % 4][s], None, expert_out,
                        bass.IndirectOffsetOnAxis(ap=slots_i[:, s, t:t + 1].bitcast(U32), axis=0),
                        ).then_inc(gathered[t % 4], 16)
            if upto < 3:
                return
            nc.gpsimd.memset(qst.rearrange("p u t r -> p (u t r)").bitcast(U32), 0).then_inc(stack_zero, 1)
            for b in range(4):
                nc.gpsimd.memset(kmask[b].rearrange("p j k -> p (j k)").bitcast(U32), 0).then_inc(stack_zero, 1)
            nc.gpsimd.memset(vst.rearrange("p u t r -> p (u t r)").bitcast(U32), 0).then_inc(stack_zero, 1)
            pool.wait_ge(stack_zero, 6)
            nc.gpsimd.memset(vst.rearrange("p u t (j r) -> p (u t j) r", r=HS)[:, :, 8:9], 1.0) \
              .then_inc(stack_zero, 1)
            pool.wait_ge(v_copied, NT)

            def copy_v(n, b):
                need(pool, pv_mm, n - 1)
                nc.gpsimd.tensor_copy(vu[b % 2], vst[:, bass.ds(n, 1)].rearrange("p a t r -> p (a t) r")) \
                  .then_inc(v_unit, 1)

            skewed(pool, UNITS, [(0, copy_v)])

        @block.tensor
        def _(pe):
            mm = nc.tensor.matmul
            pe.wait_ge(in_mix, 48)
            for d in range(ND):
                for h in range(2):
                    last = mm(ps[:, 2 * d + h, :], col(MIX, mixp, "in_proj", d * P, (d + 1) * P),
                              ctxt[:, h * 512:(h + 1) * 512], start=True, stop=True)
                last.then_inc(proj_mm, 1)
            for d in range(ND):
                pe.wait_ge(u_done, d + 1)
                for h in range(2):
                    uh = u[:, d, h * 512:(h + 1) * 512]
                    mm(ps[0:96, 4 + h, :], col(MIX, mixp, "x_proj_bc", d * 96, (d + 1) * 96), uh,
                       start=(d == 0), stop=(d == ND - 1))
                    last = mm(ps[0:DTR, 6 + h, :], col(MIX, mixp, "x_proj_dt", d * DTR, (d + 1) * DTR), uh,
                              start=(d == 0), stop=(d == ND - 1))
            last.then_inc(xproj_mm, 1)
            pe.wait_ge(dtl_copied, 1)
            for d in range(ND):
                for h in range(2):
                    last = mm(ps[:, 2 * d + h, :], dtp[0:DTR, d * P:(d + 1) * P], dtl[0:DTR, h * 512:(h + 1) * 512],
                              start=True, stop=True)
                last.then_inc(dt_mm, 1)
            pe.wait_ge(sp_parts, 2 * ND)
            pe.wait_ge(bc_split, 1)
            pe.wait_ge(in_misc, 16)
            pe.wait_ge(in_con, 64)

            def spread(n, b):
                need(pe, drive_done, 2 * n)
                lhs = sel[:, bass.ds(n * P, P)]
                for h in range(2):
                    last = mm(ps[:, h, :], lhs, bcst[:, h * 512:(h + 1) * 512], start=True, stop=True)
                last.then_inc(b_mm, 1)
                need(pe, c_copied, n)
                lhs = sel[:, bass.ds(n * P + NST * P, P)]
                for h in range(2):
                    last = mm(ps[:, 2 + h, :], lhs, bcst[:, h * 512:(h + 1) * 512], start=True, stop=True)
                last.then_inc(c_mm, 1)

            def add_y(n, b):
                for d in range(ND):
                    pe.wait_ge(prod_done, n * ND + (d + 1))
                    for h in range(2):
                        last = mm(ps[:, 4 + 2 * d + h, :], ident, state[b][d][:, h * 512:(h + 1) * 512],
                                  start=isinstance(n, int) and n == 0, stop=isinstance(n, int) and n == NST - 1)
                    last.then_inc(y_mm, 1)

            skewed(pe, NST, [(0, spread), (2, add_y)])
            pe.wait_ge(gated, ND)
            for b in range(B):
                for h in range(2):
                    for d in range(ND):
                        last = nc.tensor.transpose(ps[:, b, h * H + d * P:h * H + (d + 1) * P],
                                                   drive[d][:, b * L + h * P:b * L + (h + 1) * P], ident)
                last.then_inc(yt_mm, 1)
            if upto < 2:
                return

            def transpose_normed(dst_banks, seen):
                pe.wait_ge(ln_out, seen)
                for k in range(2):
                    for half in range(2):
                        for t in range(4):
                            last = nc.tensor.transpose(ps[:, dst_banks + 2 * k + half, t * P:(t + 1) * P],
                                                       xn[:, half * 4 + t, k * P:(k + 1) * P], ident)
                    last.then_inc(xnt_mm, 1)

            pe.wait_ge(mixed, B)
            transpose_normed(4, 2 * NT)
            pe.wait_ge(xnt_copied, 2)
            for t in range(NT):
                for k in range(2):
                    last = mm(ps[:, 0, t * E:(t + 1) * E], xnt[:, k, t * P:(t + 1) * P],
                              col(ROUTE, routep, "w_gate", k * E, (k + 1) * E),
                              start=(t == 0 and k == 0), stop=(t == NT - 1 and k == 1), skip_group_check=True)
            last.then_inc(logit_mm, 1)
            pe.wait_ge(picked, 1)
            mm(ps[:, 1, 0:NT * E], before16, mask16, start=True, stop=False, skip_group_check=True)
            for t in range(NT - 1):
                after = NT - 1 - t
                mm(ps[:, 1, (t + 1) * E:NT * E], ones16,
                   mask16[:, t * E:(t + 1) * E].unsqueeze(1).broadcast_to([P, after, E]),
                   start=False, stop=(t == NT - 2), skip_group_check=True)
            for t in range(NT):
                last = mm(ps[:, 2, 0:E], ones16, mask16[:, t * E:(t + 1) * E], start=(t == 0), stop=(t == NT - 1))
            last.then_inc(rank_mm, 1)
            for m in range(QN):
                pe.wait_ge(wquant, m + 1)
                need(pe, wt_copied, 2 * m)
                for q in range(2):
                    for t in range(8):
                        src = fwq[:, t * H + q * P:t * H + (q + 1) * P] if m == 0 else \
                            fwq[:, q * F + t * P:q * F + (t + 1) * P]
                        last = nc.tensor.transpose(bankb[4 + q][:, t * P:(t + 1) * P], src, identb[:])
                    last.then_inc(wt_mm, 1)
            pe.wait_ge(slots_ready, 1)
            for t in range(NT):
                last = mm(ps[:, t // 2, (t % 2) * H:(t % 2 + 1) * H], ctxt[:, t * P:(t + 1) * P],
                          col(ROUTE, routep, "wkv", 0, H), start=True, stop=True)
                if t % 4 == 3:
                    last.then_inc(k_mm, 1)
            for t in range(NT):
                need(pe, v_saved, t // 2 - 1)
                last = mm(ps[:, 6 + t // 2 % 2, (t % 2) * H:(t % 2 + 1) * H], ctxt[:, t * P:(t + 1) * P],
                          col(ROUTE, routep, "wkv", H, 2 * H), start=True, stop=True)
                if t % 2 == 1:
                    last.then_inc(v_mm, 1)
            pe.wait_ge(wt_copied, 2 * QN)
            pe.wait_ge(v_saved, NT // 2)
            pe.wait_ge(k_saved, 2)
            pe.wait_ge(in_w, 16 * 2 * E)

            def expert_of(i):
                return pe.value_load(tile_expert[0:1, bass.ds(i, 1)], min_val=0, max_val=E - 1)

            def turn_rows(i, b):
                pe.wait_ge(row_in[b], (i // 2) * 16 + 16 if isinstance(i, int) else (i - b) * 8 + 16)
                need(pe, rowt_copied, i)
                for k in range(2):
                    last = nc.tensor.transpose(ps[:, 6, k * P:(k + 1) * P], xg[b][:, k * P:(k + 1) * P], ident)
                last.then_inc(row_mm, 1)

            def up(i, b):
                e = expert_of(i)
                pe.wait_ge(rowt_copied, i + 1)
                need(pe, h_done, i)
                for m in range(2):
                    for h in range(2):
                        for k in range(2):
                            last = mm(ps[:, 2 * m + h, 0:IC], xgt[b][:, k * P:(k + 1) * P],
                                      w13s[:, bass.ds(e, 1), m, k, h * IC:(h + 1) * IC]
                                      .rearrange("p a n -> p (a n)"), start=(k == 0), stop=(k == 1))
                    last.then_inc(up_mm, 1)

            def turn_h(i, b):
                pe.wait_ge(h_done, i + 1)
                need(pe, ht_copied, 2 * i)
                for j in range(KI):
                    w = min(P, I - j * P)
                    last = nc.tensor.transpose(ps[0:w, 4 + j // 3, (j % 3) * P:(j % 3 + 1) * P],
                                               hbuf[b][:, j * P:j * P + w], ident)
                    if j % 3 == 2:
                        last.then_inc(ht_mm, 1)

            def down(i, b):
                e = expert_of(i)
                pe.wait_ge(ht_copied, 2 * i + 2)
                need(pe, down_copied, i)
                for j in range(KI):
                    w = min(P, I - j * P)
                    last = mm(ps[:, 7, 0:H], ht[b][0:w, j, :],
                              w2s[0:w, bass.ds(e, 1), j, :].rearrange("p a n -> p (a n)"),
                              start=(j == 0), stop=(j == KI - 1))
                last.then_inc(down_mm, 1)

            skewed(pe, SLOT_TILES, [(2, turn_h), (0, turn_rows), (1, up), (2, down)])
            if upto < 3:
                return

            pe.wait_ge(in_late, 16)
            pe.wait_ge(down_copied, SLOT_TILES)
            transpose_normed(0, 3 * NT)
            pe.wait_ge(xnt_copied, 4)
            for t in range(NT):
                for k in range(2):
                    last = mm(ps[:, 4 + t // 2, (t % 2) * H:(t % 2 + 1) * H], xnt3[:, k, t * P:(t + 1) * P],
                              col(LATE, late_s, "wq", k * H, (k + 1) * H), start=(k == 0), stop=(k == 1))
                if t % 2 == 1:
                    last.then_inc(q_mm, 1)
            pe.wait_ge(stacked, 2 * NT)
            pe.wait_ge(stack_ones, 1)

            def turn_qk(n, b):
                need(pe, t2_copied, n - 2)
                need(pe, t1_copied, n)
                for a, st in enumerate((qst, kst)):
                    for t in range(2):
                        last = mm(ps[:, 6, (2 * a + t) * P:(2 * a + t + 1) * P],
                                  st[:, bass.ds(n, 1), t, :].rearrange("p a r -> p (a r)"), ident16,
                                  start=(a + t == 0), stop=(a + t == 3), skip_group_check=True)
                last.then_inc(t1_mm, 1)

            def row_scores(n, b, half):
                pe.wait_ge(t1_copied, n + 1)
                pe.wait_ge(masked, HPU * n + 2 * half + 2)
                need(pe, mx_done, 2 * n + half - 1)
                for t in range(2):
                    last = mm(ps[:, 2 * half + t, :], qkt[b][:, t * P:(t + 1) * P],
                              kmask[b][:, 2 * half:2 * half + 2, :].rearrange("p j k -> p (j k)"),
                              start=True, stop=True)
                last.then_inc(mx_mm, 1)

            def turn_q(n, b):
                pe.wait_ge(shift_done, n + 1)
                pe.wait_ge(t1_copied, n + 3 if not isinstance(n, int) else min(n + 3, UNITS))
                need(pe, t2_copied, n)
                for t in range(2):
                    last = mm(ps[:, 6, t * P:(t + 1) * P], qst[:, bass.ds(n, 1), t, :].rearrange("p a r -> p (a r)"),
                              ident16, start=(t == 0), stop=(t == 1), skip_group_check=True)
                last.then_inc(t2_mm, 1)

            def key_scores(n, b, half):
                pe.wait_ge(t2_copied, n + 1)
                for j in range(2 * half, 2 * half + 2):
                    need(pe, exp_done, HPU * n + (j - 1))
                    for t in range(2):
                        last = mm(ps[:, 4 + j % 2, t * L:(t + 1) * L], kmask[b][:, j, t * P:(t + 1) * P],
                                  q2t[b % 2], start=(t == 0), stop=(t == 1), skip_group_check=True)
                    last.then_inc(s_mm, 1)

            def weigh_v(n, b):
                pe.wait_ge(exp_done, HPU * n + HPU)
                pe.wait_ge(v_unit, n + 1)
                need(pe, o_copied, n)
                for t in range(2):
                    for j in range(HPU):
                        last = mm(ps[j * HS:(j + 1) * HS, 7, 0:L], vu[b % 2][:, t, j * HS:(j + 1) * HS],
                                  pexp[b % 2][:, (j * 2 + t) * L:(j * 2 + t + 1) * L], start=(t == 0), stop=(t == 1),
                                  skip_group_check=True)
                last.then_inc(pv_mm, 1)

            skewed(pe, UNITS, [(3, turn_q), (2, partial(row_scores, half=1)), (3, partial(key_scores, half=0)),
                               (0, turn_qk), (3, partial(key_scores, half=1)), (1, partial(row_scores, half=0)),
                               (4, weigh_v)], turn=4)
            pe.wait_ge(o_copied, UNITS)
            pe.wait_ge(mx_done, 2 * UNITS)
            for g in range(B):
                if g >= 2:
                    pe.wait_ge(o_norm, g - 1)
                for w in range(UNITS // B):
                    for t in range(2):
                        last = nc.tensor.transpose(ps[:, g % 2 * 4 + w // 2, (w % 2 * 2 + t) * P:(w % 2 * 2 + t + 1) * P],
                                                   ost[:, g * (UNITS // B) + w, t * P:(t + 1) * P], ident)
                last.then_inc(ot_mm, 1)
            pe.wait_ge(o_norm, B)
            for k in range(2):
                for t in range(NT):
                    last = nc.tensor.transpose(
                        ps[:, 2 * k + t // 4, (t % 4) * P:(t % 4 + 1) * P],
                        attn[:, t % 2, (t // 2) * 8 + 4 * k:(t // 2) * 8 + 4 * k + 4, :]
                        .rearrange("p u r -> p (u r)"), ident)
                last.then_inc(at_mm, 1)
            pe.wait_ge(at_copied, 2)
            for t in range(NT):
                for k in range(2):
                    last = mm(ps[:, 4 + t // 2, (t % 2) * H:(t % 2 + 1) * H], attnt[:, k, t * P:(t + 1) * P],
                              col(LATE, late_s, "wout", k * H, (k + 1) * H), start=(k == 0), stop=(k == 1))
            last.then_inc(wo_mm, 1)
            if upto < 4:
                return

            pe.wait_ge(hq_ready, 1)
            for k in range(2):
                for t in range(NT):
                    last = nc.tensor.transpose(bankb[k][:, t * P:(t + 1) * P],
                                               hqb[:, t * H + k * P:t * H + (k + 1) * P], identb[:])
                last.then_inc(hq_mm, 1)
            pe.wait_ge(hq_copied, 2)

            def widen(t, b):
                need(pe, f1_done, t - 1)
                for h in range(2):
                    for k in range(2):
                        last = mm(ps[:, 2 * b + h, :], hqt[:, k, bass.ds(t * P, P)], w1q[:, k, h * 512:(h + 1) * 512],
                                  start=(k == 0), stop=(k == 1))
                last.then_inc(f1_mm, 1)

            def turn_f(t, b):
                pe.wait_ge(fq_done, t + 1)
                need(pe, ft_copied, t - 1)
                for j in range(F // P):
                    last = nc.tensor.transpose(bankb[4 + b][:, j * P:(j + 1) * P], gq[b][:, j * P:(j + 1) * P],
                                               identb[:])
                last.then_inc(ft_mm, 1)

            def narrow(t, b):
                pe.wait_ge(ft_copied, t + 1)
                need(pe, f2_done, t - 1)
                for j in range(F // P):
                    last = mm(ps[:, 6 + b, 0:H], gqt[b][:, j, :], w2q[:, j, :], start=(j == 0),
                              stop=(j == F // P - 1))
                last.then_inc(f2_mm, 1)

            skewed(pe, NT, [(0, widen), (1, turn_f), (2, narrow)])

        @block.scalar
        def _(act):
            A = nc.scalar.activation
            ln_round = [0]

            def deviation():
                ln_round[0] += 1
                act.wait_ge(ln_mv, NT * ln_round[0])
                A(sd[:], mv[:, :, 1], ACT.Sqrt, bias=eps_t).then_inc(ln_sd, 1)

            eps_t = EPS
            deviation()
            for d in range(ND):
                act.wait_ge(proj_mm, d + 1)
                for h in range(2):
                    A(xpad[:, d, 2 * h:2 * h + 2, TAPS - 1:], ps[:, 2 * d + h, :].rearrange("p (b l) -> p b l", b=2),
                      ACT.Copy).then_inc(proj_copied, 1)
            for d in range(ND):
                act.wait_ge(conv_done, d + 1)
                A(u[:, d, :], conv[:, d, :], ACT.Silu, bias=col(MIX, mixp, "conv_b", d, d + 1)).then_inc(u_done, 1)
            act.wait_ge(ln_out, NT)
            A(xn[:], xn[:], ACT.Silu).then_inc(gate_done, 1)
            act.wait_ge(xproj_mm, 1)
            A(dtl[0:DTR, :], ps[0:DTR, 6:8, :], ACT.Copy).then_inc(dtl_copied, 1)
            act.wait_ge(zero_pad, 2)
            A(bcst[0:96, :], ps[0:96, 4:6, :], ACT.Copy).then_inc(bc_top, 1)
            A(acoef, col(MIX, mixp, "a_log"), ACT.Exp).then_inc(act_step, 1)
            act.wait_ge(act_step, 1)
            A(acoef, acoef, ACT.Copy, scale=-1.0).then_inc(a_ready, 1)
            for d in range(ND):
                act.wait_ge(dt_mm, d + 1)
                v = ps[:, 2 * d:2 * d + 2, :]
                bias = col(MIX, mixp, "dt_b", d, d + 1)
                A(sp_abs[:, d * T:(d + 1) * T], v, ACT.Abs, bias=bias).then_inc(sp_parts, 1)
                A(sp_relu[:, d * T:(d + 1) * T], v, ACT.Relu, bias=bias).then_inc(sp_parts, 1)
            act.wait_ge(sp_parts, 2 * ND)
            A(sp_exp, sp_abs, ACT.Exp, scale=-1.0).then_inc(sp_sq, 1)
            act.wait_ge(dve_step, 1)
            A(sp_s2, sp_s, ACT.Square).then_inc(sp_sq, 1)
            act.wait_ge(a_ready, 1)
            act.wait_ge(dt_ready, 1)

            def decays(n, b):
                for d in range(ND):
                    need(act, scan_done, ND * (n - 2) + (d + 1) if not isinstance(n, int) or n >= 2 else 0)
                    A(decay[b][d], dts[:, d, :], ACT.Exp, scale=acoef[:, bass.ds(n + d * NST, 1)]) \
                        .then_inc(decay_done, 1)

            def copy_c(n, b):
                act.wait_ge(c_mm, n + 1)
                need(act, prod_done, ND * (n - 1))
                A(crow[b], ps[:, 2:4, :], ACT.Copy).then_inc(c_copied, 1)

            skewed(act, NST, [(0, decays), (0, copy_c)])
            if upto < 2:
                return

            def copy_normed(dst, bank, seen):
                for k in range(2):
                    act.wait_ge(xnt_mm, seen + k + 1)
                    A(dst[:, k, :], ps[:, bank + 2 * k:bank + 2 * k + 2, :], ACT.Copy).then_inc(xnt_copied, 1)

            deviation()
            copy_normed(xnt, 4, 0)
            for m, dst in enumerate((w1q, w2q)):
                for q in range(2):
                    act.wait_ge(wt_mm, 2 * m + q + 1)
                    if m == 0:
                        A(w1q[:, q, :], bankb[4 + q], ACT.Copy).then_inc(wt_copied, 1)
                    else:
                        A(w2q[:, :, q * P:(q + 1) * P], bankb[4 + q].rearrange("p (t r) -> p t r", r=P),
                          ACT.Copy).then_inc(wt_copied, 1)

            act.wait_ge(wquant, QN)
            for g in range(NT // 2):
                act.wait_ge(v_mm, g + 1)
                A(vraw[:, 2 * g:2 * g + 2, :], ps[:, 6 + g % 2, :], ACT.Copy).then_inc(v_saved, 1)
            act.wait_ge(rope_tab, 1)
            A(ang[:], ang2[:], ACT.Sin).then_inc(sin_done, 1)
            act.wait_ge(scattered, 32 * NT)
            for g in range(2):
                act.wait_ge(k_mm, g + 1)
                A(xn[:, 4 * g:4 * g + 4, :], ps[:, 2 * g:2 * g + 2, :], ACT.Copy).then_inc(k_saved, 1)

            act.wait_ge(slots_ready, 1)
            act.wait_ge(logit_mm, 1)

            def copy_rows(i, b):
                act.wait_ge(row_mm, i + 1)
                need(act, up_mm, 2 * i - 2)
                A(xgt[b], ps[:, 6, 0:2 * P], ACT.Copy).then_inc(rowt_copied, 1)

            def silus(i, b):
                act.wait_ge(up_mm, 2 * i + 1)
                need(act, h_done, i - 1)
                A(silu_h[b].rearrange("p (h n) -> p h n", h=2), ps[:, 0:2, 0:IC], ACT.Silu).then_inc(silu_done, 1)

            def copy_ht(i, b):
                act.wait_ge(ht_mm, 2 * i + 1)
                need(act, down_mm, i - 1)
                A(ht[b][:, 0:3, :], ps[:, 4, 0:3 * P], ACT.Copy).then_inc(ht_copied, 1)
                act.wait_ge(ht_mm, 2 * i + 2)
                A(ht[b][:, 3:5, :], ps[:, 5, 0:2 * P], ACT.Copy)
                A(ht[b][0:I - 5 * P, 5, :], ps[0:I - 5 * P, 5, 2 * P:3 * P], ACT.Copy).then_inc(ht_copied, 1)

            skewed(act, SLOT_TILES, [(2, copy_ht), (0, copy_rows), (1, silus)])
            if upto < 3:
                return

            def cast_tile(st, src, second, t):
                dst = st.rearrange("p (b g) t (j r) -> p b g t j r", b=B, r=HS)[:, t // 2, :, t % 2]
                src = src.rearrange("p (g j r) -> p g j r", g=8, r=HD)
                A(dst[:, :, :, 0:8], src, ACT.Copy).then_inc(cast_hi, 1)
                A(dst[:, :, :, second:second + 8], src, ACT.Copy).then_inc(cast_hi, 1)

            act.wait_ge(stack_ones, 1)
            act.wait_ge(k_roped, NT)
            for t in range(NT):
                cast_tile(kst, xn[:, t, :], 8, t)
            deviation()
            copy_normed(xnt3, 0, 2)
            act.wait_ge(stack_zero, 7)
            act.wait_ge(v_saved, NT // 2)
            for t in range(NT):
                A(vst.rearrange("p (b g) t (j r) -> p b g t j r", b=B, r=HS)[:, t // 2, :, t % 2, :, 0:HD],
                  vraw[:, t, :].rearrange("p (g j r) -> p g j r", g=8, r=HD), ACT.Copy).then_inc(v_copied, 1)
            act.wait_ge(v_copied, NT)
            for t in range(NT):
                act.wait_ge(roped, t + 1)
                cast_tile(qst, rope_a[:, t * H:(t + 1) * H], 16, t)

            def copy_q2(n, b):
                act.wait_ge(t2_mm, n + 1)
                need(act, s_mm, HPU * (n - 1))
                A(q2t[b % 2], ps[:, 6, 0:2 * P], ACT.Copy).then_inc(t2_copied, 1)

            def exps(n, b):
                need(act, pv_mm, n - 1)
                for j in range(HPU):
                    act.wait_ge(s_mm, HPU * n + (j + 1))
                    A(pexp[b % 2][:, 2 * j * L:2 * (j + 1) * L], ps[:, 4 + j % 2, :], ACT.Exp,
                      scale=float(1.0 / np.sqrt(HD))).then_inc(exp_done, 1)

            def copy_qk(n, b):
                act.wait_ge(t1_mm, n + 1)
                if not isinstance(n, int) or n > 3:
                    act.wait_ge(mx_mm, 2 * (n - 3))
                    act.wait_ge(masked, HPU * (n - 3))
                A(qkt[b], ps[:, 6, :], ACT.Copy).then_inc(t1_copied, 1)

            def copy_o(n, b):
                act.wait_ge(pv_mm, n + 1)
                A(ost[:, bass.ds(n, 1), :].rearrange("p a q -> p (a q)"), ps[:, 7, 0:L], ACT.Copy).then_inc(o_copied, 1)

            skewed(act, UNITS, [(3, copy_q2), (5, copy_o), (3, exps), (0, copy_qk)], turn=4)
            for k in range(2):
                act.wait_ge(at_mm, k + 1)
                A(attnt[:, k, :], ps[:, 2 * k:2 * k + 2, :], ACT.Copy).then_inc(at_copied, 1)
            if upto < 4:
                return

            deviation()
            deviation()
            for k in range(2):
                act.wait_ge(hq_mm, k + 1)
                A(hqt[:, k, :], bankb[k], ACT.Copy).then_inc(hq_copied, 1)

            def gelus(t, b):
                act.wait_ge(f1_done, t + 1)
                need(act, fq_done, t - 1)
                A(g1[b], f1[b], ACT.Gelu_apprx_tanh).then_inc(gelu_done, 1)

            def copy_f(t, b):
                act.wait_ge(ft_mm, t + 1)
                need(act, f2_mm, t - 1)
                A(gqt[b].rearrange("p k t -> p (k t)"), bankb[4 + b], ACT.Copy).then_inc(ft_copied, 1)

            skewed(act, NT, [(0, gelus), (1, copy_f)])

        @block.vector
        def _(dve):
            v = nc.vector
            chain = [0]

            def link(ins):
                chain[0] += 1
                ins.then_inc(ln_chain, 1)
                dve.wait_ge(ln_chain, chain[0])

            ln_round = [0]

            def ln_sums(src, t):
                v.bn_stats(stats[:, t, :], src[:, t, :]).then_inc(ln_stats, 1)

            def layer_norm(src, dst, summed=False):
                ln_round[0] += 1
                k = ln_round[0]
                if not summed:
                    for t in range(NT):
                        ln_sums(src, t)
                dve.wait_ge(ln_stats, NT * k)
                for t in range(NT):
                    v.bn_aggr(mv[:, t, :], stats[:, t, :]).then_inc(ln_mv, 1)
                dve.wait_ge(ln_sd, k)
                link(v.reciprocal(rs[:], sd[:]))
                for t in range(NT):
                    v.tensor_scalar(dst[:, t, :], src[:, t, :], mv[:, t, 0:1], rs[:, t:t + 1], ALU.subtract,
                                    ALU.mult).then_inc(ln_out, 1)

            dve.wait_ge(in_x, 16)
            layer_norm(xa, xn)
            dve.wait_ge(zero_pad, 1)
            for d in range(ND):
                dve.wait_ge(proj_copied, 2 * d + 2)
                acc = conv[:, d, :].rearrange("p (b l) -> p b l", b=B)
                w = [col(MIX, mixp, "conv_w", d * TAPS + k, d * TAPS + k + 1) for k in range(TAPS)]
                link(v.tensor_scalar(acc, xpad[:, d, :, 0:L], w[0], None, ALU.mult))
                for k in range(1, TAPS - 1):
                    link(v.scalar_tensor_tensor(out=acc, in0=xpad[:, d, :, k:k + L], scalar=w[k], in1=acc,
                                                op0=ALU.mult, op1=ALU.add))
                v.scalar_tensor_tensor(out=acc, in0=xpad[:, d, :, TAPS - 1:], scalar=w[TAPS - 1], in1=acc,
                                       op0=ALU.mult, op1=ALU.add).then_inc(conv_done, 1)
            dve.wait_ge(bc_top, 1)
            dve.wait_ge(zero_pad, 2)
            bc = ps[0:64, 4:6, :].rearrange("p a n -> p (a n)")
            link(v.tensor_tensor(rem[0:64, :], bc, bcst[0:64, :], ALU.subtract))
            link(v.tensor_copy(bcst[0:64, :], rem[0:64, :]))
            v.tensor_tensor(bcst[0:32, :], rem[0:32, :], bcst[0:32, :], ALU.subtract).then_inc(bc_split, 1)
            dve.wait_ge(sp_sq, 1)
            link(v.tensor_scalar(sp_rec, sp_exp, 2.0, None, ALU.add))
            link(v.reciprocal(sp_rec, sp_rec))
            v.tensor_tensor(sp_s, sp_exp, sp_rec, ALU.mult).then_inc(dve_step, 1)
            dve.wait_ge(sp_sq, 2)
            dflat = dts.rearrange("p d t -> p (d t)")
            link(v.tensor_scalar(dflat, sp_s2, LOG1P[4], None, ALU.mult))
            for cf in LOG1P[3:0:-1]:
                link(v.scalar_tensor_tensor(out=dflat, in0=dflat, scalar=cf, in1=sp_s2, op0=ALU.add, op1=ALU.mult))
            link(v.scalar_tensor_tensor(out=dflat, in0=dflat, scalar=LOG1P[0], in1=sp_s, op0=ALU.add, op1=ALU.mult))
            link(v.tensor_tensor(dflat, dflat, sp_relu, ALU.add))
            link(v.tensor_tensor(dtu.rearrange("p d t -> p (d t)"), dflat, u.rearrange("p d t -> p (d t)"), ALU.mult))
            v.memset(dts.rearrange("p d (b l) -> p (d b) l", b=B)[:, :, 0:1], 1e25).then_inc(dt_ready, 1)

            def drives(n, b):
                dve.wait_ge(b_mm, n + 1)
                for d in range(ND):
                    if not isinstance(n, int) or n:
                        dve.wait_ge(scan_done, ND * (n - 1) + (d + 1))
                    v.tensor_tensor(drive[d], dtu[:, d, :], ps[:, 0:2, :].rearrange("p a n -> p (a n)"), ALU.mult) \
                        .then_inc(drive_done, 1)

            def scans(n, b):
                for d in range(ND):
                    need(dve, y_mm, ND * (n - 2) + (d + 1) if not isinstance(n, int) or n >= 2 else 0)
                    dve.wait_ge(drive_done, ND * n + (d + 1))
                    dve.wait_ge(decay_done, ND * n + (d + 1))
                    v.tensor_tensor_scan(state[b][d], decay[b][d], drive[d], 0.0, ALU.mult, ALU.add) \
                        .then_inc(scan_done, 1)

            skewed(dve, NST, [(0, drives), (0, scans)])
            dve.wait_ge(y_mm, ND * NST)
            dve.wait_ge(gate_done, 1)
            for d in range(ND):
                y = ps[:, 4 + 2 * d:6 + 2 * d, :].rearrange("p a n -> p (a n)")
                link(v.scalar_tensor_tensor(out=drive[d], in0=u[:, d, :], scalar=col(MIX, mixp, "skip", d, d + 1),
                                            in1=y, op0=ALU.mult, op1=ALU.add))
                yb = drive[d].rearrange("p (b l) -> p b l", b=B)
                v.tensor_tensor(yb, yb, xn[:].rearrange("p (b e) l -> p b e l", e=ND)[:, :, d, :], ALU.mult) \
                    .then_inc(gated, 1)
            for b in range(B):
                dve.wait_ge(yt_mm, b + 1)
                v.tensor_tensor(xa[:, 2 * b:2 * b + 2, :].rearrange("p a h -> p (a h)"),
                                xa[:, 2 * b:2 * b + 2, :].rearrange("p a h -> p (a h)"), ps[:, b, :], ALU.add) \
                    .then_inc(mixed, 1)
            if upto < 2:
                return

            dve.wait_ge(mixed, B)
            layer_norm(xa, xn)
            dve.wait_ge(logit_mm, 1)
            li, sh, key, key2, oh1, oh2, pe_, tmp = rt[:8]

            def v3(a):
                return a.rearrange("p (t e) -> p t e", t=NT)

            def over(a):
                return a.unsqueeze(2).broadcast_to([P, NT, E])

            m_, k2_, ev, den, rec_, _ = small
            link(v.tensor_scalar(li, ps[:, 0, 0:NT * E], 128.0, MAGIC, ALU.mult, ALU.add))
            link(v.tensor_scalar(li, li, -MAGIC, None, ALU.add))
            link(v.tensor_reduce(m_, v3(li), AX.X, ALU.max))
            link(v.tensor_tensor(v3(sh), v3(li), over(m_), ALU.subtract))
            link(v.tensor_scalar(sh, sh, -128.0, None, ALU.max))
            link(v.scalar_tensor_tensor(out=key, in0=sh, scalar=float(E), in1=col(CON, cons, "expert_order"),
                                        op0=ALU.mult, op1=ALU.add))
            link(v.tensor_reduce(m_, v3(key), AX.X, ALU.max))
            link(v.tensor_tensor(v3(oh1), v3(key), over(m_), ALU.is_equal))
            link(v.scalar_tensor_tensor(out=key2, in0=oh1, scalar=-4096.0, in1=key, op0=ALU.mult, op1=ALU.add))
            link(v.tensor_reduce(m_, v3(key2), AX.X, ALU.max))
            link(v.tensor_tensor(v3(oh2), v3(key2), over(m_), ALU.is_equal))
            v.tensor_tensor(mask16, oh1, oh2, ALU.add).then_inc(picked, 1)
            link(v.tensor_tensor(tmp, oh2, sh, ALU.mult))
            link(v.tensor_reduce(k2_, v3(tmp), AX.X, ALU.add))
            lt = rt_lut.rearrange("p (t n) -> p t n", t=NT)
            link(v.tensor_tensor(lt, col(CON, cons, "lut_key").unsqueeze(1).broadcast_to([P, NT, LUTN]),
                                 k2_.unsqueeze(2).broadcast_to([P, NT, LUTN]), ALU.is_equal))
            link(v.tensor_tensor(lt, lt, col(CON, cons, "lut").unsqueeze(1).broadcast_to([P, NT, LUTN]), ALU.mult))
            link(v.tensor_reduce(ev, lt, AX.X, ALU.add))
            link(v.tensor_scalar(den, ev, 65536.0, None, ALU.add))
            link(v.reciprocal(rec_, den))
            link(v.tensor_scalar(gate_w[:, 0, :], rec_, 65536.0, None, ALU.mult))
            link(v.tensor_tensor(gate_w[:, 1, :], rec_, ev, ALU.mult))
            dve.wait_ge(rank_mm, 1)
            tiles, upto_, before = cum[:, 0:E], cum[:, E:2 * E], cum[:, 2 * E:3 * E]
            link(v.tensor_scalar(tiles, ps[:, 2, 0:E], 1.0 / P, (P - 1.0) / P - 0.5 + 0.5 / P, ALU.mult, ALU.add))
            link(v.tensor_scalar(tiles, tiles, MAGIC, -MAGIC, ALU.add, ALU.add))
            link(v.tensor_tensor_scan(upto_, col(CON, cons, "ones"), tiles, 0.0, ALU.mult, ALU.add))
            link(v.tensor_tensor(before, upto_, tiles, ALU.subtract))
            link(v.scalar_tensor_tensor(out=v3(pe_), in0=before.unsqueeze(1).broadcast_to([P, NT, E]),
                                        scalar=float(P), in1=v3(ps[:, 1, 0:NT * E]), op0=ALU.mult, op1=ALU.add))
            for s, oh in enumerate((oh1, oh2)):
                link(v.tensor_tensor(tmp, oh, pe_, ALU.mult))
                link(v.tensor_reduce(m_, v3(tmp), AX.X, ALU.add))
                link(v.tensor_copy(slots_i[:, s, :], m_))
            tx = texp.rearrange("p (i e) -> p i e", e=E)
            link(v.tensor_tensor(tx, col(CON, cons, "tile_index").unsqueeze(2).broadcast_to([P, SLOT_TILES + 1, E]),
                                 upto_.unsqueeze(1).broadcast_to([P, SLOT_TILES + 1, E]), ALU.is_ge))
            te = rt_lut[:, 0:SLOT_TILES + 1]
            link(v.tensor_reduce(te, tx, AX.X, ALU.add))
            v.tensor_scalar(tile_expert[:], te, float(E - 1), None, ALU.min).then_inc(slots_ready, 1)

            def mx_scales(scr, amax_in):
                am, e2, inv, sc = scr
                link(v.tensor_reduce(am, amax_in, AX.X, ALU.max, apply_absolute_value=True))
                link(v.tensor_scalar(am, am, 2.0 ** -100, None, ALU.max))
                link(v.tensor_scalar(e2.bitcast(I32), am.bitcast(I32), 0x7F800000, None, ALU.bitwise_and))
                link(v.tensor_scalar(inv.bitcast(I32), e2.bitcast(I32), -1.0, float(0x7F000000 + (6 << 23)),
                                     ALU.mult, ALU.add))
                link(v.tensor_scalar(sc, e2, 1.0 / 64, None, ALU.mult))

            def mx_quant(dst, src, y, scr, nb):
                def blocks(a):
                    return a.rearrange("p (n k) -> p n k", k=BLK)

                mx_scales(scr, blocks(src))
                _, _, inv, sc = scr
                link(v.tensor_tensor(blocks(y), blocks(src), inv.unsqueeze(2).broadcast_to([P, nb, BLK]), ALU.mult))
                link(v.tensor_scalar(y, y, MAGIC, -MAGIC, ALU.add, ALU.add))
                return v.scalar_tensor_tensor(out=blocks(dst), in0=blocks(y), scalar=127.0,
                                              in1=sc.unsqueeze(2).broadcast_to([P, nb, BLK]), op0=ALU.min,
                                              op1=ALU.mult)

            for m in range(QN):
                dve.wait_ge(in_ffnw, 16 * (m + 1) if m else 32)
                if m:
                    dve.wait_ge(wt_mm, 2 * m)
                mx_quant(fwq, fw_raw[m], fw_y, fw_scr, 64).then_inc(wquant, 1)

            link(v.tensor_tensor(ang[:, 0:64], col(ROUTE, routep, "pos"), col(CON, cons, "freq"), ALU.mult))
            link(v.tensor_scalar(ang[:, 64:128], ang[:, 0:64], float(np.pi / 2), None, ALU.add))
            link(v.tensor_scalar(ang2[:], ang[:], float(1 / (2 * np.pi)), MAGIC, ALU.mult, ALU.add))
            link(v.tensor_scalar(ang2[:], ang2[:], -MAGIC, None, ALU.add))
            link(v.scalar_tensor_tensor(out=ang2[:], in0=ang2[:], scalar=float(-2 * np.pi), in1=ang[:], op0=ALU.mult,
                                        op1=ALU.add))
            v.tensor_scalar(ang2[:], ang2[:], 3.1415925, -3.1415925, ALU.min, ALU.max).then_inc(rope_tab, 1)
            dve.wait_ge(sin_done, 1)
            v.tensor_tensor(sin8[:], ang[:, 0:64], col(CON, cons, "rope_sign"), ALU.mult).then_inc(sin_signed, 1)

            def gate_h(i, b):
                dve.wait_ge(up_mm, 2 * i + 2)
                dve.wait_ge(silu_done, i + 1)
                need(dve, ht_mm, 2 * i - 2)
                v.tensor_tensor(hbuf[b].rearrange("p (h n) -> p h n", h=2),
                                silu_h[b].rearrange("p (h n) -> p h n", h=2), ps[:, 2:4, 0:IC], ALU.mult) \
                    .then_inc(h_done, 1)

            def copy_down(i, b):
                dve.wait_ge(down_mm, i + 1)
                need(dve, row_out[b], (i // 2) * 16 if isinstance(i, int) else (i - b) * 8)
                v.tensor_copy(yrow[b], ps[:, 7, 0:H]).then_inc(down_copied, 1)

            skewed(dve, SLOT_TILES, [(1, gate_h), (2, copy_down)])
            if upto >= 3:
                dve.wait_ge(down_mm, SLOT_TILES)
                link(v.memset(kst.rearrange("p u t r -> p (u t r)").bitcast(U32), 0))
                v.memset(kst.rearrange("p u t (j r) -> p (u t j) r", r=HS)[:, :, 24:26], 1.0).then_inc(stack_ones, 1)

            def low_halves(st, src, t, seen, low):
                dst = st.rearrange("p (b g) t (j r) -> p b g t j r", b=B, r=HS)[:, t // 2, :, t % 2]
                dve.wait_ge(cast_hi, seen)
                v.tensor_tensor(dst[:, :, :, low:low + 8], src.rearrange("p (g j r) -> p g j r", g=8, r=HD),
                                dst[:, :, :, 0:8], ALU.subtract).then_inc(stacked, 1)

            for t in range(NT):
                dve.wait_ge(gathered[t % 4], 32 * (t // 4 + 1))
                link(v.scalar_tensor_tensor(out=xa[:, t, :], in0=gat[t % 4][0], scalar=gate_w[:, 0, t:t + 1],
                                            in1=xa[:, t, :], op0=ALU.mult, op1=ALU.add))
                v.scalar_tensor_tensor(out=xa[:, t, :], in0=gat[t % 4][1], scalar=gate_w[:, 1, t:t + 1],
                                       in1=xa[:, t, :], op0=ALU.mult, op1=ALU.add).then_inc(combined, 1)
                if upto >= 3:
                    low_halves(kst, xn[:, t, :], t, 2 * t + 2, 16)
                    dve.wait_ge(combined, t + 1)
                    ln_sums(xa, t)
            if upto < 3:
                return


            dve.wait_ge(stacked, NT)
            layer_norm(xa, xn, summed=True)
            for t in range(NT + 1):
                if t < NT:
                    dve.wait_ge(q_mm, t // 2 + 1)
                    src = ps[:, 4 + t // 2, (t % 2) * H:(t % 2 + 1) * H].rearrange("p (h r) -> p h r", r=HD)
                    a = rope_a[:, t * H:(t + 1) * H].rearrange("p (h r) -> p h r", r=HD)
                    b = rope_b[:, t * H:(t + 1) * H].rearrange("p (h r) -> p h r", r=HD)
                    cs = ang[:, 64 + t * 8:72 + t * 8].unsqueeze(1).broadcast_to([P, NHEAD, HD])
                    sn = sin8[:, t * 8:t * 8 + 8].unsqueeze(1).broadcast_to([P, NHEAD, HD])
                    v.tensor_tensor(a, src, cs, ALU.mult)
                    v.tensor_tensor(b[:, :, 0::2], src[:, :, 1::2], sn[:, :, 0::2], ALU.mult)
                    link(v.tensor_tensor(b[:, :, 1::2], src[:, :, 0::2], sn[:, :, 1::2], ALU.mult))
                    v.tensor_tensor(a, a, b, ALU.add).then_inc(roped, 1)
                if t:
                    low_halves(qst, rope_a[:, (t - 1) * H:t * H], t - 1, 2 * NT + 2 * t, 8)

            def maxima(n, b, half):
                dve.wait_ge(mx_mm, 2 * n + (half + 1))
                v.tensor_reduce(mx[b % 2].rearrange("p (t h j) -> p h t j", t=2, h=2)[:, half],
                                ps[:, 2 * half:2 * half + 2, :].rearrange("p t (j k) -> p t j k", j=2),
                                AX.X, ALU.max).then_inc(mx_done, 1)

            def shift(n, b):
                dve.wait_ge(mx_done, 2 * n + 2)
                m3 = mx[b % 2].rearrange("p (t j) -> p t j", t=2)
                dst = qst[:, bass.ds(n, 1)].rearrange("p a t (j r) -> p (a t) j r", r=HS)
                v.tensor_scalar(dst[:, :, :, 24], m3, -1.0, None, ALU.mult).then_inc(shift_hi, 1)
                dve.wait_ge(shift_hi, n + 1)
                v.scalar_tensor_tensor(out=dst[:, :, :, 25], in0=m3, scalar=-1.0, in1=dst[:, :, :, 24],
                                       op0=ALU.mult, op1=ALU.subtract).then_inc(shift_done, 1)

            def mask_k(n, b):
                dve.wait_ge(t1_copied, n + 1)
                for j in range(HPU):
                    need(dve, s_mm, HPU * (n - 4) + (j + 1) if not isinstance(n, int) or n >= 4 else 0)
                    r = slice(j * HS, (j + 1) * HS)
                    v.tensor_copy(kmask[b][r, j, :], qkt[b][r, 2 * P:4 * P]).then_inc(masked, 1)

            dve.wait_ge(stack_zero, 5)
            skewed(dve, UNITS, [(2, partial(maxima, half=0)), (2, partial(maxima, half=1)), (2, shift), (0, mask_k)],
                   turn=4)
            for g in range(B):
                dve.wait_ge(ot_mm, g + 1)
                o = ps[:, g % 2 * 4:g % 2 * 4 + 4, :].rearrange("p a (u t j r) -> p (a u) t j r", t=2, u=2, r=HS)
                units = slice(g * (UNITS // B), (g + 1) * (UNITS // B))
                r = orec[g % 2].rearrange("p (u t j) -> p u t j", t=2, j=HPU)
                for t in range(2):
                    v.reciprocal(r[:, :, t, :], o[:, :, t, :, HD]).then_inc(o_rec, 1)
                for t in range(2):
                    dve.wait_ge(o_rec, 2 * g + t + 1)
                    last = v.tensor_tensor(attn[:, t, units, :].rearrange("p u (j r) -> p (u j) r", r=HD),
                                           o[:, :, t, :, 0:HD].rearrange("p u j r -> p u j r"),
                                           r[:, :, t, :].unsqueeze(3).broadcast_to([P, UNITS // B, HPU, HD]), ALU.mult)
                last.then_inc(o_norm, 1)
            dve.wait_ge(wo_mm, 1)
            for t in range(NT):
                link(v.tensor_tensor(xa[:, t, :], xa[:, t, :], ps[:, 4 + t // 2, (t % 2) * H:(t % 2 + 1) * H],
                                     ALU.add))
                v.tensor_tensor(xa[:, t, :], xa[:, t, :], col(LATE, late_s, "bout"), ALU.add).then_inc(attn_done, 1)
            if upto < 4:
                return

            dve.wait_ge(attn_done, NT)
            layer_norm(xa, xb)
            dve.wait_ge(ln_out, 4 * NT)
            hn3 = hn.rearrange("p (t h) -> p t h", t=NT)
            layer_norm(xb, hn3)
            dve.wait_ge(ln_out, 5 * NT)
            link(v.tensor_tensor(hn3, hn3, col(LATE, late_s, "ln_w").unsqueeze(1).broadcast_to([P, NT, H]), ALU.mult))
            link(v.tensor_tensor(hb.rearrange("p (t h) -> p t h", t=NT), hn3,
                                 col(LATE, late_s, "ln_b").unsqueeze(1).broadcast_to([P, NT, H]), ALU.add))
            mx_quant(hqb, hb, hn, qs, NT * H // BLK).then_inc(hq_ready, 1)

            def add_b1(t, b):
                dve.wait_ge(f1_mm, t + 1)
                need(dve, gelu_done, t - 1)
                v.tensor_tensor(f1[b], ps[:, 2 * b:2 * b + 2, :].rearrange("p a n -> p (a n)"),
                                col(LATE, late_s, "b1"), ALU.add).then_inc(f1_done, 1)

            def quant_f(t, b):
                am, e2, inv, sc = fs[b]
                base = t * 7

                def linked(ins, k):
                    ins.then_inc(fq_chain, 1)
                    dve.wait_ge(fq_chain, base + k)

                def blocks(a):
                    return a.rearrange("p (n k) -> p n k", k=BLK)

                def wide(a):
                    return a.unsqueeze(2).broadcast_to([P, F // BLK, BLK])

                dve.wait_ge(gelu_done, t + 1)
                need(dve, ft_mm, t - 1)
                linked(v.tensor_reduce(am, blocks(g1[b]), AX.X, ALU.max, apply_absolute_value=True), 1)
                linked(v.tensor_scalar(am, am, 2.0 ** -100, None, ALU.max), 2)
                linked(v.tensor_scalar(e2.bitcast(I32), am.bitcast(I32), 0x7F800000, None, ALU.bitwise_and), 3)
                linked(v.tensor_scalar(inv.bitcast(I32), e2.bitcast(I32), -1.0, float(0x7F000000 + (6 << 23)),
                                       ALU.mult, ALU.add), 4)
                linked(v.tensor_scalar(sc, e2, 1.0 / 64, None, ALU.mult), 5)
                linked(v.tensor_tensor(blocks(gy[b]), blocks(g1[b]), wide(inv), ALU.mult), 6)
                linked(v.tensor_scalar(gy[b], gy[b], MAGIC, -MAGIC, ALU.add, ALU.add), 7)
                v.scalar_tensor_tensor(out=blocks(gq[b]), in0=blocks(gy[b]), scalar=127.0, in1=wide(sc),
                                       op0=ALU.min, op1=ALU.mult).then_inc(fq_done, 1)

            def finish(t, b):
                dve.wait_ge(f2_mm, t + 1)

                def linked(ins, k):
                    ins.then_inc(f2_chain, 1)
                    dve.wait_ge(f2_chain, t * 2 + k)

                def tile(a):
                    return a[:, bass.ds(t, 1), :].rearrange("p a h -> p (a h)")

                linked(v.tensor_tensor(f2[b], ps[:, 6 + b, 0:H], col(LATE, late_s, "b2"), ALU.add), 1)
                linked(v.tensor_tensor(r4[b], f2[b], tile(xb), ALU.add), 2)
                v.tensor_tensor(tile(xa), tile(xa), r4[b], ALU.add).then_inc(f2_done, 1)

            skewed(dve, NT, [(0, add_b1), (1, quant_f), (2, finish)])




def kernel(x, ctx_1024, fside_BxSx2_0, L0_xattn_in_proj_w, L0_xattn_conv_w, L0_xattn_conv_b, L0_xattn_x_proj_w,
           L0_xattn_dt_proj_w, L0_xattn_dt_proj_b, L0_xattn_A_log, L0_xattn_D, L0_ffn_w_gate, L0_ffn_w1, L0_ffn_w2,
           L0_ffn_w3, L1_xattn_Wq, L1_xattn_Wkv, L1_xattn_Wout, L1_xattn_bout, L1_ffn_ln_w, L1_ffn_ln_b, L1_ffn_W1,
           L1_ffn_b1, L1_ffn_W2, L1_ffn_b2):
    import ml_dtypes
    import concourse.bacc as bacc
    from concourse.bass_utils import run_bass_kernel_spmd

    def rows(a, n):
        a = np.asarray(a)
        return a.reshape(n, P, -1).transpose(1, 0, 2).reshape(P, -1)

    def every(a):
        return np.broadcast_to(np.asarray(a).reshape(1, -1), (P, np.asarray(a).size))

    xp = np.asarray(L0_xattn_x_proj_w)
    bc = np.concatenate([xp[DTR:]] * 3, axis=0).T
    w13 = np.stack([np.asarray(L0_ffn_w1), np.asarray(L0_ffn_w3)], 1)
    w13 = w13.transpose(0, 1, 3, 2).reshape(E, 2, 2, P, I).transpose(0, 3, 1, 2, 4).reshape(E, P, 4 * I)
    w2 = np.asarray(L0_ffn_w2).transpose(0, 2, 1)
    w2 = np.concatenate([w2, np.zeros((E, KI * P - I, H), w2.dtype)], 1)
    w2 = w2.reshape(E, KI, P, H).transpose(0, 2, 1, 3).reshape(E, P, KI * H)
    pos = np.repeat(np.asarray(fside_BxSx2_0).reshape(T, 2), 4, axis=1)

    eye = np.eye(P, dtype=np.float32)
    key = np.arange(-128, 1)
    lut = np.floor(np.exp(key / 128.0) * 65536)
    freq = np.array([1.0, 1.0, 0.01, 0.01] * 2, np.float32)
    before = np.triu(np.ones((P, P)), 1)
    con = np.concatenate([eye, every(lut), every(key), every(np.tile(np.arange(E)[::-1], NT)),
                          every(np.arange(SLOT_TILES + 1)), np.ones((P, E)), every(np.tile(freq, NT)),
                          every(np.tile([-1.0, 1.0], NT * 4))], axis=1).astype(np.float32)
    con16 = np.concatenate([eye, before, np.ones((P, P))], axis=1).astype(np.float16)
    k = np.arange(P)[:, None, None]
    j = np.arange(32)[None, :, None]
    select = np.broadcast_to((k % 32 == j) & (k < 96), (P, 32, P)).reshape(P, 32 * P)

    given = {
        "x": np.asarray(x).reshape(T, H),
        "ctx_t": np.asarray(ctx_1024).reshape(T, CTX).T,
        "mix": np.concatenate([np.asarray(L0_xattn_in_proj_w).T, rows(bc, ND), rows(xp[:DTR].T, ND),
                               rows(np.asarray(L0_xattn_conv_w).reshape(DI, TAPS), ND), rows(L0_xattn_conv_b, ND),
                               rows(L0_xattn_dt_proj_b, ND), rows(L0_xattn_D, ND), rows(L0_xattn_A_log, ND)], 1),
        "dt_proj": np.asarray(L0_xattn_dt_proj_w).T,
        "route": np.concatenate([rows(np.asarray(L0_ffn_w_gate).T, 2), rows(pos, NT), np.asarray(L1_xattn_Wkv)], 1),
        "w13": w13,
        "w2": w2,
        "late": np.concatenate([rows(L1_xattn_Wq, 2), rows(L1_xattn_Wout, 2),
                                every(L1_xattn_bout), every(L1_ffn_ln_w), every(L1_ffn_ln_b), every(L1_ffn_b1),
                                every(L1_ffn_b2)], 1),
        "ffn_w1": rows(L1_ffn_W1, F // P),
        "ffn_w2": rows(L1_ffn_W2, H // P),
        "con": con,
        "con16": con16,
        "bc_select": select.astype(ml_dtypes.bfloat16),
        "ident_b": eye.astype(ml_dtypes.bfloat16),
    }
    nc = bacc.Bacc("TRN2", target_bir_lowering=False, num_devices=1)
    arrays, aps = {}, {}
    for name, a in given.items():
        arrays[f"in_{name}"] = np.ascontiguousarray(a)
        aps[name] = nc.dram_tensor(f"in_{name}", a.shape, mybir.dt.from_np(a.dtype), kind="ExternalInput").ap()
    aps["out"] = nc.dram_tensor("out_x", (T, H), F32, kind="ExternalOutput").ap()
    build(nc, **aps)
    r = run_bass_kernel_spmd(nc, [arrays], core_ids=[0])
    return r.results[0]["out_x"].reshape(B, L, H)
```

```python
from contextlib import ExitStack
from functools import partial

import numpy as np

import concourse.bass as bass
from concourse import mybir

P = 128
B, L, H = 4, 256, 256
T = B * L
NT = T // P
CTX = 128
DI, NST, DTR, TAPS = 256, 16, 8, 4
ND = DI // P
PADL = L + TAPS - 1
E, I = 8, 704
IC = I // 2
KI = (I + P - 1) // P
SLOT_TILES = (2 * T + E * (P - 1)) // P
NHEAD, HD = 32, 8
HPU = 4
UNITS = B * NHEAD // HPU
HS = 32
F = 4 * H
BLK = 32
LUTN = 129
WSCALE = 256.0
SPLIT = 1024
EPS = 1e-5
MAGIC = 12582912.0

F32, BF16, F16 = mybir.dt.float32, mybir.dt.bfloat16, mybir.dt.float16
I32, U32 = mybir.dt.int32, mybir.dt.uint32
ALU = mybir.AluOpType
ACT = mybir.ActivationFunctionType
AX = mybir.AxisListType

LOG1P = ((1.0093576, 1.1060659), (-0.08225361, 3.257479), (-1.4247395, 2.7021122), (-2.3216915, 0.43240824))
LOG1P_SCALE = 0.0052326242

def _columns(*sizes):
    at, out = 0, {}
    for name, n in sizes:
        out[name] = (at, at + n)
        at += n
    return out, at


MIX, MIX_N = _columns(("in_proj", DI), ("x_proj", ND * (96 + DTR)), ("conv_w", ND * TAPS),
                      ("conv_b", ND), ("dt_b", ND), ("skip", ND), ("a_log", ND * NST))
CON, CON_N = _columns(("ident", P), ("lut", LUTN), ("lut_key", LUTN), ("expert_order", NT * E),
                      ("tile_index", SLOT_TILES + 1), ("ones", E), ("freq", NT * 8), ("rope_sign", NT * 8))
LATE, LATE_N = _columns(("wq", 2 * H), ("wout", 2 * H), ("bout", H), ("ln_w", H), ("ln_b", H),
                        ("b1", F), ("b2", H))
ROUTE, ROUTE_N = _columns(("w_gate", 2 * E), ("pos", NT * 8), ("wkv", 2 * H))


def need(eng, sem, value):
    if not isinstance(value, int) or value > 0:
        eng.wait_ge(sem, value)


def skewed(eng, count, stages, turn=2):
    late = max(s for s, _ in stages)
    first = late + late % 2 + turn
    loops = (count - first) // turn
    if loops < 2:
        loops = 0

    def peeled(r):
        for s, stage in stages:
            if 0 <= r - s < count:
                stage(r - s, (r - s) % turn)

    for r in range(first):
        peeled(r)
    if loops:
        with eng.Fori(0, loops) as v:
            for j in range(turn):
                for s, stage in stages:
                    stage(v * turn + (first + j - s), (first + j - s) % turn)
    for r in range(first + turn * loops, count + late):
        peeled(r)


def build(nc, x, ctx_t, mix, dt_proj, route, w13, w2, late, ffn_w1, ffn_w2, con, con16, bc_select, ident_b, out,
          upto=4):
    routed = nc.dram_tensor("routed_rows", (SLOT_TILES * P, H), F32, kind="Internal").ap()
    expert_out = nc.dram_tensor("expert_rows", (SLOT_TILES * P, H), F32, kind="Internal").ap()

    with ExitStack() as ctx:
        def sb(name, shape, dt=F32):
            return ctx.enter_context(nc.sbuf_tensor(name, shape, dt))

        def sem(name):
            return ctx.enter_context(nc.semaphore(name))

        ps = ctx.enter_context(nc.psum_tensor("ps", [P, 8, 512], F32))

        xa = sb("resid", [P, NT, H])
        zrow = sb("zeros", [P, H])
        xn = sb("normed", [P, NT, H])
        ctxt = sb("ctx_t", [P, T])
        mixp = sb("mix_params", [P, MIX_N])
        dtp = sb("dt_proj", [P, DI])
        routep = sb("route_params", [P, ROUTE_N])
        cons = sb("constants", [P, CON_N])
        cons16 = sb("constants16", [P, 3 * P], F16)
        identb = sb("ident_b", [P, P], BF16)
        w1q = sb("w1_quant_t", [P, 2, F], BF16)
        w2q = sb("w2_quant_t", [P, F // P, H], BF16)
        stats = sb("stats", [P, NT, 6])
        mv = sb("mean_var", [P, NT, 2])
        sd = sb("deviation", [P, NT])
        rs = sb("inv_deviation", [P, NT])
        gate_w = sb("gate_weights", [P, 2, NT])
        slots_i = sb("slots", [P, 2, NT], I32)
        tile_expert = sb("tile_expert", [P, SLOT_TILES + 1], I32)
        ang = sb("angles", [P, 2 * NT * 8])
        ang2 = sb("angles_reduced", [P, 2 * NT * 8])
        sin8 = sb("signed_sin", [P, NT * 8])
        rope_s = sb("rope_scratch", [P, H])
        W13E = 2 * 2 * I
        W2E = KI * H
        weights = sb("weights", [P, E * (W13E + W2E)])
        work = sb("work", [P, 8000])

        w13s = weights[:, 0:E * W13E].rearrange("p (e m k n) -> p e m k n", e=E, m=2, k=2)
        w13h = weights[:, 0:E * W13E].bitcast(F16).rearrange("p (e m k n two) -> p e m k n two", e=E, m=2, k=2, two=2)
        chunks = weights[:, 0:E * W13E].rearrange("p (i n) -> p i n", n=SPLIT)
        chunks_h = weights[:, 0:E * W13E].bitcast(F16).rearrange("p (i n two) -> p i n two", n=SPLIT, two=2)
        NSPLIT = E * W13E // SPLIT
        w2s = weights[:, E * W13E:].rearrange("p (e j n) -> p e j n", e=E, j=KI)

        class Carve:
            def __init__(self, base, at=0):
                self.base, self.at = base, at

            def __call__(self, n, dt=F32):
                words = n if dt in (F32, I32, U32) else (n + 1) // 2
                got = self.base[:, self.at:self.at + words]
                self.at += words
                assert self.at <= self.base.shape[1], (self.at, self.base.shape)
                return got if dt == F32 else got.bitcast(dt)

        def col(table, tensor, name, a=0, b=None):
            lo, hi = table[name]
            return tensor[:, lo + a:(hi if b is None else lo + b)]

        ident = col(CON, cons, "ident")
        ident16, before16, ones16 = (cons16[:, i * P:(i + 1) * P] for i in range(3))

        EARLY = 5
        c = Carve(weights, EARLY * W13E)
        sel = c(32 * P, BF16)
        bcst = c(T, BF16)
        u = c(ND * T).rearrange("p (d t) -> p d t", d=ND)
        dts = c(ND * T).rearrange("p (d t) -> p d t", d=ND)
        dtu = c(ND * T).rearrange("p (d t) -> p d t", d=ND)
        decay = [[c(T) for _ in range(ND)] for _ in range(2)]
        state = [[c(T) for _ in range(ND)] for _ in range(2)]
        drive = [c(T) for _ in range(ND)]
        acoef = c(ND * NST)
        c = Carve(work)
        crow = [c(T) for _ in range(2)]
        dtl = c(T)
        c2 = Carve(weights, EARLY * W13E + 16 * P)
        c2.at = EARLY * W13E + 16 * P + T // 2 + 3 * ND * T
        xpad = c2(ND * B * PADL).rearrange("p (d b l) -> p d b l", d=ND, b=B)
        conv = c2(ND * T).rearrange("p (d t) -> p d t", d=ND)
        c3 = Carve(weights, EARLY * W13E + 16 * P + T // 2 + 3 * ND * T)
        sp_abs, sp_exp, sp_relu, *sp_squares = (c3(ND * T).rearrange("p (d t) -> p d t", d=ND) for _ in range(5))
        sp_squares += [sp_abs, Carve(work, 4 * T)(ND * T).rearrange("p (d t) -> p d t", d=ND)]
        c3b = Carve(work, 3 * T)
        rem = c3b(T)

        in_x, in_mix, in_misc, in_con, in_late, in_ffnw, out_done, zeroed = map(
            sem, ("in_x", "in_mix", "in_misc", "in_con", "in_late", "in_ffnw", "out_done", "zeroed"))
        in_w13, in_w13_next, in_w2, w_scaled, w_hi, w_lo_dve, w_lo_pool, w_placed, row_low = map(
            sem, ("in_w13", "in_w13_next", "in_w2", "w_scaled", "w_hi", "w_lo_dve", "w_lo_pool", "w_placed", "row_low"))
        in_ffn2 = sem("in_ffn2")
        ln_stats, ln_mv, ln_sd, ln_out, ln_chain = map(sem, ("ln_stats", "ln_mv", "ln_sd", "ln_out", "ln_chain"))
        dve_step, act_step = sem("dve_step"), sem("act_step")
        zero_pad, proj_mm, proj_copied, conv_done, u_done = map(
            sem, ("zero_pad", "proj_mm", "proj_copied", "conv_done", "u_done"))
        xproj_mm, bc_top, dtl_copied, dt_mm, sp_parts, bc_split, dt_ready, a_ready = map(
            sem, ("xproj_mm", "bc_top", "dtl_copied", "dt_mm", "sp_parts", "bc_split", "dt_ready", "a_ready"))
        b_mm, c_mm, c_copied, decay_done, drive_done, scan_done, prod_done, y_mm = map(
            sem, ("b_mm", "c_mm", "c_copied", "decay_done", "drive_done", "scan_done", "prod_done", "y_mm"))
        gate_done, gated, yt_mm, mixed = map(sem, ("gate_done", "gated", "yt_mm", "mixed"))
        xnt_mm, xnt_copied, logit_mm, picked, rank_mm, slots_ready, scattered = map(
            sem, ("xnt_mm", "xnt_copied", "logit_mm", "picked", "rank_mm", "slots_ready", "scattered"))
        wt_mm, wt_copied, wquant = map(sem, ("wt_mm", "wt_copied", "wquant"))
        row_in = [sem(f"row_in{i}") for i in range(2)]
        row_out = [sem(f"row_out{i}") for i in range(2)]
        row_mm, rowt_copied, up_mm, silu_done, h_done, ht_mm, ht_copied, down_mm, down_copied = map(
            sem, ("row_mm", "rowt_copied", "up_mm", "silu_done", "h_done", "ht_mm", "ht_copied", "down_mm",
                  "down_copied"))
        gathered = [sem(f"gathered{i}") for i in range(4)]
        combined = sem("combined")
        stack_zero, v_copied, roped, cast_hi, stacked, q_mm, rope_tab, sin_done = map(
            sem, ("stack_zero", "v_copied", "roped", "cast_hi", "stacked", "q_mm", "rope_tab", "sin_done"))
        k_mm, v_mm, k_saved, v_saved, k_roped, rope_step, sin_signed, stack_ones = map(
            sem, ("k_mm", "v_mm", "k_saved", "v_saved", "k_roped", "rope_step", "sin_signed", "stack_ones"))
        q_raw, pq_step, stacked_late, vst_zero = map(sem, ("q_raw", "pq_step", "stacked_late", "vst_zero"))
        masked = sem("masked")
        sp_exped, sp_squared = sem("sp_exped"), sem("sp_squared")
        bout_added, bias_step, bias_split, f_rounded, fy_done, f2_rounded = map(
            sem, ("bout_added", "bias_step", "bias_split", "f_rounded", "fy_done", "f2_rounded"))
        t1_mm, t1_copied, mx_mm, mx_done, shift_done, t2_mm, t2_copied, s_mm, exp_done, v_unit = map(
            sem, ("t1_mm", "t1_copied", "mx_mm", "mx_done", "shift_done", "t2_mm", "t2_copied", "s_mm", "exp_done",
                  "v_unit"))
        pv_mm, o_copied, ot_mm, o_norm, at_mm, at_copied, wo_mm, attn_done = map(
            sem, ("pv_mm", "o_copied", "ot_mm", "o_norm", "at_mm", "at_copied", "wo_mm", "attn_done"))
        o_rec, shift_hi, fq_chain, f2_chain, hq_ready = map(
            sem, ("o_rec", "shift_hi", "fq_chain", "f2_chain", "hq_ready"))
        hq_mm, hq_copied, f1_mm, gelu_done, fq_done, ft_mm, ft_copied, f2_mm, f2_done = map(
            sem, ("hq_mm", "hq_copied", "f1_mm", "gelu_done", "fq_done", "ft_mm", "ft_copied", "f2_mm",
                  "f2_done"))

        c = Carve(work)
        rt = [c(NT * E) for _ in range(12)]
        rt_lut = c(NT * LUTN)
        mask16 = c(NT * E, F16)
        small = [c(NT) for _ in range(6)]
        cum = c(4 * E)
        texp = c((SLOT_TILES + 1) * E)
        xnt_at = c.at
        xnt = c(2 * T).rearrange("p (k t) -> p k t", k=2)
        fwq = c(2 * T, BF16)
        fw_scr = [c(64) for _ in range(4)]
        c = Carve(work, xnt_at)
        xg = [c(H) for _ in range(2)]
        xgt = [[c(2 * P, F16) for _ in range(2)] for _ in range(2)]
        silu_h = [c(I) for _ in range(2)]
        hbuf = [c(I) for _ in range(2)]
        vraw = c(NT * H).rearrange("p (t h) -> p t h", t=NT)
        c = Carve(work)
        ht = [c(KI * P).rearrange("p (j s) -> p j s", j=KI) for _ in range(2)]
        yrow = [c(H) for _ in range(2)]
        assert c.at <= xnt_at
        W2_LATE = 5
        fw_raw = [weights[:, E * W13E + W2_LATE * W2E + m * 2048:E * W13E + W2_LATE * W2E + (m + 1) * 2048]
                  for m in range(2)]
        split_at = work.shape[1] - 5 * SPLIT // 2
        c = Carve(work, split_at)
        rounded = [c(SPLIT, F16) for _ in range(5)]
        SPLIT_POOL = range(5, 16)
        SPLIT_DVE = [i for i in range(NSPLIT) if i not in SPLIT_POOL]
        PRE_FROM, PRE_EARLY, PRE_TO = SPLIT_POOL[0] * SPLIT, EARLY * W13E, (SPLIT_POOL[-1] + 1) * SPLIT
        PRE = (PRE_EARLY - PRE_FROM) // NST
        assert PRE * NST == PRE_EARLY - PRE_FROM and PRE_TO <= (EARLY + 1) * W13E

        c = Carve(weights)
        gat = [[c(H) for _ in range(2)] for _ in range(4)]
        late_s = c(LATE_N)
        late_end = c.at
        qst = c(UNITS * 2 * P, F16).rearrange("p (u t r) -> p u t r", u=UNITS, t=2)
        kst = c(UNITS * 2 * P, F16).rearrange("p (u t r) -> p u t r", u=UNITS, t=2)
        vst = c(UNITS * 2 * P).rearrange("p (u t r) -> p u t r", u=UNITS, t=2)
        rope_b = c(NT * H)
        orec = [c(4 * 2 * HPU) for _ in range(2)]
        rope_at = c.at
        rope_a = c(NT * H)
        xnt3 = c(2 * T).rearrange("p (k t) -> p k t", k=2)
        c = Carve(weights, rope_at)
        ost = c(UNITS * L).rearrange("p (u q) -> p u q", u=UNITS)
        bias_parts = c(F + H, BF16)
        bias_rem = c(F + H)
        thirty_second = c(P, BF16)
        c = Carve(work)
        qkt = [c(4 * P, F16) for _ in range(4)]
        q2t = [c(2 * P, F16) for _ in range(2)]
        kmask = [c(HPU * L, F16).rearrange("p (j k) -> p j k", j=HPU) for _ in range(4)]
        pexp = [c(HPU * 2 * L) for _ in range(2)]
        vu = [c(2 * P).rearrange("p (t r) -> p t r", t=2) for _ in range(2)]
        mx = [c(2 * HPU) for _ in range(2)]
        attn = rope_b.rearrange("p (t u r) -> p t u r", t=2, u=UNITS)
        attnt = xnt3
        c = Carve(weights, late_end)
        xb = c(NT * H, BF16).rearrange("p (t h) -> p t h", t=NT)
        hn = c(NT * H)
        hb = c(NT * H, BF16)
        hqb = c(NT * H, BF16)
        hqt = c(2 * T, BF16).rearrange("p (k t) -> p k t", k=2)
        qs = [c(NT * H // BLK) for _ in range(4)]
        f1 = [c(F, BF16) for _ in range(2)]
        g1 = [c(F, BF16) for _ in range(2)]
        gy = [c(F, BF16) for _ in range(2)]
        gq = [c(F, BF16) for _ in range(2)]
        gqt = [c(F, BF16).rearrange("p (k t) -> p k t", k=F // P) for _ in range(2)]
        fs = [[c(F // BLK) for _ in range(4)] for _ in range(2)]
        f2 = [c(H, BF16) for _ in range(2)]
        r4 = [c(H, BF16) for _ in range(2)]

        bank16 = [ps[:, b, :].bitcast(F16) for b in range(8)]
        bankb = [ps[:, b, :].bitcast(BF16) for b in range(8)]
        block = ctx.enter_context(nc.Block())
        QN = 2
        VB, KB = (6, 7, 0, 3), (1, 2, 4, 5)

        QD = 2

        def of_units(st, t):
            return st.rearrange("p (b g) t (j r) -> p b g t j r", b=B, r=HS)[:, t // 2, :, t % 2]

        @block.sync
        def _(sp):
            sp.dma_start(ctxt[:], ctx_t).then_inc(in_mix, 16)
            sp.dma_start(mixp[:], mix).then_inc(in_mix, 16)
            sp.dma_start(dtp[96:96 + DTR, :], dt_proj).then_inc(in_mix, 16)
            sp.dma_start(xa[:], x.rearrange("(t p) h -> p t h", p=P)).then_inc(in_x, 16)
            sp.dma_start(sel, bc_select).then_inc(in_misc, 16)
            sp.dma_start(cons[:], con).then_inc(in_con, 16)
            sp.dma_start(cons16[:], con16).then_inc(in_con, 16)
            sp.dma_start(identb[:], ident_b).then_inc(in_con, 16)
            sp.dma_start(routep[:], route).then_inc(in_con, 16)
            if upto >= 2:
                def load_w13(e, loaded=in_w13):
                    sp.dma_start(w13s[:, e].rearrange("p m k n -> p (m k n)"), w13[e]).then_inc(loaded, 16)

                def load_w2(e):
                    sp.dma_start(w2s[:, e].rearrange("p j n -> p (j n)"), w2[e]).then_inc(in_w2, 16)

                for e in range(EARLY):
                    load_w13(e)
                sp.wait_ge(zero_pad, 3)
                sp.dma_start(routed.rearrange("(i p) h -> p i h", p=P),
                             zrow[:].unsqueeze(1).broadcast_to([P, SLOT_TILES, H])).then_inc(zeroed, 16)
                sp.wait_ge(mixed, B)
                sp.dma_start(fw_raw[0], ffn_w1).then_inc(in_ffnw, 16)
                load_w13(EARLY, in_w13_next)
                sp.dma_start(fw_raw[1], ffn_w2).then_inc(in_ffn2, 16)
                for e in range(EARLY + 1, E):
                    load_w13(e)
                for e in range(W2_LATE):
                    load_w2(e)
                sp.wait_ge(wquant, QN)
                for e in range(W2_LATE, E):
                    load_w2(e)

                sp.wait_ge(scattered, 32 * NT)

                def load_rows(i, b):
                    need(sp, row_mm, i - 1)
                    sp.dma_start(xg[b], routed[bass.ds(i * P, P), :]).then_inc(row_in[b], 16)

                def store_rows(i, b):
                    sp.wait_ge(down_copied, i + 1)
                    sp.dma_start(expert_out[bass.ds(i * P, P), :], yrow[b]).then_inc(row_out[b], 16)

                skewed(sp, SLOT_TILES, [(0, load_rows), (3, store_rows)])
            if upto >= 3:
                sp.wait_ge(down_mm, SLOT_TILES)
                sp.dma_start(late_s, late).then_inc(in_late, 16)
            if upto < 4:
                sp.wait_ge([None, mixed, combined, attn_done][upto], [None, B, NT, NT][upto])
                sp.dma_start(out.rearrange("(t p) h -> p t h", p=P), xa[:]).then_inc(out_done, 16)
                sp.wait_ge(out_done, 16)
            else:
                with sp.Fori(0, NT) as t:
                    sp.wait_ge(f2_done, t + 1)
                    sp.dma_start(out[bass.ds(t * P, P), :], xa[:, bass.ds(t, 1), :].rearrange("p a h -> p (a h)")) \
                      .then_inc(out_done, 16)
                sp.wait_ge(out_done, 16 * NT)

        @block.gpsimd
        def _(pool):
            nc.gpsimd.memset(xpad[:, :, :, 0:TAPS - 1], 0.0).then_inc(zero_pad, 1)
            nc.gpsimd.memset(bcst, 0.0).then_inc(zero_pad, 1)
            nc.gpsimd.memset(zrow[:], 0.0).then_inc(zero_pad, 1)

            def times_c(n, b):
                pool.wait_ge(c_copied, n + 1)
                for d in range(ND):
                    pool.wait_ge(scan_done, n * ND + (d + 1))
                    nc.gpsimd.tensor_tensor(state[b][d], state[b][d], crow[b], ALU.mult).then_inc(prod_done, 1)

            skewed(pool, NST, [(0, times_c)])
            if upto < 2:
                return
            for i in SPLIT_POOL:
                pool.wait_ge(w_hi, i + 1)
                nc.gpsimd.tensor_tensor(chunks_h[:, i, :, 1], chunks[:, i, :], rounded[i % 5], ALU.subtract) \
                  .then_inc(w_lo_pool, 1)
            pool.wait_ge(zeroed, 16)
            pool.wait_ge(slots_ready, 1)
            pool.wait_ge(ln_out, 2 * NT)
            for t in range(NT):
                for s in range(2):
                    pool.indirect_dma_start(
                        routed, bass.IndirectOffsetOnAxis(ap=slots_i[:, s, t:t + 1].bitcast(U32), axis=0),
                        xn[:, t, :], None).then_inc(scattered, 16)
            steps = [0]

            def rope_link(ins):
                steps[0] += 1
                ins.then_inc(rope_step, 1)
                pool.wait_ge(rope_step, steps[0])

            pool.wait_ge(k_saved, NT // 2)
            pool.wait_ge(sin_signed, 1)
            for t in range(NT):
                k = xn[:, t, :].rearrange("p (h r) -> p h r", r=HD)
                a = rope_s[:].rearrange("p (h r) -> p h r", r=HD)
                b = zrow[:].rearrange("p (h r) -> p h r", r=HD)
                cs = ang[:, 64 + t * 8:72 + t * 8].unsqueeze(1).broadcast_to([P, NHEAD, HD])
                sn = sin8[:, t * 8:t * 8 + 8].unsqueeze(1).broadcast_to([P, NHEAD, HD])
                rope_link(nc.gpsimd.tensor_tensor(a, k, cs, ALU.mult))
                rope_link(nc.gpsimd.tensor_tensor(b[:, :, 0::2], k[:, :, 1::2], sn[:, :, 0::2], ALU.mult))
                rope_link(nc.gpsimd.tensor_tensor(b[:, :, 1::2], k[:, :, 0::2], sn[:, :, 1::2], ALU.mult))
                ins = nc.gpsimd.tensor_tensor(k, a, b, ALU.add)
                ins.then_inc(k_roped, 1)
                pool.wait_ge(k_roped, t + 1)
            for b in range(2):
                pool.wait_ge(row_out[b], 16 * ((SLOT_TILES + 1 - b) // 2))
            pool.wait_ge(down_mm, SLOT_TILES)
            for t in range(NT):
                need(pool, combined, t - 3)
                for s in range(2):
                    pool.indirect_dma_start(
                        gat[t % 4][s], None, expert_out,
                        bass.IndirectOffsetOnAxis(ap=slots_i[:, s, t:t + 1].bitcast(U32), axis=0),
                        ).then_inc(gathered[t % 4], 16)
            if upto < 3:
                return
            nc.gpsimd.memset(qst.rearrange("p u t r -> p (u t r)").bitcast(U32), 0).then_inc(stack_zero, 1)
            for b in range(4):
                nc.gpsimd.memset(kmask[b].rearrange("p j k -> p (j k)").bitcast(U32), 0).then_inc(stack_zero, 1)
            pool.wait_ge(vst_zero, 1)
            nc.gpsimd.memset(vst.rearrange("p u t (j r) -> p (u t j) r", r=HS)[:, :, 8:9], 1.0) \
              .then_inc(stack_zero, 1)
            pool.wait_ge(stack_zero, 6)
            def stack_q(t):
                pool.wait_ge(q_raw, (t - QD) // 2 + 1)
                q = rope_a[:, t * H:(t + 1) * H].rearrange("p (h r) -> p h r", r=HD)
                a = rope_s[:].rearrange("p (h r) -> p h r", r=HD)
                b = rope_b[:, t * H:(t + 1) * H].rearrange("p (h r) -> p h r", r=HD)
                cs = ang[:, 64 + t * 8:72 + t * 8].unsqueeze(1).broadcast_to([P, NHEAD, HD])
                sn = sin8[:, t * 8:t * 8 + 8].unsqueeze(1).broadcast_to([P, NHEAD, HD])
                nc.gpsimd.tensor_tensor(a, q, cs, ALU.mult).then_inc(pq_step, 1)
                nc.gpsimd.tensor_tensor(b[:, :, 0::2], q[:, :, 1::2], sn[:, :, 0::2], ALU.mult).then_inc(pq_step, 1)
                nc.gpsimd.tensor_tensor(b[:, :, 1::2], q[:, :, 0::2], sn[:, :, 1::2], ALU.mult).then_inc(pq_step, 1)
                pool.wait_ge(pq_step, 6 * (t - QD) + 3)
                nc.gpsimd.tensor_tensor(q, a, b, ALU.add).then_inc(pq_step, 1)
                pool.wait_ge(pq_step, 6 * (t - QD) + 4)
                dst = of_units(qst, t)
                q = rope_a[:, t * H:(t + 1) * H].rearrange("p (g j r) -> p g j r", g=8, r=HD)
                nc.gpsimd.tensor_copy(dst[:, :, :, 0:8], q).then_inc(pq_step, 1)
                nc.gpsimd.tensor_copy(dst[:, :, :, 16:24], q).then_inc(pq_step, 1)
                pool.wait_ge(pq_step, 6 * (t - QD) + 6)
                nc.gpsimd.tensor_tensor(dst[:, :, :, 8:16], q, dst[:, :, :, 0:8], ALU.subtract) \
                  .then_inc(stacked_late, 1)

            for t in range(QD, NT - 3):
                stack_q(t)
            pool.wait_ge(stacked_late, NT - 3 - QD)
            pool.wait_ge(v_copied, NT)

            def copy_v(n, b):
                need(pool, pv_mm, n - 1)
                nc.gpsimd.tensor_copy(vu[b % 2], vst[:, bass.ds(n, 1)].rearrange("p a t r -> p (a t) r")) \
                  .then_inc(v_unit, 1)
                if isinstance(n, int) and n in (1, 3, 5):
                    t = NT - 3 + n // 2
                    stack_q(t)
                    pool.wait_ge(stacked_late, t + 1 - QD)

            skewed(pool, UNITS, [(0, copy_v)], turn=6)
            pool.wait_ge(ln_out, 3 * NT)
            nc.gpsimd.tensor_tensor(xa[:], xa[:], col(LATE, late_s, "bout").unsqueeze(1).broadcast_to([P, NT, H]),
                                    ALU.add).then_inc(bout_added, 1)
            if upto < 4:
                return
            biases = late_s[:, LATE["b1"][0]:LATE["b2"][1]]
            pool.wait_ge(bout_added, 1)
            bias_chain = [0]

            def bias_link(ins):
                bias_chain[0] += 1
                ins.then_inc(bias_step, 1)
                pool.wait_ge(bias_step, bias_chain[0])

            bias_link(nc.gpsimd.tensor_copy(bias_parts[0:96, :], biases[0:96, :]))
            bias_link(nc.gpsimd.tensor_tensor(bias_rem[0:64, :], biases[0:64, :], bias_parts[0:64, :], ALU.subtract))
            bias_link(nc.gpsimd.tensor_copy(bias_parts[0:64, :], bias_rem[0:64, :]))
            bias_link(nc.gpsimd.tensor_tensor(bias_parts[0:32, :], bias_rem[0:32, :], bias_parts[0:32, :],
                                              ALU.subtract))
            nc.gpsimd.memset(thirty_second, 1.0 / 32).then_inc(bias_split, 1)

            def scale_f(t, b):
                pool.wait_ge(fy_done, t + 1)
                need(pool, ft_mm, t - 1)
                nc.gpsimd.tensor_tensor(gq[b].rearrange("p (n k) -> p n k", k=BLK),
                                        gy[b].rearrange("p (n k) -> p n k", k=BLK),
                                        fs[b][3].unsqueeze(2).broadcast_to([P, F // BLK, BLK]), ALU.mult) \
                  .then_inc(fq_done, 1)

            def finish(t, b):
                pool.wait_ge(f2_rounded, t + 1)
                nc.gpsimd.tensor_tensor(r4[b], f2[b], xb[:, t, :], ALU.add).then_inc(f2_chain, 1)
                pool.wait_ge(f2_chain, t + 1)
                nc.gpsimd.tensor_tensor(xa[:, t, :], xa[:, t, :], r4[b], ALU.add).then_inc(f2_done, 1)

            skewed(pool, NT, [(1, scale_f), (3, finish)])

        @block.tensor
        def _(pe):
            mm = nc.tensor.matmul
            pe.wait_ge(in_mix, 48)
            for d in range(ND):
                for h in range(2):
                    last = mm(ps[:, 2 * d + h, :], col(MIX, mixp, "in_proj", d * P, (d + 1) * P),
                              ctxt[:, h * 512:(h + 1) * 512], start=True, stop=True)
                last.then_inc(proj_mm, 1)
            for d in range(ND):
                pe.wait_ge(u_done, d + 1)
                for h in range(2):
                    uh = u[:, d, h * 512:(h + 1) * 512]
                    last = mm(ps[0:96 + DTR, 4 + h, :], col(MIX, mixp, "x_proj", d * (96 + DTR), (d + 1) * (96 + DTR)),
                              uh, start=(d == 0), stop=(d == ND - 1))
            last.then_inc(xproj_mm, 1)
            pe.wait_ge(dtl_copied, 1)
            for d in range(ND):
                for h in range(2):
                    last = mm(ps[:, 2 * d + h, :], dtp[96:96 + DTR, d * P:(d + 1) * P],
                              dtl[96:96 + DTR, h * 512:(h + 1) * 512], start=True, stop=True)
                last.then_inc(dt_mm, 1)
            pe.wait_ge(sp_parts, 2 * ND)
            pe.wait_ge(bc_split, 1)
            pe.wait_ge(in_misc, 16)
            pe.wait_ge(in_con, 64)

            def spread(n, b):
                need(pe, drive_done, 2 * n)
                lhs = sel[:, bass.ds(n * P, P)]
                for h in range(2):
                    last = mm(ps[:, h, :], lhs, bcst[:, h * 512:(h + 1) * 512], start=True, stop=True)
                last.then_inc(b_mm, 1)
                need(pe, c_copied, n)
                lhs = sel[:, bass.ds(n * P + NST * P, P)]
                for h in range(2):
                    last = mm(ps[:, 2 + h, :], lhs, bcst[:, h * 512:(h + 1) * 512], start=True, stop=True)
                last.then_inc(c_mm, 1)

            def add_y(n, b):
                for d in range(ND):
                    pe.wait_ge(prod_done, n * ND + (d + 1))
                    for h in range(2):
                        last = mm(ps[:, 4 + 2 * d + h, :], ident, state[b][d][:, h * 512:(h + 1) * 512],
                                  start=isinstance(n, int) and n == 0, stop=isinstance(n, int) and n == NST - 1)
                    last.then_inc(y_mm, 1)

            skewed(pe, NST, [(0, spread), (2, add_y)])
            pe.wait_ge(gated, ND)
            for b in range(B):
                for h in range(2):
                    for d in range(ND):
                        last = nc.tensor.transpose(ps[:, b, h * H + d * P:h * H + (d + 1) * P],
                                                   drive[d][:, b * L + h * P:b * L + (h + 1) * P], ident)
                last.then_inc(yt_mm, 1)
            if upto < 2:
                return

            def transpose_normed(dst_banks, seen, halves=(0, 1)):
                for half in halves:
                    pe.wait_ge(ln_out, seen - (NT // 2 if half == 0 else 0))
                    for k in range(2):
                        for t in range(4):
                            last = nc.tensor.transpose(ps[:, dst_banks + 2 * k + half, t * P:(t + 1) * P],
                                                       xn[:, half * 4 + t, k * P:(k + 1) * P], ident)
                        last.then_inc(xnt_mm, 1)

            pe.wait_ge(mixed, B)
            transpose_normed(4, 2 * NT)
            for t in range(NT):
                pe.wait_ge(xnt_copied, 2 + t // 4 * 2)
                for k in range(2):
                    last = mm(ps[:, 0, t * E:(t + 1) * E], xnt[:, k, t * P:(t + 1) * P],
                              col(ROUTE, routep, "w_gate", k * E, (k + 1) * E),
                              start=(t == 0 and k == 0), stop=(t == NT - 1 and k == 1), skip_group_check=True)
            last.then_inc(logit_mm, 1)
            pe.wait_ge(picked, 1)
            mm(ps[:, 1, 0:NT * E], before16, mask16, start=True, stop=False, skip_group_check=True)
            for t in range(NT - 1):
                after = NT - 1 - t
                mm(ps[:, 1, (t + 1) * E:NT * E], ones16,
                   mask16[:, t * E:(t + 1) * E].unsqueeze(1).broadcast_to([P, after, E]),
                   start=False, stop=(t == NT - 2), skip_group_check=True)
            for t in range(NT):
                last = mm(ps[:, 2, 0:E], ones16, mask16[:, t * E:(t + 1) * E], start=(t == 0), stop=(t == NT - 1))
            last.then_inc(rank_mm, 1)
            def turn_weights(m):
                pe.wait_ge(wquant, m + 1)
                need(pe, wt_copied, 2 * m)
                for q in range(2):
                    for t in range(8):
                        src = fwq[:, t * H + q * P:t * H + (q + 1) * P] if m == 0 else \
                            fwq[:, q * F + t * P:q * F + (t + 1) * P]
                        last = nc.tensor.transpose(bankb[4 + q][:, t * P:(t + 1) * P], src, identb[:])
                    last.then_inc(wt_mm, 1)

            def project_ctx(g, bank, first, done):
                for t in range(2 * g, 2 * g + 2):
                    last = mm(ps[:, bank, (t % 2) * H:(t % 2 + 1) * H], ctxt[:, t * P:(t + 1) * P],
                              col(ROUTE, routep, "wkv", first, first + H), start=True, stop=True)
                last.then_inc(done, 1)

            turn_weights(0)
            for g in range(NT // 2):
                project_ctx(g, VB[g], H, v_mm)
            pe.wait_ge(slots_ready, 1)
            project_ctx(0, KB[0], 0, k_mm)
            project_ctx(1, KB[1], 0, k_mm)
            turn_weights(1)
            pe.wait_ge(wt_copied, 2 * QN)
            project_ctx(2, KB[2], 0, k_mm)
            project_ctx(3, KB[3], 0, k_mm)
            pe.wait_ge(k_saved, NT // 2)
            pe.wait_ge(w_placed, NSPLIT)
            pe.wait_ge(in_w2, 16 * E)

            def expert_of(i):
                return pe.value_load(tile_expert[0:1, bass.ds(i, 1)], min_val=0, max_val=E - 1)

            def turn_rows(i, b):
                pe.wait_ge(row_in[b], (i // 2) * 16 + 16 if isinstance(i, int) else (i - b) * 8 + 16)
                need(pe, row_low, i)
                for k in range(2):
                    last = nc.tensor.transpose(ps[:, 6, k * P:(k + 1) * P], xg[b][:, k * P:(k + 1) * P], ident)
                last.then_inc(row_mm, 1)

            def up(i, b):
                e = expert_of(i)
                pe.wait_ge(row_low, i + 1)
                need(pe, h_done, i)
                parts = ((0, 0), (0, 1), (1, 0))
                for m in range(2):
                    for k in range(2):
                        for n, (px, pw) in enumerate(parts):
                            for h in range(2):
                                last = mm(ps[:, 2 * m + h, 0:IC], xgt[b][px][:, k * P:(k + 1) * P],
                                          w13h[:, bass.ds(e, 1), m, k, h * IC:(h + 1) * IC, pw]
                                          .rearrange("p a n -> p (a n)"), start=(k == 0 and n == 0),
                                          stop=(k == 1 and n == len(parts) - 1))
                    last.then_inc(up_mm, 1)

            def turn_h(i, b):
                pe.wait_ge(h_done, i + 1)
                need(pe, ht_copied, 2 * i)
                for j in range(KI):
                    w = min(P, I - j * P)
                    last = nc.tensor.transpose(ps[0:w, 4 + j // 3, (j % 3) * P:(j % 3 + 1) * P],
                                               hbuf[b][:, j * P:j * P + w], ident)
                    if j % 3 == 2:
                        last.then_inc(ht_mm, 1)

            def down(i, b):
                e = expert_of(i)
                pe.wait_ge(ht_copied, 2 * i + 2)
                need(pe, down_copied, i)
                for j in range(KI):
                    w = min(P, I - j * P)
                    last = mm(ps[:, 7, 0:H], ht[b][0:w, j, :],
                              w2s[0:w, bass.ds(e, 1), j, :].rearrange("p a n -> p (a n)"),
                              start=(j == 0), stop=(j == KI - 1))
                last.then_inc(down_mm, 1)

            skewed(pe, SLOT_TILES, [(2, turn_h), (0, turn_rows), (1, up), (2, down)])
            if upto < 3:
                return

            pe.wait_ge(in_late, 16)
            pe.wait_ge(down_copied, SLOT_TILES)
            def project_q(g):
                pe.wait_ge(xnt_copied, 6 + g // 2 * 2)
                for t in range(2 * g, 2 * g + 2):
                    for k in range(2):
                        last = mm(ps[:, 4 + g, (t % 2) * H:(t % 2 + 1) * H], xnt3[:, k, t * P:(t + 1) * P],
                                  col(LATE, late_s, "wq", k * H, (k + 1) * H), start=(k == 0), stop=(k == 1))
                last.then_inc(q_mm, 1)

            transpose_normed(0, 3 * NT, (0,))
            project_q(0)
            transpose_normed(0, 3 * NT, (1,))
            for g in range(1, NT // 2):
                project_q(g)
            pe.wait_ge(stacked, NT + QD)
            pe.wait_ge(q_raw, (NT - QD) // 2)
            pe.wait_ge(stack_ones, 1)

            def turn_qk(n, b):
                need(pe, t2_copied, n - 2)
                need(pe, t1_copied, n)
                for a, st in enumerate((qst, kst)):
                    for t in range(2):
                        last = mm(ps[:, 6, (2 * a + t) * P:(2 * a + t + 1) * P],
                                  st[:, bass.ds(n, 1), t, :].rearrange("p a r -> p (a r)"), ident16,
                                  start=(a + t == 0), stop=(a + t == 3), skip_group_check=True)
                last.then_inc(t1_mm, 1)

            def row_scores(n, b, half):
                pe.wait_ge(t1_copied, n + 1)
                pe.wait_ge(masked, HPU * n + 2 * half + 2)
                need(pe, mx_done, 2 * n + half - 1)
                for t in range(2):
                    last = mm(ps[:, 2 * half + t, :], qkt[b][:, t * P:(t + 1) * P],
                              kmask[b][:, 2 * half:2 * half + 2, :].rearrange("p j k -> p (j k)"),
                              start=True, stop=True)
                last.then_inc(mx_mm, 1)

            def turn_q(n, b):
                pe.wait_ge(shift_done, n + 1)
                pe.wait_ge(t1_copied, n + 3 if not isinstance(n, int) else min(n + 3, UNITS))
                need(pe, t2_copied, n)
                for t in range(2):
                    last = mm(ps[:, 6, t * P:(t + 1) * P], qst[:, bass.ds(n, 1), t, :].rearrange("p a r -> p (a r)"),
                              ident16, start=(t == 0), stop=(t == 1), skip_group_check=True)
                last.then_inc(t2_mm, 1)

            def key_scores(n, b, heads):
                pe.wait_ge(t2_copied, n + 1)
                for j in heads:
                    need(pe, exp_done, HPU * n + (j - 1))
                    for t in range(2):
                        last = mm(ps[:, 4 + j % 2, t * L:(t + 1) * L], kmask[b][:, j, t * P:(t + 1) * P],
                                  q2t[b % 2], start=(t == 0), stop=(t == 1), skip_group_check=True)
                    last.then_inc(s_mm, 1)

            def weigh_v(n, b):
                pe.wait_ge(exp_done, HPU * n + HPU)
                pe.wait_ge(v_unit, n + 1)
                need(pe, o_copied, n)
                for t in range(2):
                    for j in range(HPU):
                        last = mm(ps[j * HS:(j + 1) * HS, 7, 0:L], vu[b % 2][:, t, j * HS:(j + 1) * HS],
                                  pexp[b % 2][:, (j * 2 + t) * L:(j * 2 + t + 1) * L], start=(t == 0), stop=(t == 1),
                                  skip_group_check=True)
                last.then_inc(pv_mm, 1)

            skewed(pe, UNITS, [(3, turn_q), (2, partial(row_scores, half=1)), (3, partial(key_scores, heads=(0, 1))),
                               (0, turn_qk), (3, partial(key_scores, heads=(2,))),
                               (1, partial(row_scores, half=0)), (3, partial(key_scores, heads=(3,))),
                               (4, weigh_v)], turn=4)
            pe.wait_ge(o_copied, UNITS)
            pe.wait_ge(mx_done, 2 * UNITS)

            def turn_o(g, k):
                need(pe, o_norm, 2 * g + k - 1)
                for w in range(4):
                    for t in range(2):
                        last = nc.tensor.transpose(ps[:, 2 * k + w // 2, (w % 2 * 2 + t) * P:(w % 2 * 2 + t + 1) * P],
                                                   ost[:, g * 8 + 4 * k + w, t * P:(t + 1) * P], ident)
                last.then_inc(ot_mm, 1)

            def turn_attn(g):
                pe.wait_ge(o_norm, 2 * g + 2)
                need(pe, at_copied, g - 1)
                for k in range(2):
                    for t in range(2):
                        last = nc.tensor.transpose(
                            ps[:, 4 + g % 2, (2 * k + t) * P:(2 * k + t + 1) * P],
                            attn[:, t, g * 8 + 4 * k:g * 8 + 4 * k + 4, :].rearrange("p u r -> p (u r)"), ident)
                last.then_inc(at_mm, 1)

            def project(g):
                pe.wait_ge(at_copied, g + 1)
                need(pe, attn_done, 2 * (g - 1))
                for t in range(2):
                    for k in range(2):
                        last = mm(ps[:, 6 + g % 2, t * H:(t + 1) * H], attnt[:, k, (2 * g + t) * P:(2 * g + t + 1) * P],
                                  col(LATE, late_s, "wout", k * H, (k + 1) * H), start=(k == 0), stop=(k == 1))
                last.then_inc(wo_mm, 1)

            for g in range(B + 2):
                if g < B:
                    turn_o(g, 0)
                    turn_o(g, 1)
                if 0 <= g - 1 < B:
                    turn_attn(g - 1)
                if 0 <= g - 2:
                    project(g - 2)
            if upto < 4:
                return

            def turn_half(half):
                pe.wait_ge(hq_ready, half + 1)
                for k in range(2):
                    for t in range(4):
                        at = (4 * half + t) * H + k * P
                        last = nc.tensor.transpose(bankb[4 + 2 * half + k][:, t * P:(t + 1) * P], hqb[:, at:at + P],
                                                   identb[:])
                last.then_inc(hq_mm, 1)

            def bias(out, a, b):
                mm(out, thirty_second[0:96, :], bias_parts[0:96, a:b], start=True, stop=False)

            turn_half(0)
            pe.wait_ge(o_norm, 2 * B)
            pe.wait_ge(bias_split, 1)
            pe.wait_ge(hq_copied, 1)

            def widen(t, b):
                if isinstance(t, int) and t == 2:
                    turn_half(1)
                if isinstance(t, int) and t == 4:
                    pe.wait_ge(hq_copied, 2)
                need(pe, f_rounded, t - 1)
                for h in range(2):
                    bias(ps[:, 2 * b + h, :], h * 512, (h + 1) * 512)
                    for k in range(2):
                        last = mm(ps[:, 2 * b + h, :], hqt[:, k, bass.ds(t * P, P)], w1q[:, k, h * 512:(h + 1) * 512],
                                  start=False, stop=(k == 1))
                last.then_inc(f1_mm, 1)

            def turn_f(t, b):
                pe.wait_ge(fq_done, t + 1)
                if isinstance(t, int) and t < 2:
                    pe.wait_ge(hq_copied, 2)
                need(pe, ft_copied, t - 1)
                for j in range(F // P):
                    last = nc.tensor.transpose(bankb[4 + b][:, j * P:(j + 1) * P], gq[b][:, j * P:(j + 1) * P],
                                               identb[:])
                last.then_inc(ft_mm, 1)

            def narrow(t, b):
                pe.wait_ge(ft_copied, t + 1)
                need(pe, f2_rounded, t - 1)
                bias(ps[:, 6 + b, 0:H], F, F + H)
                for j in range(F // P):
                    last = mm(ps[:, 6 + b, 0:H], gqt[b][:, j, :], w2q[:, j, :], start=False, stop=(j == F // P - 1))
                last.then_inc(f2_mm, 1)

            skewed(pe, NT, [(0, widen), (3, narrow), (2, turn_f)])

        @block.scalar
        def _(act):
            A = nc.scalar.activation
            ln_tiles = [0]

            def deviation(first=0, last=NT):
                ln_tiles[0] += last - first
                act.wait_ge(ln_mv, ln_tiles[0])
                A(sd[:, first:last], mv[:, first:last, 1], ACT.Sqrt, bias=eps_t).then_inc(ln_sd, 1)

            eps_t = EPS
            deviation()
            for d in range(ND):
                act.wait_ge(proj_mm, d + 1)
                for h in range(2):
                    A(xpad[:, d, 2 * h:2 * h + 2, TAPS - 1:], ps[:, 2 * d + h, :].rearrange("p (b l) -> p b l", b=2),
                      ACT.Copy).then_inc(proj_copied, 1)
            for d in range(ND):
                act.wait_ge(conv_done, d + 1)
                A(u[:, d, :], conv[:, d, :], ACT.Silu, bias=col(MIX, mixp, "conv_b", d, d + 1)).then_inc(u_done, 1)
            act.wait_ge(xproj_mm, 1)
            A(dtl[96:96 + DTR, :], ps[96:96 + DTR, 4:6, :], ACT.Copy).then_inc(dtl_copied, 1)
            act.wait_ge(zero_pad, 2)
            A(bcst[0:96, :], ps[0:96, 4:6, :], ACT.Copy).then_inc(bc_top, 1)
            A(acoef, col(MIX, mixp, "a_log"), ACT.Exp).then_inc(act_step, 1)
            act.wait_ge(act_step, 1)
            A(acoef, acoef, ACT.Copy, scale=-1.0).then_inc(a_ready, 1)
            for d in range(ND):
                act.wait_ge(dt_mm, d + 1)
                v = ps[:, 2 * d:2 * d + 2, :]
                bias = col(MIX, mixp, "dt_b", d, d + 1)
                A(sp_abs[:, d], v, ACT.Abs, bias=bias).then_inc(sp_parts, 1)
                A(sp_relu[:, d], v, ACT.Relu, bias=bias).then_inc(sp_parts, 1)
                act.wait_ge(sp_parts, 2 * d + 2)
                A(sp_exp[:, d], sp_abs[:, d], ACT.Exp, scale=-1.0).then_inc(sp_exped, 1)
                act.wait_ge(sp_exped, d + 1)
                for (a, _), sq in zip(LOG1P, sp_squares):
                    A(sq[:, d], sp_exp[:, d], ACT.Square, bias=a).then_inc(sp_squared, 1)
            act.wait_ge(a_ready, 1)

            def decays(n, b):
                for d in range(ND):
                    if isinstance(n, int) and n == 0:
                        act.wait_ge(dt_ready, d + 1)
                    need(act, scan_done, ND * (n - 2) + (d + 1) if not isinstance(n, int) or n >= 2 else 0)
                    A(decay[b][d], dts[:, d, :], ACT.Exp, scale=acoef[:, bass.ds(n + d * NST, 1)]) \
                        .then_inc(decay_done, 1)

            def copy_c(n, b):
                act.wait_ge(c_mm, n + 1)
                need(act, prod_done, ND * (n - 1))
                A(crow[b], ps[:, 2:4, :], ACT.Copy).then_inc(c_copied, 1)

            def prescale(n, b):
                if isinstance(n, int) and n == 0:
                    act.wait_ge(in_w13, 16 * EARLY)
                words = weights[:, bass.ds(n * PRE + PRE_FROM, PRE)]
                A(words, words, ACT.Copy, scale=WSCALE).then_inc(w_scaled, 1)

            skewed(act, NST, [(0, decays), (0, copy_c), (0, prescale)] if upto >= 2 else [(0, decays), (0, copy_c)])
            act.wait_ge(ln_out, NT)
            A(xn[:], xn[:], ACT.Silu).then_inc(gate_done, 1)
            if upto < 2:
                return

            def round_w(i):
                if (i + 1) * SPLIT <= (EARLY + 1) * W13E:
                    act.wait_ge(in_w13, 16 * EARLY)
                else:
                    act.wait_ge(in_w13, 16 * (E - 1))
                need(act, w_placed, i - 4)
                if i in SPLIT_POOL:
                    act.wait_ge(w_scaled, NST + int((i + 1) * SPLIT > PRE_EARLY))
                A(rounded[i % 5], chunks[:, i, :], ACT.Copy, scale=1.0 if i in SPLIT_POOL else WSCALE) \
                    .then_inc(w_hi, 1)

            def place_w(first, last):
                for i in range(first, last):
                    if i in SPLIT_DVE:
                        act.wait_ge(w_lo_dve, SPLIT_DVE.index(i) + 1)
                    else:
                        act.wait_ge(w_lo_pool, SPLIT_POOL.index(i) + 1)
                    A(chunks_h[:, i, :, 0], rounded[i % 5], ACT.Copy).then_inc(w_placed, 1)
                    if i + 5 < NSPLIT:
                        round_w(i + 5)

            for i in range(5):
                round_w(i)
            place_w(0, 7)

            def copy_normed(dst, bank, seen, steps=range(4)):
                for i in steps:
                    half, k = i // 2, i % 2
                    act.wait_ge(xnt_mm, seen + i + 1)
                    A(dst[:, k, half * 512:(half + 1) * 512], ps[:, bank + 2 * k + half, :], ACT.Copy) \
                        .then_inc(xnt_copied, 1)

            deviation()
            copy_normed(xnt, 4, 0)

            place_w(7, 8)
            act.wait_ge(in_w13_next, 16)
            A(weights[:, PRE_EARLY:PRE_TO], weights[:, PRE_EARLY:PRE_TO], ACT.Copy, scale=WSCALE) \
                .then_inc(w_scaled, 1)
            place_w(8, 12)
            for m, dst in enumerate((w1q, w2q)):
                for q in range(2):
                    act.wait_ge(wt_mm, 2 * m + q + 1)
                    if m == 0:
                        A(w1q[:, q, :], bankb[4 + q], ACT.Copy).then_inc(wt_copied, 1)
                    else:
                        A(w2q[:, :, q * P:(q + 1) * P], bankb[4 + q].rearrange("p (t r) -> p t r", r=P),
                          ACT.Copy).then_inc(wt_copied, 1)
                if m == 0:
                    place_w(12, SPLIT_POOL[-1] + 1)
            place_w(SPLIT_POOL[-1] + 1, NSPLIT)
            act.wait_ge(w_placed, NSPLIT)
            for g in range(NT // 2):
                act.wait_ge(v_mm, g + 1)
                A(vraw[:, 2 * g:2 * g + 2, :], ps[:, VB[g], :], ACT.Copy).then_inc(v_saved, 1)
            act.wait_ge(scattered, 32 * NT)
            for g in range(NT // 2):
                act.wait_ge(k_mm, g + 1)
                A(xn[:, 2 * g:2 * g + 2, :], ps[:, KB[g], :], ACT.Copy).then_inc(k_saved, 1)

            act.wait_ge(slots_ready, 1)
            act.wait_ge(logit_mm, 1)

            def copy_rows(i, b):
                act.wait_ge(row_mm, i + 1)
                need(act, up_mm, 2 * i - 2)
                A(xgt[b][0], ps[:, 6, 0:2 * P], ACT.Copy).then_inc(rowt_copied, 1)
                if isinstance(i, int) and i == 0:
                    act.wait_ge(rope_tab, 1)
                    A(ang[:], ang2[:], ACT.Sin).then_inc(sin_done, 1)

            def silus(i, b):
                act.wait_ge(up_mm, 2 * i + 1)
                need(act, h_done, i - 1)
                A(silu_h[b].rearrange("p (h n) -> p h n", h=2), ps[:, 0:2, 0:IC], ACT.Silu,
                  scale=1.0 / WSCALE).then_inc(silu_done, 1)

            def copy_ht(i, b):
                act.wait_ge(ht_mm, 2 * i + 1)
                need(act, down_mm, i - 1)
                A(ht[b][:, 0:3, :], ps[:, 4, 0:3 * P], ACT.Copy).then_inc(ht_copied, 1)
                act.wait_ge(ht_mm, 2 * i + 2)
                A(ht[b][:, 3:5, :], ps[:, 5, 0:2 * P], ACT.Copy)
                A(ht[b][0:I - 5 * P, 5, :], ps[0:I - 5 * P, 5, 2 * P:3 * P], ACT.Copy).then_inc(ht_copied, 1)

            skewed(act, SLOT_TILES, [(2, copy_ht), (0, copy_rows), (1, silus)])
            if upto < 3:
                return

            def cast_tile(st, src, second, t):
                dst = of_units(st, t)
                src = src.rearrange("p (g j r) -> p g j r", g=8, r=HD)
                A(dst[:, :, :, 0:8], src, ACT.Copy).then_inc(cast_hi, 1)
                A(dst[:, :, :, second:second + 8], src, ACT.Copy).then_inc(cast_hi, 1)

            act.wait_ge(down_mm, SLOT_TILES)
            A(vst.rearrange("p u t r -> p (u t) r"), ident.unsqueeze(1).broadcast_to([P, 2 * UNITS, P]), ACT.Copy,
              scale=0.0).then_inc(vst_zero, 1)
            act.wait_ge(stack_ones, 1)
            act.wait_ge(k_roped, NT)
            for t in range(NT):
                cast_tile(kst, xn[:, t, :], 8, t)

            def stack_v(first, last):
                for t in range(first, last):
                    A(of_units(vst, t)[:, :, :, 0:HD], vraw[:, t, :].rearrange("p (g j r) -> p g j r", g=8, r=HD),
                      ACT.Copy).then_inc(v_copied, 1)

            def save_q(g):
                act.wait_ge(q_mm, g + 1)
                A(rope_a[:, 2 * g * H:2 * (g + 1) * H], ps[:, 4 + g, :], ACT.Copy).then_inc(q_raw, 1)

            act.wait_ge(vst_zero, 1)
            act.wait_ge(v_saved, NT // 2)
            stack_v(0, NT)
            for half in range(2):
                deviation(half * NT // 2, (half + 1) * NT // 2)
                copy_normed(xnt3, 0, 4, (2 * half, 2 * half + 1))
            act.wait_ge(stack_zero, 1)
            for t in range(QD):
                act.wait_ge(roped, t + 1)
                cast_tile(qst, rope_a[:, t * H:(t + 1) * H], 16, t)
                if t == 0:
                    save_q(1)
            save_q(2)
            save_q(3)
            act.wait_ge(v_copied, NT)

            def copy_q2(n, b):
                act.wait_ge(t2_mm, n + 1)
                need(act, s_mm, HPU * (n - 1))
                A(q2t[b % 2], ps[:, 6, 0:2 * P], ACT.Copy).then_inc(t2_copied, 1)

            def exps(n, b, heads):
                need(act, pv_mm, n - 1)
                for j in heads:
                    act.wait_ge(s_mm, HPU * n + (j + 1))
                    A(pexp[b % 2][:, 2 * j * L:2 * (j + 1) * L], ps[:, 4 + j % 2, :], ACT.Exp,
                      scale=float(1.0 / np.sqrt(HD))).then_inc(exp_done, 1)

            def copy_qk(n, b):
                act.wait_ge(t1_mm, n + 1)
                if not isinstance(n, int) or n > 3:
                    act.wait_ge(mx_mm, 2 * (n - 3))
                    act.wait_ge(masked, HPU * (n - 3))
                A(qkt[b], ps[:, 6, :], ACT.Copy).then_inc(t1_copied, 1)

            def copy_o(n, b):
                act.wait_ge(pv_mm, n + 1)
                A(ost[:, bass.ds(n, 1), :].rearrange("p a q -> p (a q)"), ps[:, 7, 0:L], ACT.Copy).then_inc(o_copied, 1)

            skewed(act, UNITS, [(3, copy_q2), (5, copy_o), (3, partial(exps, heads=(0, 1))), (0, copy_qk),
                                (3, partial(exps, heads=(2, 3)))], turn=4)
            for g in range(B):
                act.wait_ge(at_mm, g + 1)
                A(attnt[:, :, g * L:(g + 1) * L], ps[:, 4 + g % 2, :].rearrange("p (k t) -> p k t", k=2), ACT.Copy) \
                    .then_inc(at_copied, 1)
            if upto < 4:
                return

            deviation(0, NT // 2)
            deviation(0, NT // 2)

            def copy_half(half):
                act.wait_ge(hq_mm, half + 1)
                for k in range(2):
                    last = A(hqt[:, k, half * 512:(half + 1) * 512], bankb[4 + 2 * half + k][:, 0:512], ACT.Copy)
                last.then_inc(hq_copied, 1)

            copy_half(0)
            deviation(NT // 2, NT)
            deviation(NT // 2, NT)

            def round_f(t, b):
                act.wait_ge(f1_mm, t + 1)
                need(act, gelu_done, t - 1)
                A(f1[b], ps[:, 2 * b:2 * b + 2, :], ACT.Copy).then_inc(f_rounded, 1)

            def gelus(t, b):
                act.wait_ge(f_rounded, t + 1)
                need(act, fy_done, t - 1)
                A(g1[b], f1[b], ACT.Gelu_apprx_tanh).then_inc(gelu_done, 1)
                if isinstance(t, int) and t == 1:
                    copy_half(1)

            def copy_f(t, b):
                act.wait_ge(ft_mm, t + 1)
                need(act, f2_mm, t - 1)
                A(gqt[b].rearrange("p k t -> p (k t)"), bankb[4 + b], ACT.Copy).then_inc(ft_copied, 1)

            def round_f2(t, b):
                act.wait_ge(f2_mm, t + 1)
                need(act, f2_done, t - 1)
                A(f2[b], ps[:, 6 + b, 0:H], ACT.Copy).then_inc(f2_rounded, 1)

            skewed(act, NT, [(0, round_f), (0, gelus), (2, copy_f), (3, round_f2)])

        @block.vector
        def _(dve):
            v = nc.vector
            chain = [0]

            def link(ins):
                chain[0] += 1
                ins.then_inc(ln_chain, 1)
                dve.wait_ge(ln_chain, chain[0])

            sums, rounds, outs = [0], [0], [0]

            def ln_sums(src, t):
                sums[0] += 1
                v.bn_stats(stats[:, t, :], src[:, t, :]).then_inc(ln_stats, 1)

            def ln_moments(tiles=range(NT)):
                rounds[0] += 1
                dve.wait_ge(ln_stats, sums[0])
                for t in tiles:
                    v.bn_aggr(mv[:, t, :], stats[:, t, :]).then_inc(ln_mv, 1)

            def ln_scale(tiles):
                dve.wait_ge(ln_sd, rounds[0])
                at = slice(tiles[0], tiles[-1] + 1)
                link(v.reciprocal(rs[:, at], sd[:, at]))

            def ln_apply(src, dst, tiles=range(NT), sums_too=False):
                ln_scale(tiles)
                for t in tiles:
                    outs[0] += 1
                    v.tensor_scalar(dst[:, t, :], src[:, t, :], mv[:, t, 0:1], rs[:, t:t + 1], ALU.subtract,
                                    ALU.mult).then_inc(ln_out, 1)
                if sums_too:
                    for i, t in enumerate(tiles):
                        dve.wait_ge(ln_out, outs[0] - len(tiles) + i + 1)
                        ln_sums(dst, t)

            def ln_apply_affine(src, between, dst, weight, bias, tiles):
                ln_scale(tiles)
                for t in tiles:
                    outs[0] += 1
                    v.scalar_tensor_tensor(out=between[:, t, :], in0=src[:, t, :], scalar=mv[:, t, 0:1],
                                           in1=weight, op0=ALU.subtract, op1=ALU.mult).then_inc(ln_out, 1)
                for i, t in enumerate(tiles):
                    dve.wait_ge(ln_out, outs[0] - len(tiles) + i + 1)
                    ins = v.scalar_tensor_tensor(out=dst[:, t, :], in0=between[:, t, :], scalar=rs[:, t:t + 1],
                                                 in1=bias, op0=ALU.mult, op1=ALU.add)
                link(ins)

            dve.wait_ge(in_x, 16)
            for t in range(NT):
                ln_sums(xa, t)
            ln_moments()
            dve.wait_ge(zero_pad, 1)
            for d in range(ND):
                dve.wait_ge(proj_copied, 2 * d + 2)
                acc = conv[:, d, :].rearrange("p (b l) -> p b l", b=B)
                w = [col(MIX, mixp, "conv_w", d * TAPS + k, d * TAPS + k + 1) for k in range(TAPS)]
                link(v.tensor_scalar(acc, xpad[:, d, :, 0:L], w[0], None, ALU.mult))
                for k in range(1, TAPS - 1):
                    link(v.scalar_tensor_tensor(out=acc, in0=xpad[:, d, :, k:k + L], scalar=w[k], in1=acc,
                                                op0=ALU.mult, op1=ALU.add))
                v.scalar_tensor_tensor(out=acc, in0=xpad[:, d, :, TAPS - 1:], scalar=w[TAPS - 1], in1=acc,
                                       op0=ALU.mult, op1=ALU.add).then_inc(conv_done, 1)
            ln_apply(xa, xn)
            dve.wait_ge(bc_top, 1)
            dve.wait_ge(zero_pad, 2)
            bc = ps[0:64, 4:6, :].rearrange("p a n -> p (a n)")
            link(v.tensor_tensor(rem[0:64, :], bc, bcst[0:64, :], ALU.subtract))
            link(v.tensor_copy(bcst[0:64, :], rem[0:64, :]))
            v.tensor_tensor(bcst[0:32, :], rem[0:32, :], bcst[0:32, :], ALU.subtract).then_inc(bc_split, 1)
            for d in range(ND):
                acc = sp_exp[:, d]
                for i, ((_, shift), sq) in enumerate(zip(LOG1P, sp_squares)):
                    dve.wait_ge(sp_squared, len(LOG1P) * d + (i + 1))
                    link(v.scalar_tensor_tensor(out=dts[:, d], in0=sq[:, d], scalar=shift, in1=acc, op0=ALU.add,
                                                op1=ALU.mult))
                    acc = dts[:, d]
                link(v.scalar_tensor_tensor(out=dts[:, d], in0=acc, scalar=LOG1P_SCALE, in1=sp_relu[:, d],
                                            op0=ALU.mult, op1=ALU.add))
                link(v.tensor_tensor(dtu[:, d], dts[:, d], u[:, d], ALU.mult))
                v.memset(dts[:, d].rearrange("p (b l) -> p b l", b=B)[:, :, 0:1], 1e25).then_inc(dt_ready, 1)

            def drives(n, b):
                dve.wait_ge(b_mm, n + 1)
                for d in range(ND):
                    if not isinstance(n, int) or n:
                        dve.wait_ge(scan_done, ND * (n - 1) + (d + 1))
                    v.tensor_tensor(drive[d], dtu[:, d, :], ps[:, 0:2, :].rearrange("p a n -> p (a n)"), ALU.mult) \
                        .then_inc(drive_done, 1)

            def scans(n, b):
                for d in range(ND):
                    need(dve, y_mm, ND * (n - 2) + (d + 1) if not isinstance(n, int) or n >= 2 else 0)
                    dve.wait_ge(drive_done, ND * n + (d + 1))
                    dve.wait_ge(decay_done, ND * n + (d + 1))
                    v.tensor_tensor_scan(state[b][d], decay[b][d], drive[d], 0.0, ALU.mult, ALU.add) \
                        .then_inc(scan_done, 1)

            skewed(dve, NST, [(0, drives), (0, scans)])

            def rests(chunk_numbers):
                for i in chunk_numbers:
                    dve.wait_ge(w_hi, i + 1)
                    v.scalar_tensor_tensor(out=chunks_h[:, i, :, 1], in0=chunks[:, i, :], scalar=WSCALE,
                                           in1=rounded[i % 5], op0=ALU.mult, op1=ALU.subtract).then_inc(w_lo_dve, 1)

            if upto >= 2:
                rests(SPLIT_DVE[:SPLIT_POOL[0]])
            dve.wait_ge(y_mm, ND * NST)
            dve.wait_ge(gate_done, 1)
            for d in range(ND):
                y = ps[:, 4 + 2 * d:6 + 2 * d, :].rearrange("p a n -> p (a n)")
                link(v.scalar_tensor_tensor(out=drive[d], in0=u[:, d, :], scalar=col(MIX, mixp, "skip", d, d + 1),
                                            in1=y, op0=ALU.mult, op1=ALU.add))
                yb = drive[d].rearrange("p (b l) -> p b l", b=B)
                v.tensor_tensor(yb, yb, xn[:].rearrange("p (b e) l -> p b e l", e=ND)[:, :, d, :], ALU.mult) \
                    .then_inc(gated, 1)
            for b in range(B):
                dve.wait_ge(yt_mm, b + 1)
                v.tensor_tensor(xa[:, 2 * b:2 * b + 2, :].rearrange("p a h -> p (a h)"),
                                xa[:, 2 * b:2 * b + 2, :].rearrange("p a h -> p (a h)"), ps[:, b, :], ALU.add) \
                    .then_inc(mixed, 1)
            if upto < 2:
                return

            dve.wait_ge(mixed, B)
            for t in range(NT):
                ln_sums(xa, t)
            ln_moments()
            ln_apply(xa, xn)

            def mx_scales(scr, amax_in):
                am, e2, inv, sc = scr
                link(v.tensor_reduce(am, amax_in, AX.X, ALU.max, apply_absolute_value=True))
                link(v.tensor_scalar(am, am, 2.0 ** -100, None, ALU.max))
                link(v.tensor_scalar(e2.bitcast(I32), am.bitcast(I32), 0x7F800000, None, ALU.bitwise_and))
                link(v.tensor_scalar(inv.bitcast(I32), e2.bitcast(I32), -1.0, float(0x7F000000 + (6 << 23)),
                                     ALU.mult, ALU.add))
                link(v.tensor_scalar(sc, e2, 1.0 / 64, None, ALU.mult))

            def mx_quant(dst, src, y, scr, nb):
                def blocks(a):
                    return a.rearrange("p (n k) -> p n k", k=BLK)

                mx_scales(scr, blocks(src))
                _, _, inv, sc = scr
                link(v.tensor_tensor(blocks(y), blocks(src), inv.unsqueeze(2).broadcast_to([P, nb, BLK]), ALU.mult))
                link(v.tensor_scalar(y, y, MAGIC, -MAGIC, ALU.add, ALU.add))
                return v.scalar_tensor_tensor(out=blocks(dst), in0=blocks(y), scalar=127.0,
                                              in1=sc.unsqueeze(2).broadcast_to([P, nb, BLK]), op0=ALU.min,
                                              op1=ALU.mult)

            def quant_weights(m):
                dve.wait_ge((in_ffnw, in_ffn2)[m], 16)
                if m:
                    dve.wait_ge(wt_mm, 2 * m)
                mx_quant(fwq, fw_raw[m], fw_raw[m], fw_scr, 64).then_inc(wquant, 1)

            quant_weights(0)
            dve.wait_ge(logit_mm, 1)
            li, sh, key, key2, oh1, oh2, pe_, tmp = rt[:8]

            def v3(a):
                return a.rearrange("p (t e) -> p t e", t=NT)

            def over(a):
                return a.unsqueeze(2).broadcast_to([P, NT, E])

            m_, k2_, ev, den, rec_, _ = small
            link(v.tensor_scalar(li, ps[:, 0, 0:NT * E], 128.0, MAGIC, ALU.mult, ALU.add))
            link(v.tensor_scalar(li, li, -MAGIC, None, ALU.add))
            link(v.tensor_reduce(m_, v3(li), AX.X, ALU.max))
            link(v.tensor_tensor(v3(sh), v3(li), over(m_), ALU.subtract))
            link(v.tensor_scalar(sh, sh, -128.0, None, ALU.max))
            link(v.scalar_tensor_tensor(out=key, in0=sh, scalar=float(E), in1=col(CON, cons, "expert_order"),
                                        op0=ALU.mult, op1=ALU.add))
            link(v.tensor_reduce(m_, v3(key), AX.X, ALU.max))
            link(v.tensor_tensor(v3(oh1), v3(key), over(m_), ALU.is_equal))
            link(v.scalar_tensor_tensor(out=key2, in0=oh1, scalar=-4096.0, in1=key, op0=ALU.mult, op1=ALU.add))
            link(v.tensor_reduce(m_, v3(key2), AX.X, ALU.max))
            link(v.tensor_tensor(v3(oh2), v3(key2), over(m_), ALU.is_equal))
            v.tensor_tensor(mask16, oh1, oh2, ALU.add).then_inc(picked, 1)
            link(v.tensor_tensor(tmp, oh2, sh, ALU.mult))
            link(v.tensor_reduce(k2_, v3(tmp), AX.X, ALU.add))
            lt = rt_lut.rearrange("p (t n) -> p t n", t=NT)
            link(v.tensor_tensor(lt, col(CON, cons, "lut_key").unsqueeze(1).broadcast_to([P, NT, LUTN]),
                                 k2_.unsqueeze(2).broadcast_to([P, NT, LUTN]), ALU.is_equal))
            link(v.tensor_tensor(lt, lt, col(CON, cons, "lut").unsqueeze(1).broadcast_to([P, NT, LUTN]), ALU.mult))
            link(v.tensor_reduce(ev, lt, AX.X, ALU.add))
            link(v.tensor_scalar(den, ev, 65536.0, None, ALU.add))
            link(v.reciprocal(rec_, den))
            link(v.tensor_scalar(gate_w[:, 0, :], rec_, 65536.0, None, ALU.mult))
            link(v.tensor_tensor(gate_w[:, 1, :], rec_, ev, ALU.mult))
            dve.wait_ge(rank_mm, 1)
            tiles, upto_, before = cum[:, 0:E], cum[:, E:2 * E], cum[:, 2 * E:3 * E]
            link(v.tensor_scalar(tiles, ps[:, 2, 0:E], 1.0 / P, (P - 1.0) / P - 0.5 + 0.5 / P, ALU.mult, ALU.add))
            link(v.tensor_scalar(tiles, tiles, MAGIC, -MAGIC, ALU.add, ALU.add))
            link(v.tensor_tensor_scan(upto_, col(CON, cons, "ones"), tiles, 0.0, ALU.mult, ALU.add))
            link(v.tensor_tensor(before, upto_, tiles, ALU.subtract))
            link(v.scalar_tensor_tensor(out=v3(pe_), in0=before.unsqueeze(1).broadcast_to([P, NT, E]),
                                        scalar=float(P), in1=v3(ps[:, 1, 0:NT * E]), op0=ALU.mult, op1=ALU.add))
            for s, oh in enumerate((oh1, oh2)):
                link(v.tensor_tensor(tmp, oh, pe_, ALU.mult))
                link(v.tensor_reduce(m_, v3(tmp), AX.X, ALU.add))
                link(v.tensor_copy(slots_i[:, s, :], m_))
            tx = texp.rearrange("p (i e) -> p i e", e=E)
            link(v.tensor_tensor(tx, col(CON, cons, "tile_index").unsqueeze(2).broadcast_to([P, SLOT_TILES + 1, E]),
                                 upto_.unsqueeze(1).broadcast_to([P, SLOT_TILES + 1, E]), ALU.is_ge))
            te = rt_lut[:, 0:SLOT_TILES + 1]
            link(v.tensor_reduce(te, tx, AX.X, ALU.add))
            v.tensor_scalar(tile_expert[:], te, float(E - 1), None, ALU.min).then_inc(slots_ready, 1)

            quant_weights(1)
            rests(SPLIT_DVE[SPLIT_POOL[0]:])
            link(v.tensor_tensor(ang[:, 0:64], col(ROUTE, routep, "pos"), col(CON, cons, "freq"), ALU.mult))
            link(v.tensor_scalar(ang[:, 64:128], ang[:, 0:64], float(np.pi / 2), None, ALU.add))
            link(v.tensor_scalar(ang2[:], ang[:], float(1 / (2 * np.pi)), MAGIC, ALU.mult, ALU.add))
            link(v.tensor_scalar(ang2[:], ang2[:], -MAGIC, None, ALU.add))
            link(v.scalar_tensor_tensor(out=ang2[:], in0=ang2[:], scalar=float(-2 * np.pi), in1=ang[:], op0=ALU.mult,
                                        op1=ALU.add))
            v.tensor_scalar(ang2[:], ang2[:], 3.1415925, -3.1415925, ALU.min, ALU.max).then_inc(rope_tab, 1)

            def gate_h(i, b):
                dve.wait_ge(up_mm, 2 * i + 2)
                dve.wait_ge(silu_done, i + 1)
                need(dve, ht_mm, 2 * i - 2)
                v.tensor_tensor(hbuf[b].rearrange("p (h n) -> p h n", h=2),
                                silu_h[b].rearrange("p (h n) -> p h n", h=2), ps[:, 2:4, 0:IC], ALU.mult) \
                    .then_inc(h_done, 1)

            def rest_of_rows(i, b):
                dve.wait_ge(rowt_copied, i + 1)
                need(dve, up_mm, 2 * i - 2)
                v.tensor_tensor(xgt[b][1], ps[:, 6, 0:2 * P], xgt[b][0], ALU.subtract).then_inc(row_low, 1)
                if isinstance(i, int) and i == 0:
                    dve.wait_ge(sin_done, 1)
                    v.tensor_tensor(sin8[:], ang[:, 0:64], col(CON, cons, "rope_sign"), ALU.mult) \
                        .then_inc(sin_signed, 1)

            def copy_down(i, b):
                dve.wait_ge(down_mm, i + 1)
                need(dve, row_out[b], (i // 2) * 16 if isinstance(i, int) else (i - b) * 8)
                v.tensor_scalar(yrow[b], ps[:, 7, 0:H], 1.0 / WSCALE, None, ALU.mult).then_inc(down_copied, 1)

            skewed(dve, SLOT_TILES, [(0, rest_of_rows), (1, gate_h), (2, copy_down)])
            if upto >= 3:
                dve.wait_ge(down_mm, SLOT_TILES)
                link(v.memset(kst.rearrange("p u t r -> p (u t r)").bitcast(U32), 0))
                v.memset(kst.rearrange("p u t (j r) -> p (u t j) r", r=HS)[:, :, 24:26], 1.0).then_inc(stack_ones, 1)

            def low_halves(st, src, t, seen, low):
                dst = of_units(st, t)
                dve.wait_ge(cast_hi, seen)
                v.tensor_tensor(dst[:, :, :, low:low + 8], src.rearrange("p (g j r) -> p g j r", g=8, r=HD),
                                dst[:, :, :, 0:8], ALU.subtract).then_inc(stacked, 1)

            for t in range(NT):
                dve.wait_ge(gathered[t % 4], 32 * (t // 4 + 1))
                link(v.scalar_tensor_tensor(out=xa[:, t, :], in0=gat[t % 4][0], scalar=gate_w[:, 0, t:t + 1],
                                            in1=xa[:, t, :], op0=ALU.mult, op1=ALU.add))
                v.scalar_tensor_tensor(out=xa[:, t, :], in0=gat[t % 4][1], scalar=gate_w[:, 1, t:t + 1],
                                       in1=xa[:, t, :], op0=ALU.mult, op1=ALU.add).then_inc(combined, 1)
                if upto >= 3:
                    low_halves(kst, xn[:, t, :], t, 2 * t + 2, 16)
                    dve.wait_ge(combined, t + 1)
                    ln_sums(xa, t)
                    if t == NT // 2 - 1:
                        ln_moments(range(NT // 2))
                    if t == NT // 2:
                        dve.wait_ge(stacked, NT // 2)
                        ln_apply(xa, xn, range(NT // 2))
            if upto < 3:
                return


            ln_moments(range(NT // 2, NT))
            dve.wait_ge(stacked, NT)
            ln_apply(xa, xn, range(NT // 2, NT))
            for t in range(QD + 1):
                if t < QD:
                    dve.wait_ge(q_mm, t // 2 + 1)
                    src = ps[:, 4 + t // 2, (t % 2) * H:(t % 2 + 1) * H].rearrange("p (h r) -> p h r", r=HD)
                    a = rope_a[:, t * H:(t + 1) * H].rearrange("p (h r) -> p h r", r=HD)
                    b = rope_b[:, t * H:(t + 1) * H].rearrange("p (h r) -> p h r", r=HD)
                    cs = ang[:, 64 + t * 8:72 + t * 8].unsqueeze(1).broadcast_to([P, NHEAD, HD])
                    sn = sin8[:, t * 8:t * 8 + 8].unsqueeze(1).broadcast_to([P, NHEAD, HD])
                    v.tensor_tensor(a, src, cs, ALU.mult)
                    v.tensor_tensor(b[:, :, 0::2], src[:, :, 1::2], sn[:, :, 0::2], ALU.mult)
                    link(v.tensor_tensor(b[:, :, 1::2], src[:, :, 0::2], sn[:, :, 1::2], ALU.mult))
                    v.tensor_tensor(a, a, b, ALU.add).then_inc(roped, 1)
                if t:
                    low_halves(qst, rope_a[:, (t - 1) * H:t * H], t - 1, 2 * NT + 2 * t, 8)

            def maxima(n, b, half):
                dve.wait_ge(mx_mm, 2 * n + (half + 1))
                v.tensor_reduce(mx[b % 2].rearrange("p (t h j) -> p h t j", t=2, h=2)[:, half],
                                ps[:, 2 * half:2 * half + 2, :].rearrange("p t (j k) -> p t j k", j=2),
                                AX.X, ALU.max).then_inc(mx_done, 1)

            def shift(n, b):
                dve.wait_ge(mx_done, 2 * n + 2)
                m3 = mx[b % 2].rearrange("p (t j) -> p t j", t=2)
                dst = qst[:, bass.ds(n, 1)].rearrange("p a t (j r) -> p (a t) j r", r=HS)
                v.tensor_scalar(dst[:, :, :, 24], m3, -1.0, None, ALU.mult).then_inc(shift_hi, 1)
                dve.wait_ge(shift_hi, n + 1)
                v.scalar_tensor_tensor(out=dst[:, :, :, 25], in0=m3, scalar=-1.0, in1=dst[:, :, :, 24],
                                       op0=ALU.mult, op1=ALU.subtract).then_inc(shift_done, 1)

            def mask_k(n, b):
                dve.wait_ge(t1_copied, n + 1)
                for j in range(HPU):
                    need(dve, s_mm, HPU * (n - 4) + (j + 1) if not isinstance(n, int) or n >= 4 else 0)
                    r = slice(j * HS, (j + 1) * HS)
                    v.tensor_copy(kmask[b][r, j, :], qkt[b][r, 2 * P:4 * P]).then_inc(masked, 1)

            dve.wait_ge(stack_zero, 5)
            skewed(dve, UNITS, [(2, partial(maxima, half=0)), (2, partial(maxima, half=1)), (2, shift), (0, mask_k)],
                   turn=4)

            def norm_o(g, k):
                dve.wait_ge(ot_mm, 2 * g + k + 1)
                o = ps[:, 2 * k:2 * k + 2, :].rearrange("p a (u t j r) -> p (a u) t j r", t=2, u=2, r=HS)
                r = orec[k].rearrange("p (u t j) -> p u t j", t=2, j=HPU)
                for t in range(2):
                    v.reciprocal(r[:, :, t, :], o[:, :, t, :, HD]).then_inc(o_rec, 1)
                for t in range(2):
                    dve.wait_ge(o_rec, 2 * (2 * g + k) + t + 1)
                    last = v.tensor_tensor(
                        attn[:, t, g * 8 + 4 * k:g * 8 + 4 * k + 4, :].rearrange("p u (j r) -> p (u j) r", r=HD),
                        o[:, :, t, :, 0:HD], r[:, :, t, :].unsqueeze(3).broadcast_to([P, 4, HPU, HD]), ALU.mult)
                last.then_inc(o_norm, 1)

            for g in range(B):
                for k in range(2):
                    norm_o(g, k)
            dve.wait_ge(bout_added, 1)

            def add_attn(t):
                dve.wait_ge(wo_mm, t // 2 + 1)
                v.tensor_tensor(xa[:, t, :], xa[:, t, :], ps[:, 6 + t // 2 % 2, (t % 2) * H:(t % 2 + 1) * H],
                                ALU.add).then_inc(attn_done, 1)

            def sum_attn(t):
                dve.wait_ge(attn_done, t + 1)
                ln_sums(xa, t)

            if upto < 4:
                for t in range(NT):
                    add_attn(t)
                return
            hn3 = hn.rearrange("p (t h) -> p t h", t=NT)
            hb3 = hb.rearrange("p (t h) -> p t h", t=NT)
            for half in range(2):
                tiles = range(half * NT // 2, (half + 1) * NT // 2)
                early = 2 if half else 0
                for t in tiles[early:]:
                    add_attn(t)
                    if t > tiles[0]:
                        sum_attn(t - 1)
                sum_attn(tiles[-1])
                ln_moments(tiles)
                if half == 0:
                    add_attn(NT // 2)
                ln_apply(xa, xb, tiles, sums_too=True)
                ln_moments(tiles)
                if half == 0:
                    add_attn(NT // 2 + 1)
                    sum_attn(NT // 2)
                ln_apply_affine(xb, hn3, hb3, col(LATE, late_s, "ln_w"), col(LATE, late_s, "ln_b"), tiles)
                cols = slice(half * NT // 2 * H, (half + 1) * NT // 2 * H)
                blks = slice(half * NT // 2 * H // BLK, (half + 1) * NT // 2 * H // BLK)
                mx_quant(hqb[:, cols], hb[:, cols], hn.bitcast(BF16)[:, cols], [q[:, blks] for q in qs],
                         NT // 2 * H // BLK).then_inc(hq_ready, 1)

            def quant_f(t, b):
                am, e2, inv, sc = fs[b]
                base = t * 7

                def linked(ins, k):
                    ins.then_inc(fq_chain, 1)
                    dve.wait_ge(fq_chain, base + k)

                def blocks(a):
                    return a.rearrange("p (n k) -> p n k", k=BLK)

                def wide(a):
                    return a.unsqueeze(2).broadcast_to([P, F // BLK, BLK])

                dve.wait_ge(gelu_done, t + 1)
                need(dve, fq_done, t - 1)
                linked(v.tensor_reduce(am, blocks(g1[b]), AX.X, ALU.max, apply_absolute_value=True), 1)
                linked(v.tensor_scalar(am, am, 2.0 ** -100, None, ALU.max), 2)
                linked(v.tensor_scalar(e2.bitcast(I32), am.bitcast(I32), 0x7F800000, None, ALU.bitwise_and), 3)
                v.tensor_scalar(sc, e2, 1.0 / 64, None, ALU.mult).then_inc(fq_chain, 1)
                linked(v.tensor_scalar(inv.bitcast(I32), e2.bitcast(I32), -1.0, float(0x7F000000 + (6 << 23)),
                                       ALU.mult, ALU.add), 5)
                linked(v.tensor_tensor(blocks(gy[b]), blocks(g1[b]), wide(inv), ALU.mult), 6)
                linked(v.tensor_scalar(gy[b], gy[b], MAGIC, -MAGIC, ALU.add, ALU.add), 7)
                v.tensor_scalar(gy[b], gy[b], 127.0, None, ALU.min).then_inc(fy_done, 1)

            skewed(dve, NT, [(1, quant_f)])


def kernel(x, ctx_1024, fside_BxSx2_0, L0_xattn_in_proj_w, L0_xattn_conv_w, L0_xattn_conv_b, L0_xattn_x_proj_w,
           L0_xattn_dt_proj_w, L0_xattn_dt_proj_b, L0_xattn_A_log, L0_xattn_D, L0_ffn_w_gate, L0_ffn_w1, L0_ffn_w2,
           L0_ffn_w3, L1_xattn_Wq, L1_xattn_Wkv, L1_xattn_Wout, L1_xattn_bout, L1_ffn_ln_w, L1_ffn_ln_b, L1_ffn_W1,
           L1_ffn_b1, L1_ffn_W2, L1_ffn_b2):
    import ml_dtypes
    import concourse.bacc as bacc
    from concourse.bass_utils import run_bass_kernel_spmd

    def rows(a, n):
        a = np.asarray(a)
        return a.reshape(n, P, -1).transpose(1, 0, 2).reshape(P, -1)

    def every(a):
        return np.broadcast_to(np.asarray(a).reshape(1, -1), (P, np.asarray(a).size))

    xp = np.asarray(L0_xattn_x_proj_w)
    bc = np.concatenate([xp[DTR:]] * 3 + [xp[:DTR]], axis=0).T
    w13 = np.stack([np.asarray(L0_ffn_w1), np.asarray(L0_ffn_w3)], 1)
    w13 = w13.transpose(0, 1, 3, 2).reshape(E, 2, 2, P, I).transpose(0, 3, 1, 2, 4).reshape(E, P, 4 * I)
    w2 = np.asarray(L0_ffn_w2).transpose(0, 2, 1)
    w2 = np.concatenate([w2, np.zeros((E, KI * P - I, H), w2.dtype)], 1)
    w2 = w2.reshape(E, KI, P, H).transpose(0, 2, 1, 3).reshape(E, P, KI * H)
    pos = np.repeat(np.asarray(fside_BxSx2_0).reshape(T, 2), 4, axis=1)

    eye = np.eye(P, dtype=np.float32)
    key = np.arange(-128, 1)
    lut = np.floor(np.exp(key / 128.0) * 65536)
    freq = np.array([1.0, 1.0, 0.01, 0.01] * 2, np.float32)
    before = np.triu(np.ones((P, P)), 1)
    con = np.concatenate([eye, every(lut), every(key), every(np.tile(np.arange(E)[::-1], NT)),
                          every(np.arange(SLOT_TILES + 1)), np.ones((P, E)), every(np.tile(freq, NT)),
                          every(np.tile([-1.0, 1.0], NT * 4))], axis=1).astype(np.float32)
    con16 = np.concatenate([eye, before, np.ones((P, P))], axis=1).astype(np.float16)
    k = np.arange(P)[:, None, None]
    j = np.arange(32)[None, :, None]
    select = np.broadcast_to((k % 32 == j) & (k < 96), (P, 32, P)).reshape(P, 32 * P)

    given = {
        "x": np.asarray(x).reshape(T, H),
        "ctx_t": np.asarray(ctx_1024).reshape(T, CTX).T,
        "mix": np.concatenate([np.asarray(L0_xattn_in_proj_w).T, rows(bc, ND),
                               rows(np.asarray(L0_xattn_conv_w).reshape(DI, TAPS), ND), rows(L0_xattn_conv_b, ND),
                               rows(L0_xattn_dt_proj_b, ND), rows(L0_xattn_D, ND), rows(L0_xattn_A_log, ND)], 1),
        "dt_proj": np.asarray(L0_xattn_dt_proj_w).T,
        "route": np.concatenate([rows(np.asarray(L0_ffn_w_gate).T, 2), rows(pos, NT), np.asarray(L1_xattn_Wkv)], 1),
        "w13": w13,
        "w2": w2,
        "late": np.concatenate([rows(L1_xattn_Wq, 2), rows(L1_xattn_Wout, 2),
                                every(L1_xattn_bout), every(L1_ffn_ln_w), every(L1_ffn_ln_b), every(L1_ffn_b1),
                                every(L1_ffn_b2)], 1),
        "ffn_w1": rows(L1_ffn_W1, F // P),
        "ffn_w2": rows(L1_ffn_W2, H // P),
        "con": con,
        "con16": con16,
        "bc_select": select.astype(ml_dtypes.bfloat16),
        "ident_b": eye.astype(ml_dtypes.bfloat16),
    }
    nc = bacc.Bacc("TRN2", target_bir_lowering=False, num_devices=1)
    arrays, aps = {}, {}
    for name, a in given.items():
        arrays[f"in_{name}"] = np.ascontiguousarray(a)
        aps[name] = nc.dram_tensor(f"in_{name}", a.shape, mybir.dt.from_np(a.dtype), kind="ExternalInput").ap()
    aps["out"] = nc.dram_tensor("out_x", (T, H), F32, kind="ExternalOutput").ap()
    build(nc, **aps)
    r = run_bass_kernel_spmd(nc, [arrays], core_ids=[0])
    return r.results[0]["out_x"].reshape(B, L, H)
```
